# Optimizing a Trainium2 kernel written in Bass

```python
import numpy as np
import jax
import jax.numpy as jnp

def _softmax(x, axis=-1):
    return jax.nn.softmax(x, axis=axis)

def _gelu(x):
    return jax.nn.gelu(x, approximate=True)

def _silu(x):
    return jax.nn.silu(x)

def _sigmoid(x):
    return jax.nn.sigmoid(x)

def _layernorm(x, axis=-1, eps=1e-05):
    m = jnp.mean(x, axis=axis, keepdims=True)
    v = jnp.var(x, axis=axis, keepdims=True)
    return (x - m) / jnp.sqrt(v + eps)

def _scatter_add(tgt, idx, src, axis=0):
    return tgt.at[idx].add(src)

def _segment_sum(src, seg, n):
    return jax.ops.segment_sum(src, seg, n)
kernel_name = 'mk_gps_d2_gnn_r32_fb1e00'

def setup_inputs(seed: int=0):
    np.random.seed(seed)
    _w = jnp.asarray

    def _rec_inputs():
        import jax
        import jax.numpy as jnp
        _gk = jax.random.key(seed)
        x = -6.415e-05 + 1 * jax.random.normal(jax.random.fold_in(_gk, 1), (625, 512), jnp.float32)
        src = jax.random.randint(jax.random.fold_in(_gk, 2), (10000,), 0, 625, jnp.int32)
        dst = jnp.minimum((625 * jax.random.uniform(jax.random.fold_in(_gk, 3), (10000,)) ** 2.0).astype(jnp.int32), 19999)
        _o = jnp.argsort(dst, stable=True)
        src = src[_o]
        dst = dst[_o]
        return (x, src, dst)
    x, src, dst = _rec_inputs()

    def _L0_gnn_setup():
        import jax, jax.numpy as jnp
        import numpy as np
        N, E, H = (625, 5000, 512)
        EPS = 1e-07

        def _ln(x, g, b, eps=1e-05):
            mu = jnp.mean(x, axis=-1, keepdims=True)
            var = jnp.mean((x - mu) ** 2, axis=-1, keepdims=True)
            return (x - mu) * jax.lax.rsqrt(var + eps) * g + b

        def _genconv(x, src, dst, t, w1, b1, lg, lb, w2, b2):
            m = jax.nn.relu(x[src]) + EPS
            z = m * t
            zmax = jax.lax.stop_gradient(jax.ops.segment_max(z, dst, num_segments=N))
            zmax = jnp.where(jnp.isfinite(zmax), zmax, 0.0)
            e = jnp.exp(z - zmax[dst])
            denom = jax.ops.segment_sum(e, dst, num_segments=N)
            alpha = e / (denom[dst] + 1e-16)
            agg = jax.ops.segment_sum(alpha * m, dst, num_segments=N)
            h = agg + x
            h = jax.nn.relu(_ln(h @ w1 + b1, lg, lb))
            return h @ w2 + b2

        def _forward(x, edge_index, p):
            src, dst = (edge_index[0], edge_index[1])
            x1 = _genconv(x, src, dst, *p['c0'])
            x2 = x1 + jax.nn.relu(_ln(_genconv(x1, src, dst, *p['c1']), p['lng_1'], p['lnb_1']))
            x3 = x2 + jax.nn.relu(_ln(_genconv(x2, src, dst, *p['c2']), p['lng_2'], p['lnb_2']))
            return jnp.concatenate([x1, x2, x3], axis=1) @ p['cw'] + p['cb']
        key = jax.random.key(seed)
        ks = iter(jax.random.split(key, 16))
        s = 0.05
        d = {'x': jax.random.normal(next(ks), (N, H), jnp.float32), 'edge_index': jax.random.randint(next(ks), (2, E), 0, N, jnp.int32)}
        for i in range(3):
            d[f't{i}'] = jnp.ones((1,), jnp.float32)
            d[f'mw1_{i}'] = jax.random.normal(next(ks), (H, 2 * H), jnp.float32) * s
            d[f'mb1_{i}'] = jnp.zeros((2 * H,), jnp.float32)
            d[f'mlg_{i}'] = jnp.ones((2 * H,), jnp.float32)
            d[f'mlb_{i}'] = jnp.zeros((2 * H,), jnp.float32)
            d[f'mw2_{i}'] = jax.random.normal(next(ks), (2 * H, H), jnp.float32) * s
            d[f'mb2_{i}'] = jnp.zeros((H,), jnp.float32)
        for i in (1, 2):
            d[f'lng_{i}'] = jnp.ones((H,), jnp.float32)
            d[f'lnb_{i}'] = jnp.zeros((H,), jnp.float32)
        d['cw'] = jax.random.normal(next(ks), (3 * H, H), jnp.float32) * s
        d['cb'] = jnp.zeros((H,), jnp.float32)
        return d
    _L0_gnn_all = _L0_gnn_setup()
    _L0_gnn_in = {k: v for k, v in _L0_gnn_all.items() if k in ('t0', 'mw1_0', 'mb1_0', 'mlg_0', 'mlb_0', 'mw2_0', 'mb2_0', 't1', 'mw1_1', 'mb1_1', 'mlg_1', 'mlb_1', 'mw2_1', 'mb2_1', 't2', 'mw1_2', 'mb1_2', 'mlg_2', 'mlb_2', 'mw2_2', 'mb2_2', 'lng_1', 'lnb_1', 'lng_2', 'lnb_2', 'cw', 'cb')}
    del _L0_gnn_all

    def _L0_mix_setup():
        import math
        import jax, jax.numpy as jnp
        import numpy as np
        NUM_HEADS = 8
        ALPHA = 20.0
        LN_EPS = 1e-05

        def _forward(x, qkv_w, qkv_b, ln_g, ln_b, out_w, out_b):
            B, N, C = x.shape
            H = NUM_HEADS
            D = C // H
            qkv = x @ qkv_w + qkv_b
            q, k, v = jnp.split(qkv, 3, axis=-1)

            def to_heads(t):
                return t.reshape(B, N, H, D).transpose(0, 2, 1, 3)
            q, k, v = (to_heads(q), to_heads(k), to_heads(v))
            q_norm = jnp.linalg.norm(q, axis=-1, keepdims=True)
            k_norm = jnp.linalg.norm(k, axis=-1, keepdims=True)
            q_t = q / q_norm
            dq = jnp.tanh(q / q_norm * ALPHA) * (math.pi / 4)
            dk = jnp.tanh(k / k_norm * ALPHA) * (math.pi / 4)
            k3 = jnp.abs(k) ** 3
            kf = jnp.concatenate([k3 * jnp.cos(dk), k3 * jnp.sin(dk)], axis=-1)
            power = 1.5 * (0.5 + jnp.tanh(q_norm))
            q_t = (q_t ** 2) ** power
            qf = jnp.concatenate([q_t * jnp.cos(dq), q_t * jnp.sin(dq)], axis=-1)
            k_mean = jnp.mean(kf, axis=2, keepdims=True)
            z = 1.0 / (jnp.einsum('bhnf,bhmf->bhnm', qf, k_mean) + 1e-06)
            scale = N ** (-0.5)
            kv = jnp.einsum('bhnf,bhnd->bhfd', kf * scale, v * scale)
            out = jnp.einsum('bhnf,bhfd->bhnd', qf, kv) * z
            out = out.transpose(0, 2, 1, 3).reshape(B, N, C)
            mu = jnp.mean(out, axis=-1, keepdims=True)
            var = jnp.var(out, axis=-1, keepdims=True)
            out = (out - mu) * jax.lax.rsqrt(var + LN_EPS) * ln_g + ln_b
            return out @ out_w + out_b
        key = jax.random.key(seed)
        ks = jax.random.split(key, 6)
        B, N, C = (8, 128, 512)
        s = 1.0 / math.sqrt(C)
        return {'x': jax.random.normal(ks[0], (B, N, C), dtype=jnp.float32), 'qkv_w': jax.random.normal(ks[1], (C, 3 * C), dtype=jnp.float32) * s, 'qkv_b': jnp.zeros((3 * C,), dtype=jnp.float32), 'ln_g': jnp.ones((C,), dtype=jnp.float32), 'ln_b': jnp.zeros((C,), dtype=jnp.float32), 'out_w': jax.random.normal(ks[2], (C, C), dtype=jnp.float32) * s, 'out_b': jnp.zeros((C,), dtype=jnp.float32)}
    _L0_mix_all = _L0_mix_setup()
    _L0_mix_in = {k: v for k, v in _L0_mix_all.items() if k in ('qkv_w', 'qkv_b', 'ln_g', 'ln_b', 'out_w', 'out_b')}
    del _L0_mix_all

    def _L0_ffn_setup():
        import jax, jax.numpy as jnp
        import numpy as np
        K = 2
        key = jax.random.key(seed)
        ks = jax.random.split(key, 6)
        B, T, d, E, dff = (2, 64, 512, 8, 64)
        x = jax.random.normal(ks[0], (B, T, d), dtype=jnp.float32)
        Wg = jax.random.normal(ks[1], (d, E), dtype=jnp.float32) * 0.02
        W1 = jax.random.normal(ks[2], (E, d, dff), dtype=jnp.float32) * 0.02
        b1 = jnp.zeros((E, dff), dtype=jnp.float32)
        W2 = jax.random.normal(ks[3], (E, dff, d), dtype=jnp.float32) * 0.02
        b2 = jnp.zeros((E, d), dtype=jnp.float32)
        return {'x': x, 'Wg': Wg, 'W1': W1, 'b1': b1, 'W2': W2, 'b2': b2}
    _L0_ffn_all = _L0_ffn_setup()
    _L0_ffn_in = {k: v for k, v in _L0_ffn_all.items() if k in ('Wg', 'W1', 'b1', 'W2', 'b2')}
    del _L0_ffn_all

    def _L1_gnn_setup():
        import jax, jax.numpy as jnp
        import numpy as np
        N = 625
        E = 10000
        F_IN = 512
        HEADS = 8
        D = 64
        ALPHA = 0.2
        EPS = 1e-16

        def _gat_forward(x, edge_index, W_e, W_r, a):
            src = edge_index[0]
            dst = edge_index[1]
            h_e = jnp.einsum('nf,hfd->hnd', x, W_e)
            h_r = jnp.einsum('nf,hfd->hnd', x, W_r)
            a_src, a_dst, a_dif, a_abs, a_prd = jnp.split(a, 5, axis=1)
            s_src = jnp.einsum('hnd,hd->hn', h_e, a_src)[:, src]
            s_dst = jnp.einsum('hnd,hd->hn', h_e, a_dst)[:, dst]
            hr_src = h_r[:, src]
            hr_dst = h_r[:, dst]
            diff = hr_dst - hr_src
            score = s_src + s_dst + jnp.einsum('hed,hd->he', diff, a_dif) + jnp.einsum('hed,hd->he', jnp.abs(diff), a_abs) + jnp.einsum('hed,hd->he', hr_src * hr_dst, a_prd)
            alpha = jax.nn.leaky_relu(score, negative_slope=ALPHA)
            alpha_t = alpha.T
            m = jax.ops.segment_max(alpha_t, src, num_segments=N)
            ex = jnp.exp(alpha_t - m[src])
            denom = jax.ops.segment_sum(ex, src, num_segments=N)[src]
            att = ex / (denom + EPS)
            msg = att[:, :, None] * jnp.transpose(h_e[:, dst], (1, 0, 2))
            out = jax.ops.segment_sum(msg, src, num_segments=N)
            return out.reshape(N, HEADS * D)
        key = jax.random.key(seed)
        k1, k2, k3, k4, k5 = jax.random.split(key, 5)
        x = jax.random.normal(k1, (N, F_IN), dtype=jnp.float32)
        edge_index = jax.random.randint(k2, (2, E), 0, N, dtype=jnp.int64)
        s_w = np.sqrt(2.0 / (F_IN + D))
        W_e = jax.random.normal(k3, (HEADS, F_IN, D), dtype=jnp.float32) * s_w
        W_r = jax.random.normal(k4, (HEADS, F_IN, D), dtype=jnp.float32) * s_w
        s_a = np.sqrt(2.0 / (1 + 5 * D))
        a = jax.random.normal(k5, (HEADS, 5 * D), dtype=jnp.float32) * s_a
        return {'x': x, 'edge_index': edge_index, 'W_e': W_e, 'W_r': W_r, 'a': a}
    _L1_gnn_all = _L1_gnn_setup()
    _L1_gnn_in = {k: v for k, v in _L1_gnn_all.items() if k in ('W_e', 'W_r', 'a')}
    del _L1_gnn_all

    def _L1_mix_setup():
        import jax, jax.numpy as jnp
        import numpy as np
        B, T, D, H = (4, 256, 512, 8)
        HD = D // H
        key = jax.random.key(seed)
        k0, k1, k2 = jax.random.split(key, 3)
        std = 1.0 / np.sqrt(D)
        return {'x': jax.random.normal(k0, (B, T, D), dtype=jnp.float32), 'W_qkv': jax.random.normal(k1, (3 * D, D), dtype=jnp.float32) * std, 'b_qkv': jnp.zeros((3 * D,), dtype=jnp.float32), 'W_out': jax.random.normal(k2, (D, D), dtype=jnp.float32) * std, 'b_out': jnp.zeros((D,), dtype=jnp.float32)}
    _L1_mix_all = _L1_mix_setup()
    _L1_mix_in = {k: v for k, v in _L1_mix_all.items() if k in ('W_qkv', 'b_qkv', 'W_out', 'b_out')}
    del _L1_mix_all

    def _L1_ffn_setup():
        import jax, jax.numpy as jnp
        import numpy as np
        S, B, D, F, E, K = (1024, 2, 512, 64, 8, 2)
        key = jax.random.key(seed)
        ks = jax.random.split(key, 12)
        s = lambda *sh: 1.0 / np.sqrt(sh[0])
        inp = {'x': jax.random.normal(ks[0], (S, B, D), dtype=jnp.float32), 'Wg': jax.random.normal(ks[1], (D, E), dtype=jnp.float32) * s(D), 'bg': jnp.zeros((E,), dtype=jnp.float32), 'W1': jax.random.normal(ks[2], (E, D, F), dtype=jnp.float32) * s(D), 'b1': jnp.zeros((E, F), dtype=jnp.float32), 'W2': jax.random.normal(ks[3], (E, F, D), dtype=jnp.float32) * s(F), 'b2': jnp.zeros((E, D), dtype=jnp.float32), 'Ws1': jax.random.normal(ks[4], (D, F), dtype=jnp.float32) * s(D), 'bs1': jnp.zeros((F,), dtype=jnp.float32), 'Ws2': jax.random.normal(ks[5], (F, D), dtype=jnp.float32) * s(F), 'bs2': jnp.zeros((D,), dtype=jnp.float32)}
        return inp
    _L1_ffn_all = _L1_ffn_setup()
    _L1_ffn_in = {k: v for k, v in _L1_ffn_all.items() if k in ('Wg', 'bg', 'W1', 'b1', 'W2', 'b2', 'Ws1', 'bs1', 'Ws2', 'bs2')}
    del _L1_ffn_all
    return {'x': x, 'src': src, 'dst': dst, 'L0_gnn_t0': _L0_gnn_in['t0'], 'L0_gnn_mw1_0': _L0_gnn_in['mw1_0'], 'L0_gnn_mb1_0': _L0_gnn_in['mb1_0'], 'L0_gnn_mlg_0': _L0_gnn_in['mlg_0'], 'L0_gnn_mlb_0': _L0_gnn_in['mlb_0'], 'L0_gnn_mw2_0': _L0_gnn_in['mw2_0'], 'L0_gnn_mb2_0': _L0_gnn_in['mb2_0'], 'L0_gnn_t1': _L0_gnn_in['t1'], 'L0_gnn_mw1_1': _L0_gnn_in['mw1_1'], 'L0_gnn_mb1_1': _L0_gnn_in['mb1_1'], 'L0_gnn_mlg_1': _L0_gnn_in['mlg_1'], 'L0_gnn_mlb_1': _L0_gnn_in['mlb_1'], 'L0_gnn_mw2_1': _L0_gnn_in['mw2_1'], 'L0_gnn_mb2_1': _L0_gnn_in['mb2_1'], 'L0_gnn_t2': _L0_gnn_in['t2'], 'L0_gnn_mw1_2': _L0_gnn_in['mw1_2'], 'L0_gnn_mb1_2': _L0_gnn_in['mb1_2'], 'L0_gnn_mlg_2': _L0_gnn_in['mlg_2'], 'L0_gnn_mlb_2': _L0_gnn_in['mlb_2'], 'L0_gnn_mw2_2': _L0_gnn_in['mw2_2'], 'L0_gnn_mb2_2': _L0_gnn_in['mb2_2'], 'L0_gnn_lng_1': _L0_gnn_in['lng_1'], 'L0_gnn_lnb_1': _L0_gnn_in['lnb_1'], 'L0_gnn_lng_2': _L0_gnn_in['lng_2'], 'L0_gnn_lnb_2': _L0_gnn_in['lnb_2'], 'L0_gnn_cw': _L0_gnn_in['cw'], 'L0_gnn_cb': _L0_gnn_in['cb'], 'L0_mix_qkv_w': _L0_mix_in['qkv_w'], 'L0_mix_qkv_b': _L0_mix_in['qkv_b'], 'L0_mix_ln_g': _L0_mix_in['ln_g'], 'L0_mix_ln_b': _L0_mix_in['ln_b'], 'L0_mix_out_w': _L0_mix_in['out_w'], 'L0_mix_out_b': _L0_mix_in['out_b'], 'L0_ffn_Wg': _L0_ffn_in['Wg'], 'L0_ffn_W1': _L0_ffn_in['W1'], 'L0_ffn_b1': _L0_ffn_in['b1'], 'L0_ffn_W2': _L0_ffn_in['W2'], 'L0_ffn_b2': _L0_ffn_in['b2'], 'L1_gnn_W_e': _L1_gnn_in['W_e'], 'L1_gnn_W_r': _L1_gnn_in['W_r'], 'L1_gnn_a': _L1_gnn_in['a'], 'L1_mix_W_qkv': _L1_mix_in['W_qkv'], 'L1_mix_b_qkv': _L1_mix_in['b_qkv'], 'L1_mix_W_out': _L1_mix_in['W_out'], 'L1_mix_b_out': _L1_mix_in['b_out'], 'L1_ffn_Wg': _L1_ffn_in['Wg'], 'L1_ffn_bg': _L1_ffn_in['bg'], 'L1_ffn_W1': _L1_ffn_in['W1'], 'L1_ffn_b1': _L1_ffn_in['b1'], 'L1_ffn_W2': _L1_ffn_in['W2'], 'L1_ffn_b2': _L1_ffn_in['b2'], 'L1_ffn_Ws1': _L1_ffn_in['Ws1'], 'L1_ffn_bs1': _L1_ffn_in['bs1'], 'L1_ffn_Ws2': _L1_ffn_in['Ws2'], 'L1_ffn_bs2': _L1_ffn_in['bs2']}

def reference(x, src, dst, L0_gnn_t0, L0_gnn_mw1_0, L0_gnn_mb1_0, L0_gnn_mlg_0, L0_gnn_mlb_0, L0_gnn_mw2_0, L0_gnn_mb2_0, L0_gnn_t1, L0_gnn_mw1_1, L0_gnn_mb1_1, L0_gnn_mlg_1, L0_gnn_mlb_1, L0_gnn_mw2_1, L0_gnn_mb2_1, L0_gnn_t2, L0_gnn_mw1_2, L0_gnn_mb1_2, L0_gnn_mlg_2, L0_gnn_mlb_2, L0_gnn_mw2_2, L0_gnn_mb2_2, L0_gnn_lng_1, L0_gnn_lnb_1, L0_gnn_lng_2, L0_gnn_lnb_2, L0_gnn_cw, L0_gnn_cb, L0_mix_qkv_w, L0_mix_qkv_b, L0_mix_ln_g, L0_mix_ln_b, L0_mix_out_w, L0_mix_out_b, L0_ffn_Wg, L0_ffn_W1, L0_ffn_b1, L0_ffn_W2, L0_ffn_b2, L1_gnn_W_e, L1_gnn_W_r, L1_gnn_a, L1_mix_W_qkv, L1_mix_b_qkv, L1_mix_W_out, L1_mix_b_out, L1_ffn_Wg, L1_ffn_bg, L1_ffn_W1, L1_ffn_b1, L1_ffn_W2, L1_ffn_b2, L1_ffn_Ws1, L1_ffn_bs1, L1_ffn_Ws2, L1_ffn_bs2):
    import jax
    import jax.numpy as jnp

    def _L0_gnn_ref(x, edge_index, t0, mw1_0, mb1_0, mlg_0, mlb_0, mw2_0, mb2_0, t1, mw1_1, mb1_1, mlg_1, mlb_1, mw2_1, mb2_1, t2, mw1_2, mb1_2, mlg_2, mlb_2, mw2_2, mb2_2, lng_1, lnb_1, lng_2, lnb_2, cw, cb):
        import jax, jax.numpy as jnp
        import numpy as np
        N, E, H = (625, 5000, 512)
        EPS = 1e-07

        def _ln(x, g, b, eps=1e-05):
            mu = jnp.mean(x, axis=-1, keepdims=True)
            var = jnp.mean((x - mu) ** 2, axis=-1, keepdims=True)
            return (x - mu) * jax.lax.rsqrt(var + eps) * g + b

        def _genconv(x, src, dst, t, w1, b1, lg, lb, w2, b2):
            m = jax.nn.relu(x[src]) + EPS
            z = m * t
            zmax = jax.lax.stop_gradient(jax.ops.segment_max(z, dst, num_segments=N))
            zmax = jnp.where(jnp.isfinite(zmax), zmax, 0.0)
            e = jnp.exp(z - zmax[dst])
            denom = jax.ops.segment_sum(e, dst, num_segments=N)
            alpha = e / (denom[dst] + 1e-16)
            agg = jax.ops.segment_sum(alpha * m, dst, num_segments=N)
            h = agg + x
            h = jax.nn.relu(_ln(h @ w1 + b1, lg, lb))
            return h @ w2 + b2

        def _forward(x, edge_index, p):
            src, dst = (edge_index[0], edge_index[1])
            x1 = _genconv(x, src, dst, *p['c0'])
            x2 = x1 + jax.nn.relu(_ln(_genconv(x1, src, dst, *p['c1']), p['lng_1'], p['lnb_1']))
            x3 = x2 + jax.nn.relu(_ln(_genconv(x2, src, dst, *p['c2']), p['lng_2'], p['lnb_2']))
            return jnp.concatenate([x1, x2, x3], axis=1) @ p['cw'] + p['cb']
        p = {'c0': (t0, mw1_0, mb1_0, mlg_0, mlb_0, mw2_0, mb2_0), 'c1': (t1, mw1_1, mb1_1, mlg_1, mlb_1, mw2_1, mb2_1), 'c2': (t2, mw1_2, mb1_2, mlg_2, mlb_2, mw2_2, mb2_2), 'lng_1': lng_1, 'lnb_1': lnb_1, 'lng_2': lng_2, 'lnb_2': lnb_2, 'cw': cw, 'cb': cb}
        return _forward(x, edge_index, p)

    def _L0_mix_ref(x, qkv_w, qkv_b, ln_g, ln_b, out_w, out_b):
        import math
        import jax, jax.numpy as jnp
        import numpy as np
        NUM_HEADS = 8
        ALPHA = 20.0
        LN_EPS = 1e-05

        def _forward(x, qkv_w, qkv_b, ln_g, ln_b, out_w, out_b):
            B, N, C = x.shape
            H = NUM_HEADS
            D = C // H
            qkv = x @ qkv_w + qkv_b
            q, k, v = jnp.split(qkv, 3, axis=-1)

            def to_heads(t):
                return t.reshape(B, N, H, D).transpose(0, 2, 1, 3)
            q, k, v = (to_heads(q), to_heads(k), to_heads(v))
            q_norm = jnp.linalg.norm(q, axis=-1, keepdims=True)
            k_norm = jnp.linalg.norm(k, axis=-1, keepdims=True)
            q_t = q / q_norm
            dq = jnp.tanh(q / q_norm * ALPHA) * (math.pi / 4)
            dk = jnp.tanh(k / k_norm * ALPHA) * (math.pi / 4)
            k3 = jnp.abs(k) ** 3
            kf = jnp.concatenate([k3 * jnp.cos(dk), k3 * jnp.sin(dk)], axis=-1)
            power = 1.5 * (0.5 + jnp.tanh(q_norm))
            q_t = (q_t ** 2) ** power
            qf = jnp.concatenate([q_t * jnp.cos(dq), q_t * jnp.sin(dq)], axis=-1)
            k_mean = jnp.mean(kf, axis=2, keepdims=True)
            z = 1.0 / (jnp.einsum('bhnf,bhmf->bhnm', qf, k_mean) + 1e-06)
            scale = N ** (-0.5)
            kv = jnp.einsum('bhnf,bhnd->bhfd', kf * scale, v * scale)
            out = jnp.einsum('bhnf,bhfd->bhnd', qf, kv) * z
            out = out.transpose(0, 2, 1, 3).reshape(B, N, C)
            mu = jnp.mean(out, axis=-1, keepdims=True)
            var = jnp.var(out, axis=-1, keepdims=True)
            out = (out - mu) * jax.lax.rsqrt(var + LN_EPS) * ln_g + ln_b
            return out @ out_w + out_b
        return _forward(x, qkv_w, qkv_b, ln_g, ln_b, out_w, out_b)

    def _L0_ffn_ref(x, Wg, W1, b1, W2, b2):
        import jax, jax.numpy as jnp
        import numpy as np
        K = 2
        logits = jnp.einsum('btd,de->bte', x, Wg)
        probs = jax.nn.softmax(logits, axis=-1)
        top_p, _top_i = jax.lax.top_k(probs, K)
        top_p = top_p / jnp.sum(top_p, axis=-1, keepdims=True)
        b2_sum = jnp.sum(b2, axis=0)
        out = jnp.zeros_like(x)
        for i in range(K):
            w_in = x * top_p[..., i:i + 1]
            h = jax.nn.gelu(jnp.einsum('btd,edf->ebtf', w_in, W1) + b1[:, None, None, :], approximate=False)
            out = out + jnp.einsum('ebtf,efd->btd', h, W2) + b2_sum
        return out

    def _L1_gnn_ref(x, edge_index, W_e, W_r, a):
        import jax, jax.numpy as jnp
        import numpy as np
        N = 625
        E = 10000
        F_IN = 512
        HEADS = 8
        D = 64
        ALPHA = 0.2
        EPS = 1e-16

        def _gat_forward(x, edge_index, W_e, W_r, a):
            src = edge_index[0]
            dst = edge_index[1]
            h_e = jnp.einsum('nf,hfd->hnd', x, W_e)
            h_r = jnp.einsum('nf,hfd->hnd', x, W_r)
            a_src, a_dst, a_dif, a_abs, a_prd = jnp.split(a, 5, axis=1)
            s_src = jnp.einsum('hnd,hd->hn', h_e, a_src)[:, src]
            s_dst = jnp.einsum('hnd,hd->hn', h_e, a_dst)[:, dst]
            hr_src = h_r[:, src]
            hr_dst = h_r[:, dst]
            diff = hr_dst - hr_src
            score = s_src + s_dst + jnp.einsum('hed,hd->he', diff, a_dif) + jnp.einsum('hed,hd->he', jnp.abs(diff), a_abs) + jnp.einsum('hed,hd->he', hr_src * hr_dst, a_prd)
            alpha = jax.nn.leaky_relu(score, negative_slope=ALPHA)
            alpha_t = alpha.T
            m = jax.ops.segment_max(alpha_t, src, num_segments=N)
            ex = jnp.exp(alpha_t - m[src])
            denom = jax.ops.segment_sum(ex, src, num_segments=N)[src]
            att = ex / (denom + EPS)
            msg = att[:, :, None] * jnp.transpose(h_e[:, dst], (1, 0, 2))
            out = jax.ops.segment_sum(msg, src, num_segments=N)
            return out.reshape(N, HEADS * D)
        return _gat_forward(x, edge_index, W_e, W_r, a)

    def _L1_mix_ref(x, W_qkv, b_qkv, W_out, b_out):
        import jax, jax.numpy as jnp
        import numpy as np
        B, T, D, H = (4, 256, 512, 8)
        HD = D // H
        b, t, d = x.shape
        qkv = x @ W_qkv.T + b_qkv
        q, k, v = jnp.split(qkv, 3, axis=-1)

        def to_heads(u):
            return u.reshape(b, t, H, HD).transpose(0, 2, 1, 3)
        q, k, v = (to_heads(q), to_heads(k), to_heads(v))
        k = jax.nn.softmax(k, axis=-2)
        context = jnp.einsum('bhtd,bhtv->bhdv', k, v)
        out = jnp.einsum('bhtd,bhdv->bhtv', q, context)
        out = out.transpose(0, 2, 1, 3).reshape(b, t, d)
        return out @ W_out.T + b_out

    def _L1_ffn_ref(x, Wg, bg, W1, b1, W2, b2, Ws1, bs1, Ws2, bs2):
        import jax, jax.numpy as jnp
        import numpy as np
        S, B, D, F, E, K = (1024, 2, 512, 64, 8, 2)
        gate_logits = jnp.einsum('sbd,de->sbe', x, Wg) + bg
        weights, selected = jax.lax.top_k(gate_logits, K)
        weights = jax.nn.softmax(weights.astype(jnp.float32), axis=-1)
        onehot = jax.nn.one_hot(selected, E, dtype=weights.dtype)
        comb = jnp.einsum('sbk,sbke->sbe', weights, onehot)
        h = jax.nn.relu(jnp.einsum('sbd,edf->sbef', x, W1) + b1)
        y = jnp.einsum('sbef,efd->sbed', h, W2) + b2
        out = jnp.einsum('sbe,sbed->sbd', comb, y)
        hs = jax.nn.relu(jnp.einsum('sbd,df->sbf', x, Ws1) + bs1)
        shared = jnp.einsum('sbf,fd->sbd', hs, Ws2) + bs2
        out = out + 1.0 / K * shared
        return out
    edge_index = jnp.stack([src, dst])
    xn = _layernorm(x, axis=-1)
    x = x + _L0_gnn_ref(xn, edge_index, L0_gnn_t0, L0_gnn_mw1_0, L0_gnn_mb1_0, L0_gnn_mlg_0, L0_gnn_mlb_0, L0_gnn_mw2_0, L0_gnn_mb2_0, L0_gnn_t1, L0_gnn_mw1_1, L0_gnn_mb1_1, L0_gnn_mlg_1, L0_gnn_mlb_1, L0_gnn_mw2_1, L0_gnn_mb2_1, L0_gnn_t2, L0_gnn_mw1_2, L0_gnn_mb1_2, L0_gnn_mlg_2, L0_gnn_mlb_2, L0_gnn_mw2_2, L0_gnn_mb2_2, L0_gnn_lng_1, L0_gnn_lnb_1, L0_gnn_lng_2, L0_gnn_lnb_2, L0_gnn_cw, L0_gnn_cb) + _L0_mix_ref(xn[None], L0_mix_qkv_w, L0_mix_qkv_b, L0_mix_ln_g, L0_mix_ln_b, L0_mix_out_w, L0_mix_out_b)[0]
    x = x + _L0_ffn_ref(_layernorm(x, axis=-1)[None], L0_ffn_Wg, L0_ffn_W1, L0_ffn_b1, L0_ffn_W2, L0_ffn_b2)[0]
    xn = _layernorm(x, axis=-1)
    x = x + _L1_gnn_ref(xn, edge_index, L1_gnn_W_e, L1_gnn_W_r, L1_gnn_a) + _L1_mix_ref(xn[None], L1_mix_W_qkv, L1_mix_b_qkv, L1_mix_W_out, L1_mix_b_out)[0]
    x = x + _L1_ffn_ref(_layernorm(x, axis=-1)[None], L1_ffn_Wg, L1_ffn_bg, L1_ffn_W1, L1_ffn_b1, L1_ffn_W2, L1_ffn_b2, L1_ffn_Ws1, L1_ffn_bs1, L1_ffn_Ws2, L1_ffn_bs2)[0]
    return x

_drawn_inputs = setup_inputs


def setup_inputs(seed=0):
    import zlib

    import numpy as np

    out = dict(_drawn_inputs(seed))
    spreads = {'L0_gnn_mb1_0': (0.0, 0.1),
     'L0_gnn_mlg_0': (1.0, 0.2),
     'L0_gnn_mlb_0': (0.0, 0.1),
     'L0_gnn_mb2_0': (0.0, 0.1),
     'L0_gnn_mb1_1': (0.0, 0.328),
     'L0_gnn_mlg_1': (1.0, 0.2),
     'L0_gnn_mlb_1': (0.0, 0.1),
     'L0_gnn_mb2_1': (0.0, 0.1),
     'L0_gnn_mb1_2': (0.0, 0.659),
     'L0_gnn_mlg_2': (1.0, 0.2),
     'L0_gnn_mlb_2': (0.0, 0.1),
     'L0_gnn_mb2_2': (0.0, 0.276),
     'L0_gnn_lng_1': (1.0, 0.2),
     'L0_gnn_lnb_1': (0.0, 0.1),
     'L0_gnn_lng_2': (1.0, 0.2),
     'L0_gnn_lnb_2': (0.0, 0.1),
     'L0_gnn_cb': (0.0, 0.1),
     'L0_mix_qkv_b': (0.0, 0.1),
     'L0_mix_ln_g': (1.0, 0.2),
     'L0_mix_ln_b': (0.0, 0.1),
     'L0_mix_out_b': (0.0, 0.1),
     'L0_ffn_b1': (0.0, 0.341),
     'L0_ffn_b2': (0.0, 0.1),
     'L1_mix_b_qkv': (0.0, 0.1),
     'L1_mix_b_out': (0.0, 0.521),
     'L1_ffn_bg': (0.0, 0.519),
     'L1_ffn_b1': (0.0, 0.8),
     'L1_ffn_b2': (0.0, 0.776),
     'L1_ffn_bs1': (0.0, 2.0),
     'L1_ffn_bs2': (0.0, 0.8)}
    factors = {'L0_ffn_Wg': 64.0}
    for name, (base, spread) in spreads.items():
        noise = np.random.default_rng([zlib.crc32(name.encode()), seed]).standard_normal(out[name].shape)
        drawn = base * np.exp(spread * noise) if base else spread * noise
        out[name] = jnp.asarray(drawn.astype(out[name].dtype))
    for name, factor in factors.items():
        out[name] = (out[name] * factor).astype(out[name].dtype)
    return out
```

```python
from contextlib import ExitStack

import concourse.bass as bass
from concourse import mybir

F32 = mybir.dt.float32
F16 = mybir.dt.float16
I32 = mybir.dt.int32
U32 = mybir.dt.uint32
ALU = mybir.AluOpType
ACT = mybir.ActivationFunctionType
AX_X = mybir.AxisListType.X
RMAX = bass.bass_isa.ReduceOp.max

N, E, D = 625, 10000, 512
P = 125
NT = N // P
ET = E // P
KC = D // 128
HID = 2 * D
HC = HID // 128
H, HD = 8, 64
LAYERS = 3
ONE_HOTS = 8
GATHERS = 4
TABLE = D + 2 * H
HEADROOM = 64.0
NO_EDGE = -1e30
LN_EPS = 1e-5
PI = 3.141592653589793
WX = D + HD + H
ROWS = [("mb1_0", HID), ("mb1_1", HID), ("mb1_2", HID), ("mb2_0", D), ("mb2_1", D), ("mb2_2", D),
        ("lng_1", D), ("lnb_1", D), ("lng_2", D), ("lnb_2", D), ("qkv_b", 3 * D), ("out_b", D),
        ("cb", D), ("f0_b1", D), ("v_b", D), ("b_out", D), ("f1_b", WX), ("a_abs", D),
        ("a_src", D), ("a_dst", D), ("a_dif", D), ("t", LAYERS)]
COLS = [("mlg_0", HC), ("mlb_0", HC), ("mlg_1", HC), ("mlb_1", HC), ("mlg_2", HC), ("mlb_2", HC),
        ("ln_g", KC), ("ln_b", KC), ("q_b", KC), ("k_b", KC), ("a_prd", KC), ("a_difT", KC)]


def offsets(parts):
    at, out = 0, {}
    for name, n in parts:
        out[name] = (at, n)
        at += n
    return out, at


ROW_AT, ROW_LEN = offsets(ROWS)
COL_AT, COL_LEN = offsets(COLS)


def psum_jobs():
    jobs = [(("xnT", 0, i), "act") for i in range(NT)]
    for i in range(NT):
        jobs += [(("qk", i), "dve"), (("v", i), "dve")]
    jobs += [(("kv",), "dve")]
    for i in range(NT + 1):
        if i < NT:
            jobs += [(("qfT", i), "act"), (("mo", i), "dve")]
        if i >= 1:
            jobs += [(("moT", i - 1), "act"), (("mw", i - 1), "dve")]
    for l in range(LAYERS):
        for j in range(KC):
            jobs += [(("den", l, j), "dve"), (("num", l, j), "dve")]
        jobs += lagged(lambda i: [(("u", l, i), "dve")],
                       lambda i: [(("gT", l, i), "act"), (("y", l, i), "dve")])
        jobs += [(("yT", l, i), "act") for i in range(NT)]
        jobs += [(("cw", l, i), "dve") for i in range(NT)]
    jobs += [(("xnT", 1, i), "act") for i in range(NT)]
    jobs += [(("f0", i), "dve") for i in range(NT)]
    for i in range(NT):
        jobs += [(("f0T", i), "act"), (("f0o", i), "dve")]
    jobs += [(("xnT", 2, i), "act") for i in range(NT)]
    jobs += [(("hre", i), "dve") for i in range(NT)]
    jobs += [(("hrT", i), "act") for i in range(NT)]
    for j in range(KC):
        jobs += [(("kT", j), "act"), (("qT", j), "act")]
    jobs += [(("v1", i), "dve") for i in range(NT)]
    jobs += [(("kn", j), "act") for j in range(KC)]
    jobs += [(("ctx",), "dve")]
    jobs += [(("oT", j), "act") for j in range(KC)]
    jobs += [(("y1", i), "dve") for i in range(NT)]
    for i in range(NT + 1):
        for h in range(H):
            jobs += [(("exT", i - 1, h), "act")] if i >= 1 else []
            jobs += [(("pair", i, h), "dve")] if i < NT else []
        jobs += [(("att", i - 1), "dve")] if i >= 1 else []
    jobs += [(("xnT", 3, i), "act") for i in range(NT)]
    jobs += [(("f1", i), "dve") for i in range(NT)]
    for i in range(NT):
        jobs += [(("f1T", i), "act"), (("f1o", i), "dve")]
    return jobs


def lagged(first, second, lag=1):
    out = []
    for i in range(NT + lag):
        if i < NT:
            out += first(i)
        if i >= lag:
            out += second(i - lag)
    return out


class PsumRing:

    SLOTS = 4

    def __init__(self, psum, filled, emptied):
        self.psum, self.filled_sem, self.emptied_sem = psum, filled, emptied
        self.place, self.nth, count = {}, [], {"act": 0, "dve": 0}
        for k, (name, who) in enumerate(psum_jobs()):
            count[who] += 1
            self.place[name] = k
            self.nth.append((who, count[who]))

    def slot(self, name):
        return self.psum[self.place[name] % self.SLOTS]

    def claim(self, pe, name):
        k = self.place[name]
        if k >= self.SLOTS:
            who, n = self.nth[k - self.SLOTS]
            pe.wait_ge(self.emptied_sem[who], n)
        return self.slot(name)

    def filled(self, last_matmul):
        last_matmul.then_inc(self.filled_sem, 1)

    def wait_filled(self, eng, name):
        eng.wait_ge(self.filled_sem, self.place[name] + 1)
        return self.slot(name)

    def emptied(self, last_read, name):
        last_read.then_inc(self.emptied_sem[self.nth[self.place[name]][0]], 1)

    def wait_emptied(self, eng, name):
        who, n = self.nth[self.place[name]]
        eng.wait_ge(self.emptied_sem[who], n)


class Steps:

    def __init__(self, eng, sem):
        self.eng, self.sem, self.n = eng, sem, 0

    def did(self, ins):
        ins.then_inc(self.sem, 1)
        self.n += 1
        return self.n

    def wait(self, n=None):
        self.eng.wait_ge(self.sem, self.n if n is None else n)


def build_gps(nc, a, out):
    with ExitStack() as ctx:
        def sb(name, shape, dt=F32):
            return ctx.enter_context(nc.sbuf_tensor(name, shape, dt))

        signals = {}

        def sig(name):
            if name not in signals:
                signals[name] = ctx.enter_context(nc.semaphore(name))
            return signals[name]

        ps = ctx.enter_context(nc.psum_tensor("ps", [128, 4096], F32))
        ring = PsumRing([ps[:, 1024 * s:1024 * (s + 1)] for s in range(4)], sig("psum_filled"),
                        {"act": sig("scalar_emptied"), "dve": sig("vector_emptied")})

        table = nc.dram_tensor("table", (N, TABLE), F32, kind="Internal").ap()
        pairs = nc.dram_tensor("pairs", (N * N, H), F32, kind="Internal").ap()
        pairs_by_src = pairs.rearrange("(i p d) h -> i p (d h)", p=P, d=N)

        x = sb("x", [P, NT, D])
        counts = sb("counts", [P, NT, N])
        ident = sb("ident", [128, 128])
        cols = sb("cols", [128, COL_LEN])
        srci = sb("srci", [P, ET], I32)
        dsti = sb("dsti", [P, ET], I32)
        pairi = sb("pairi", [P, ET], I32)
        tcol = sb("tcol", [128, LAYERS])
        one_row = sb("one_row", [H, P])
        stat = sb("stat", [P, 6 * 16])
        small = sb("small", [128, 64 * 16])
        xn = sb("xn", [P, NT, D])
        xnT = sb("xnT", [128, KC, N])
        arena = sb("arena", [128, 40500])

        def view(at, *shape, parts=128):
            n = 1
            for s in shape:
                n *= s
            v = arena[0:parts, at:at + n]
            if len(shape) == 2:
                v = v.rearrange("p (a b) -> p a b", a=shape[0])
            if len(shape) == 3:
                v = v.rearrange("p (a b c) -> p a b c", a=shape[0], b=shape[1])
            return v

        def sm(k, *shape, parts=P):
            n = 1
            for s in shape:
                n *= s
            v = small[0:parts, 64 * k:64 * k + n]
            return v.rearrange("p (a b) -> p a b", a=shape[0]) if len(shape) == 2 else v

        def col(name, k, lo=0, hi=128):
            at = COL_AT[name][0] + k
            return cols[lo:hi, at:at + 1]

        def row(name, parts=P, lo=0, n=None):
            at, full = ROW_AT[name]
            n = n or full
            return a["rows"][at + lo:at + lo + n].partition_broadcast(parts)

        w1 = view(0, KC, HID)
        w2 = view(4096, HC, D)
        cw = view(8192, KC, D)
        b1r = view(10240, HID, parts=P)
        b2r = view(11264, D, parts=P)
        lngr = view(11776, D, parts=P)
        lnbr = view(12288, D, parts=P)
        biasr = view(12800, 2 * D, parts=P)
        G0 = 13824
        ytmp = view(28672, D, parts=P)
        iota16z = view(39500, 256, parts=P).bitcast(F16)
        ex = view(G0, NT, D, parts=P)
        exm = view(G0 + 2560, NT, D, parts=P)
        gT = view(G0, HC, N)
        hT = view(G0 + 5120, KC, N)
        u = view(G0 + 7680, 2, HID, parts=P)
        xl = view(G0 + 9728, NT, D, parts=P)
        xlT = view(G0 + 12288, KC, N)
        one_hot = view(G0 + 14848, ONE_HOTS * N, parts=P).bitcast(F16) \
            .rearrange("p (k s n) -> p k s n", k=ONE_HOTS, s=2)
        iota16 = view(G0 + 14848 + ONE_HOTS * N, 320, parts=P).bitcast(F16)[:, 0:N]
        iotai = view(G0, N, parts=P)
        fill = view(G0 + 2560, N * H, parts=P)
        srcf = view(G0 + 1024, ET, parts=P)
        dstf = view(G0 + 1152, ET, parts=P)
        pairf = view(G0 + 1280, ET, parts=P)
        wqkv = view(0, KC, 3 * D)
        wo = view(6144, KC, D)
        qkvr = view(10240, 3 * D, parts=P)
        M0 = 13824
        qk = view(M0, NT, 2 * D, parts=P)
        th = view(M0 + 5120, NT, 2 * D, parts=P)
        qf = view(M0 + 10240, NT, 2 * D, parts=P)
        kf = view(M0 + 15360, NT, 2 * D, parts=P)
        va = view(M0 + 20480, NT, H * (HD + 1), parts=P)
        k3 = view(M0 + 23080, NT, D, parts=P)
        kv = view(8192, H * (HD + 1))
        q2 = qk[:, :, 0:D]
        qfT = view(M0 + 5120, 2, H * P)
        mo = view(M0 + 7200, 2, D, parts=P)
        moT = view(M0 + 8300, 2, KC * P)
        f0w1 = view(0, KC, D)
        f0w2 = view(2048, KC, D)
        f0wg = view(4096, KC, H)
        f0b2 = view(4200, D, parts=H)
        f0b1r = view(12800, D, parts=P)
        fh = view(G0, NT, D, parts=P)
        fg1 = view(G0 + 2560, NT, D, parts=P)
        fg2 = view(G0 + 5120, NT, D, parts=P)
        fT = view(G0 + 7680, 2, KC * P)
        wer = view(4800, KC, 2 * D)
        ar = view(8896, 4, D, parts=P)
        hr = view(10944, NT * TABLE, parts=P).rearrange("p (i c) -> p i c", i=NT)
        hea = view(13584, NT, H * (HD + 1), parts=P)
        hrT = view(16184, KC, N)
        hrTs = view(18684, KC, N)
        gs = view(21200, GATHERS, TABLE, parts=P)
        gd = view(23312, GATHERS, TABLE, parts=P)
        dif = view(25424, GATHERS, D, parts=P)
        tmp = view(25424, 3, D, parts=P)
        sc = view(27472, GATHERS, H, parts=P)
        ix = arena[0:P, 27520:27520 + 3 * GATHERS].bitcast(I32)
        wqkv1 = view(27600, KC, 3 * D)
        ek = view(33744, KC, N)
        kn = view(27600, NT, D, parts=P)
        qT = view(36300, KC, N)
        v1 = xn
        wo1 = view(0, KC, D)
        ctxb = view(2048, KC, 128)
        oT = view(30200, KC, N)
        v1r = view(38800, D, parts=P)
        b1or = view(39312, D, parts=P)
        DT = N * H
        pt = [view(21200 + DT * s, DT, parts=P) for s in range(2)]
        S = view(31200, H, N, parts=P)
        exTh = view(5600, H, N, parts=P)
        otmp = view(11000, D, parts=P)
        f1w = view(0, KC, WX)
        f1w2 = view(2336, KC, D)
        f1w3 = view(4384, D, parts=HD + H + 1)
        f1r = view(4896, WX, parts=P)
        g1 = view(G0, NT, WX + 1, parts=P)
        g1T = view(G0 + 3000, 2, 640)

        mv = sm(0, NT, 2)
        rstd = sm(1, NT)
        nrm2 = small[0:P, 256:336]
        rn = small[0:P, 336:416]
        tn = small[0:P, 416:496]
        pw = small[0:P, 496:536].rearrange("p (i h) -> p i h", i=NT)
        zmax = small[:, 540:541]
        zall = small[:, 541:542]
        zneg = small[:, 542:543]
        lg8 = small[0:P, 544:584].rearrange("p (i h) -> p i h", i=NT)
        top8 = small[0:P, 584:624].rearrange("p (i h) -> p i h", i=NT)
        idx8 = small[0:P, 624:664].bitcast(U32).rearrange("p (i h) -> p i h", i=NT)
        idf8 = small[0:P, 664:704].rearrange("p (i h) -> p i h", i=NT)
        p12 = small[0:P, 704:724].rearrange("p (k i) -> p k i", k=4)
        io8 = small[0:P, 724:732]
        kmax = small[:, 732:736]
        ksum = small[:, 736:740]
        krec = small[:, 740:744]
        smax = small[0:P, 744:824].rearrange("p (k h) -> p k h", h=H)
        rden = small[0:P, 824:840]
        e8 = small[0:P, 840:872].rearrange("p (k h) -> p k h", h=H)
        tnew = small[0:P, 880:960]

        HALVES = [(0, 512), (512, N)]

        block = ctx.enter_context(nc.Block())

        @block.sync
        def _(sp):
            def load(dst, src, name):
                sp.dma_start(dst, src).then_inc(sig(name), 16)

            def w(name):
                return a[name].rearrange("(k p) n -> p k n", p=128)

            load(srci[:, :], a["src"].rearrange("(p t) -> p t", t=ET), "edges_loaded")
            load(dsti[:, :], a["dst"].rearrange("(p t) -> p t", t=ET), "edges_loaded")
            load(x[:, :, :], a["x"].rearrange("(i p) d -> p i d", p=P), "x_loaded")
            load(cols[:, :], a["cols"], "cols_loaded")
            load(tcol[:, :], row("t", 128), "cols_loaded")
            load(wqkv, w("qkv_w"), "mix0_loaded")
            load(wo, w("out_w"), "mix0_loaded")
            load(qkvr, row("qkv_b"), "mix0_loaded")
            sp.wait_ge(sig("fill_ready"), 1)
            for i in range(NT):
                load(pairs_by_src[i], fill, "pairs_filled")
            ring.wait_emptied(sp, ("mw", NT - 1))
            load(w1, w("mw1_0"), "w1_loaded")
            load(w2, w("mw2_0"), "w2_loaded")
            load(cw, w("cw")[:, 0:KC, :], "cw_loaded")
            load(b1r, row("mb1_0"), "b1_loaded")
            load(b2r, row("mb2_0"), "b2_loaded")
            load(biasr[:, 0:D], row("out_b"), "bias_loaded")
            load(biasr[:, D:2 * D], row("cb"), "bias_loaded")
            for l in range(1, LAYERS):
                ring.wait_emptied(sp, ("u", l - 1, NT - 1))
                load(w1, w(f"mw1_{l}"), "w1_loaded")
                load(b1r, row(f"mb1_{l}"), "b1_loaded")
                ring.wait_emptied(sp, ("y", l - 1, NT - 1))
                load(w2, w(f"mw2_{l}"), "w2_loaded")
                load(b2r, row(f"mb2_{l}"), "b2_loaded")
                if l > 1:
                    sp.wait_ge(sig("xl_ready"), NT * (l - 1))
                load(lngr, row(f"lng_{l}"), "lng_loaded")
                load(lnbr, row(f"lnb_{l}"), "lng_loaded")
                ring.wait_emptied(sp, ("cw", l - 1, NT - 1))
                load(cw, w("cw")[:, KC * l:KC * (l + 1), :], "cw_loaded")
            ring.wait_emptied(sp, ("u", LAYERS - 1, NT - 1))
            load(f0w1, w("f0_w1"), "f0_loaded")
            ring.wait_emptied(sp, ("y", LAYERS - 1, NT - 1))
            load(f0w2, w("f0_w2"), "f0_loaded")
            load(f0wg, w("f0_wg"), "f0_loaded")
            load(f0b2, a["f0_b2"], "f0_loaded")
            load(f0b1r, row("f0_b1"), "f0_loaded")
            ring.wait_emptied(sp, ("cw", LAYERS - 1, NT - 1))
            load(wer, w("w_er"), "gat_loaded")
            for n, name in enumerate(("a_abs", "a_src", "a_dst", "a_dif")):
                load(ar[:, n, :], row(name), "gat_loaded")
            ring.wait_emptied(sp, ("f0o", NT - 1))
            load(wqkv1, w("w_qkvT"), "mix1_loaded")
            load(wo1, w("w_outT"), "mix1_loaded")
            load(v1r, row("v_b"), "mix1_loaded")
            load(b1or, row("b_out"), "mix1_loaded")
            sp.wait_ge(sig("table_ready"), NT)
            load(table.rearrange("(i p) c -> p i c", p=P), hr, "table_stored")
            sp.wait_ge(sig("scattered"), 16 * ET)
            ring.wait_emptied(sp, ("y1", NT - 1))
            for i in range(NT):
                if i >= 2:
                    ring.wait_emptied(sp, ("pair", i - 2, H - 1))
                load(pt[i % 2], pairs_by_src[i], f"pairs_loaded_{i % 2}")
                if i == 0:
                    load(f1w, w("f1_w"), "f1_loaded")
                    load(f1w2, w("f1_w2"), "f1_loaded")
                    load(f1w3, a["f1_w3"], "f1_loaded")
                    load(f1r, row("f1_b"), "f1_loaded")
            for i in range(NT):
                ring.wait_emptied(sp, ("f1o", i))
                load(out[P * i:P * (i + 1), :], x[:, i, :], "out_stored")
            sp.wait_ge(sig("out_stored"), 16 * NT)

        @block.gpsimd
        def _(pool):
            st = Steps(pool, sig("pool_step"))
            st.did(pool.iota(iotai, pattern=[[1, N]], base=0, channel_multiplier=0,
                             allow_small_or_imprecise_dtypes=True))
            st.did(pool.memset(ident[:, :], 0.0))
            st.wait()
            pool.affine_select(out=ident[:, :], in_=ident[:, :], compare_op=ALU.not_equal, fill=1.0,
                               base=0, pattern=[[-1, 128]],
                               channel_multiplier=1).then_inc(sig("ident_ready"), 1)
            pool.memset(fill, NO_EDGE).then_inc(sig("fill_ready"), 1)
            pool.memset(one_row[:, :], 2.0).then_inc(sig("ones_ready"), 1)
            pool.iota(io8, pattern=[[1, H]], base=0, channel_multiplier=0,
                      allow_small_or_imprecise_dtypes=True).then_inc(sig("ones_ready"), 1)
            pool.wait_ge(sig("k_abs"), NT)
            st.did(pool.tensor_tensor(k3, k3, qk[:, :, D:2 * D], ALU.mult))
            st.wait()
            pool.tensor_tensor(k3, k3, qk[:, :, D:2 * D], ALU.mult).then_inc(sig("k_cubed"), 1)
            for l in range(LAYERS):
                pool.wait_ge(sig("zmax_ready"), l + 1)
                pool.partition_all_reduce(zall, zmax, 128, RMAX).then_inc(sig("zall_ready"), 1)
            pool.wait_ge(sig("table_stored"), 16)
            pool.wait_ge(sig("pairs_filled"), 16 * NT)

            def gather(k):
                pool.indirect_dma_start(
                    out=gs[:, k, :], out_offset=None, in_=table,
                    in_offset=bass.IndirectOffsetOnAxis(ap=ix[:, 3 * k:3 * k + 1], axis=0)
                ).then_inc(sig(f"gathered_{k}"), 16)
                pool.indirect_dma_start(
                    out=gd[:, k, :], out_offset=None, in_=table,
                    in_offset=bass.IndirectOffsetOnAxis(ap=ix[:, 3 * k + 1:3 * k + 2], axis=0)
                ).then_inc(sig(f"gathered_{k}"), 16)

            def scatter(k):
                pool.indirect_dma_start(
                    out=pairs, out_offset=bass.IndirectOffsetOnAxis(
                        ap=ix[:, 3 * k + 2:3 * k + 3], axis=0),
                    in_=sc[:, k, :], in_offset=None).then_inc(sig("scattered"), 16)

            for k in range(GATHERS):
                pool.wait_ge(sig("indices_ready"), k + 1)
                gather(k)

            def gather_and_scatter(it, k):
                pool.wait_ge(sig("indices_ready"), it * GATHERS + k + 1)
                pool.sem_inc(sig("gathers_begun"), 1)
                gather(k)
                pool.wait_ge(sig("scores_ready"), it * GATHERS + (k - GATHERS + 1))
                if not (isinstance(it, int) and it == 1 and k == 0):
                    pool.wait_ge(sig("scattered"), it * (16 * GATHERS) + 16 * (k - GATHERS))
                pool.sem_inc(sig("scatters_begun"), 1)
                scatter(k)

            for k in range(GATHERS):
                gather_and_scatter(1, k)
            with pool.Fori(2, ET // GATHERS) as it:
                for k in range(GATHERS):
                    gather_and_scatter(it, k)
            for k in range(GATHERS):
                pool.wait_ge(sig("scores_ready"), ET - GATHERS + k + 1)
                pool.wait_ge(sig("scattered"), 16 * (ET - GATHERS + k))
                scatter(k)
            for i in range(NT):
                for h in range(H):
                    pool.wait_ge(sig("pair_exp"), i * H + h + 1)
                    pool.tensor_tensor(S[:, h, :], S[:, h, :], counts[:, i, :],
                                       ALU.mult).then_inc(sig("pair_weighted"), 1)

        @block.tensor
        def _(pe):
            mm = pe.matmul

            def turn(name, src_of, widths, at_of=None):
                slot = ring.claim(pe, name)
                for k, n in enumerate(widths):
                    at = at_of(k)
                    src = src_of(k)
                    rows = src.shape[0]
                    last = pe.transpose(slot[0:n, at:at + rows], src, ident[0:rows, 0:rows])
                ring.filled(last)

            def four_to_bank(k):
                return 512 * (k // 4) + P * (k % 4)

            def product(slot, m, lhsT_of, rhs_of, ks, n, extra=None):
                for lo in range(0, n, 512):
                    hi = min(lo + 512, n)
                    for k in range(ks):
                        last = mm(slot[0:m, lo:hi], lhsT_of(k), rhs_of(k)[:, lo:hi],
                                  start=(k == 0), stop=(k == ks - 1))
                return last

            def nodes(t, i):
                return lambda k: t[:, k, P * i:P * (i + 1)]

            regions = [(512 * i, 0, 512, i) for i in range(NT)] + \
                      [(2560 + (N - 512) * i, 512, N, i) for i in range(4)] + \
                      [(3072, 512, N, 4)]

            pe.wait_ge(sig("zeros_ready"), 1)
            for b in range(7):
                mm(ps[:, 512 * b:512 * (b + 1)], iota16z[:, 0:128], iota16z[:, 0:512],
                   start=True, stop=False, skip_group_check=True)
            with pe.Fori(0, ET // ONE_HOTS) as it:
                for k in range(ONE_HOTS):
                    pe.wait_ge(sig("one_hots_ready"), it * (2 * ONE_HOTS) + 2 * (k + 1))
                    for at, lo, hi, i in regions:
                        last = mm(ps[0:P, at:at + hi - lo], one_hot[:, k, 0, P * i:P * (i + 1)],
                                  one_hot[:, k, 1, lo:hi], start=False, stop=False,
                                  skip_group_check=True)
                    last.then_inc(sig("one_hots_used"), 1)
            pe.wait_ge(sig("counts_ready"), 3)

            def turn_xn(n):
                for i in range(NT):
                    pe.wait_ge(sig("xn_ready"), NT * n + i + 1)
                    turn(("xnT", n, i), lambda k: xn[:, i, 128 * k:128 * (k + 1)], [128] * KC,
                         four_to_bank)

            pe.wait_ge(sig("ident_ready"), 1)
            turn_xn(0)

            pe.wait_ge(sig("mix0_loaded"), 48)
            for i in range(NT):
                ring.wait_emptied(pe, ("xnT", 0, i))
                slot = ring.claim(pe, ("qk", i))
                ring.filled(product(slot, P, nodes(xnT, i), lambda k: wqkv[:, k, :], KC, 2 * D))
                slot = ring.claim(pe, ("v", i))
                ring.filled(product(slot, P, nodes(xnT, i), lambda k: wqkv[:, k, 2 * D:], KC, D))
            pe.wait_ge(sig("kf_ready"), NT)
            pe.wait_ge(sig("va_ones"), 1)
            slot = ring.claim(pe, ("kv",))
            for h in range(H):
                at = 512 * (h // 4) + (HD + 1) * (h % 4)
                for i in range(NT):
                    last = mm(slot[:, at:at + HD + 1], kf[:, i, 128 * h:128 * (h + 1)],
                              va[:, i, (HD + 1) * h:(HD + 1) * (h + 1)],
                              start=(i == 0), stop=(i == NT - 1), skip_group_check=True)
            ring.filled(last)
            for i in range(NT + 1):
                if i < NT:
                    pe.wait_ge(sig("qf_ready"), i + 1)
                    turn(("qfT", i), lambda k: qf[:, i, 128 * k:128 * (k + 1)], [128] * H,
                         four_to_bank)
                    slot = ring.claim(pe, ("mo", i))
                    ring.wait_emptied(pe, ("kv",))
                    ring.wait_emptied(pe, ("qfT", i))
                    for h in range(H):
                        at = 512 * (h // 4) + (HD + 1) * (h % 4)
                        last = mm(slot[0:P, at:at + HD + 1], qfT[:, i % 2, P * h:P * (h + 1)],
                                  kv[:, (HD + 1) * h:(HD + 1) * (h + 1)], start=True, stop=True)
                    ring.filled(last)
                if i >= 1:
                    j = i - 1
                    pe.wait_ge(sig("mo_ready"), j + 1)
                    turn(("moT", j), lambda k: mo[:, j % 2, 128 * k:128 * (k + 1)], [128] * KC,
                         four_to_bank)
                    slot = ring.claim(pe, ("mw", j))
                    ring.wait_emptied(pe, ("moT", j))
                    ring.filled(product(slot, P, lambda k: moT[:, j % 2, P * k:P * (k + 1)],
                                        lambda k: wo[:, k, :], KC, D))

            for l in range(LAYERS):
                pe.wait_ge(sig("ex_ready"), NT * (l + 1))
                pe.wait_ge(sig("exm_ready"), NT * (l + 1))
                for j in range(KC):
                    for name, t in (("den", ex), ("num", exm)):
                        slot = ring.claim(pe, (name, l, j))
                        ring.filled(product(slot, 128, lambda i: t[:, i, 128 * j:128 * (j + 1)],
                                            lambda i: counts[:, i, :], NT, N))
                pe.wait_ge(sig("w1_loaded"), 16 * (l + 1))
                pe.wait_ge(sig("hT_ready"), KC * (l + 1))
                for i in range(NT + 1):
                    if i < NT:
                        slot = ring.claim(pe, ("u", l, i))
                        ring.filled(product(slot, P, nodes(hT, i), lambda k: w1[:, k, :], KC, HID))
                    if i >= 1:
                        j = i - 1
                        pe.wait_ge(sig("u_normed"), NT * l + i)
                        turn(("gT", l, j), lambda k: u[:, j % 2, 128 * k:128 * (k + 1)],
                             [128] * HC, four_to_bank)
                        slot = ring.claim(pe, ("y", l, j))
                        if j == 0:
                            pe.wait_ge(sig("w2_loaded"), 16 * (l + 1))
                        ring.wait_emptied(pe, ("gT", l, j))
                        ring.filled(product(slot, P, nodes(gT, j), lambda k: w2[:, k, :], HC, D))
                for i in range(NT):
                    if l:
                        pe.wait_ge(sig("xl_ready"), NT * (l - 1) + i + 1)
                    else:
                        ring.wait_emptied(pe, ("y", l, i))
                    turn(("yT", l, i), lambda k: xl[:, i, 128 * k:128 * (k + 1)], [128] * KC,
                         four_to_bank)
                pe.wait_ge(sig("cw_loaded"), 16 * (l + 1))
                for i in range(NT):
                    slot = ring.claim(pe, ("cw", l, i))
                    ring.wait_emptied(pe, ("yT", l, i))
                    ring.filled(product(slot, P, nodes(xlT, i), lambda k: cw[:, k, :], KC, D))

            turn_xn(1)
            pe.wait_ge(sig("f0_loaded"), 80)
            for i in range(NT):
                slot = ring.claim(pe, ("f0", i))
                ring.wait_emptied(pe, ("xnT", 1, i))
                product(slot, P, nodes(xnT, i), lambda k: f0w1[:, k, :], KC, D)
                ring.filled(product(slot[:, 512:], P, nodes(xnT, i), lambda k: f0wg[:, k, :], KC, H))
            for i in range(NT):
                pe.wait_ge(sig("fg_ready"), i + 1)
                turn(("f0T", i), lambda k: fg1[:, i, 128 * k:128 * (k + 1)], [128] * KC,
                     four_to_bank)
                slot = ring.claim(pe, ("f0o", i))
                ring.wait_emptied(pe, ("f0T", i))
                for k in range(KC):
                    mm(slot[0:P, 0:D], fT[:, i % 2, P * k:P * (k + 1)], f0w2[:, k, :],
                       start=(k == 0), stop=False)
                ring.filled(mm(slot[0:P, 0:D], one_row[:, :], f0b2, start=False, stop=True))

            turn_xn(2)
            pe.wait_ge(sig("gat_loaded"), 80)
            for i in range(NT):
                slot = ring.claim(pe, ("hre", i))
                ring.wait_emptied(pe, ("xnT", 2, i))
                ring.filled(product(slot, P, nodes(xnT, i), lambda k: wer[:, k, :], KC, 2 * D))
            for i in range(NT):
                ring.wait_emptied(pe, ("hre", i))
                turn(("hrT", i), lambda k: hr[:, i, 128 * k:128 * (k + 1)], [128] * KC,
                     four_to_bank)

            pe.wait_ge(sig("mix1_loaded"), 64)
            for j in range(KC):
                for name, lo in (("kT", D), ("qT", 0)):
                    slot = ring.claim(pe, (name, j))
                    ring.filled(product(
                        slot, 128, lambda k: wqkv1[:, k, lo + 128 * j:lo + 128 * (j + 1)],
                        lambda k: xnT[:, k, :], KC, N))
            for i in range(NT):
                slot = ring.claim(pe, ("v1", i))
                ring.filled(product(slot, P, nodes(xnT, i), lambda k: wqkv1[:, k, 2 * D:], KC, D))
            for j in range(KC):
                pe.wait_ge(sig("ek_ready"), j + 1)
                turn(("kn", j), lambda k: ek[:, j, P * k:P * (k + 1)], [P] * NT, lambda k: 128 * k)
            slot = ring.claim(pe, ("ctx",))
            ring.wait_emptied(pe, ("kn", KC - 1))
            ring.wait_emptied(pe, ("v1", NT - 1))
            for j in range(KC):
                for i in range(NT):
                    last = mm(slot[:, 128 * j:128 * (j + 1)], kn[:, i, 128 * j:128 * (j + 1)],
                              v1[:, i, 128 * j:128 * (j + 1)], start=(i == 0),
                              stop=(i == NT - 1), skip_group_check=True)
            ring.filled(last)
            ring.wait_emptied(pe, ("ctx",))
            for j in range(KC):
                slot = ring.claim(pe, ("oT", j))
                ring.filled(product(slot, 128, lambda k: ctxb[:, j, :],
                                    lambda k: qT[:, j, :], 1, N))
            ring.wait_emptied(pe, ("oT", KC - 1))
            for i in range(NT):
                slot = ring.claim(pe, ("y1", i))
                ring.filled(product(slot, P, nodes(oT, i), lambda k: wo1[:, k, :], KC, D))

            pe.wait_ge(sig("hrTs_ready"), 1)
            for i in range(NT + 1):
                j = i - 1
                for h in range(H):
                    if i >= 1:
                        pe.wait_ge(sig("pair_weighted"), j * H + h + 1)
                        turn(("exT", j, h), lambda k: S[:, h, P * k:P * (k + 1)], [P] * NT,
                             lambda k: 128 * k)
                    if i < NT:
                        slot = ring.claim(pe, ("pair", i, h))
                        lo = HD * (h % 2)
                        ring.filled(product(
                            slot, P, lambda k: hrTs[lo:lo + HD, h // 2, P * i:P * (i + 1)],
                            lambda k: hrT[lo:lo + HD, h // 2, :], 1, N))
                if i >= 1:
                    slot = ring.claim(pe, ("att", j))
                    for h in range(H):
                        ring.wait_emptied(pe, ("exT", j, h))
                        at = 512 * (h // 4) + (HD + 1) * (h % 4)
                        for k in range(NT):
                            last = mm(slot[0:P, at:at + HD + 1],
                                      exTh[:, h, P * k:P * (k + 1)],
                                      hea[:, k, (HD + 1) * h:(HD + 1) * (h + 1)],
                                      start=(k == 0), stop=(k == NT - 1), skip_group_check=True)
                    ring.filled(last)

            turn_xn(3)
            pe.wait_ge(sig("f1_loaded"), 64)
            for i in range(NT):
                slot = ring.claim(pe, ("f1", i))
                ring.wait_emptied(pe, ("xnT", 3, i))
                ring.filled(product(slot, P, nodes(xnT, i), lambda k: f1w[:, k, :], KC, WX))
            KX = HD + H + 1
            for i in range(NT):
                pe.wait_ge(sig("g1_ready"), i + 1)
                turn(("f1T", i), lambda k: g1[:, i, 128 * k:min(128 * (k + 1), WX + 1)],
                     [128] * KC + [KX], four_to_bank)
                slot = ring.claim(pe, ("f1o", i))
                ring.wait_emptied(pe, ("f1T", i))
                for k in range(KC):
                    mm(slot[0:P, 0:D], g1T[:, i % 2, P * k:P * (k + 1)], f1w2[:, k, :],
                       start=(k == 0), stop=False)
                ring.filled(mm(slot[0:P, 0:D], g1T[0:KX, i % 2, 512:512 + P], f1w3,
                               start=False, stop=True))

        @block.scalar
        def _(act):
            st = Steps(act, sig("scalar_step"))
            ln = [0]

            def rsqrt(dst, src, eps=0.0):
                st.did(act.activation(dst, src, ACT.Ln, bias=eps))
                st.wait()
                act.activation(dst, dst, ACT.Exp, scale=-0.5).then_inc(sig("rsqrt_ready"), 1)
                ln[0] += 1

            def ln_tile(n):
                act.wait_ge(sig("variance_ready"), n + 1)
                i = n % NT
                rsqrt(rstd[:, i:i + 1], mv[:, i, 1:2])

            def copy(dst, src):
                return act.activation(dst, src, ACT.Copy)

            def empty_turned(name, dst, n, k=KC):
                slot = ring.wait_filled(act, name)
                ring.emptied(copy(dst, slot[0:128, 0:k * P].rearrange("p (k n) -> p k n", k=k)),
                             name)

            def xn_turned(n):
                for i in range(NT):
                    empty_turned(("xnT", n, i), xnT[:, :, P * i:P * (i + 1)], P)

            lns = [0]

            def lns_next(k=1):
                for _ in range(k):
                    ln_tile(lns[0])
                    lns[0] += 1

            lns_next(NT)
            act.wait_ge(sig("one_hots_used"), ET)
            act.activation(counts[:, 3, 0:512], ps[0:P, 1536:2048], ACT.Copy)\
               .then_inc(sig("counts_ready"), 1)
            act.activation(counts[:, 4, 0:512], ps[0:P, 2048:2560], ACT.Copy)\
               .then_inc(sig("counts_ready"), 1)
            xn_turned(0)

            for i in range(NT):
                ring.wait_emptied(act, ("qk", i))
                act.activation(th[:, i, :], qk[:, i, :], ACT.Square).then_inc(sig("squares"), 1)
                act.activation(k3[:, i, :], qk[:, i, D:], ACT.Abs).then_inc(sig("k_abs"), 1)
            act.wait_ge(sig("square_sums"), NT)
            rsqrt(rn, nrm2)
            act.wait_ge(sig("norms_ready"), 1)
            act.activation(pw, tn[:, 0:NT * 2 * H].rearrange("p (i s h) -> p i s h", i=NT, s=2)
                           [:, :, 0, :], ACT.Tanh).then_inc(sig("tanh_norm"), 1)
            for i in range(NT):
                act.wait_ge(sig("scaled"), i + 1)
                act.wait_ge(sig("k_cubed"), 1)
                st.did(act.activation(q2[:, i, :], th[:, i, 0:D], ACT.Square))
            for i in range(NT):
                st.wait(st.n - NT + 1)
                st.did(act.activation(th[:, i, :], th[:, i, :], ACT.Tanh, scale=20.0))
            st.wait()
            for i in range(NT):
                for f, s, n in ((qf, 0, "q_angles"), (kf, 1, "k_angles")):
                    o = f[:, i, :].rearrange("p (h c e) -> p h c e", h=H, c=2)
                    t = th[:, i, D * s:D * (s + 1)].rearrange("p (h e) -> p h e", h=H)
                    act.activation(o[:, :, 0, :], t, ACT.Sin, scale=PI / 4, bias=PI / 2)\
                       .then_inc(sig(n), 1)
                    act.activation(o[:, :, 1, :], t, ACT.Sin, scale=PI / 4).then_inc(sig(n), 1)
            for i in range(NT):
                act.activation(q2[:, i, :], q2[:, i, :], ACT.Ln, bias=1e-19)\
                   .then_inc(sig("q_logs"), 1)
            for i in range(NT):
                act.wait_ge(sig("q_powers"), i + 1)
                act.activation(q2[:, i, :], q2[:, i, :], ACT.Exp).then_inc(sig("q_feats"), 1)
            for i in range(NT + 1):
                if i < NT:
                    slot = ring.wait_filled(act, ("qfT", i))
                    if i >= 2:
                        ring.wait_emptied(act, ("mo", i - 2))
                    o = qfT[:, i % 2, :].rearrange("p (b n) -> p b n", b=2)
                    v = slot.rearrange("p (b n) -> p b n", b=2)[:, :, 0:4 * P]
                    ring.emptied(copy(o, v), ("qfT", i))
                    lns_next()
                if i >= 1:
                    j = i - 1
                    slot = ring.wait_filled(act, ("moT", j))
                    if j >= 2:
                        ring.wait_emptied(act, ("mw", j - 2))
                    for k in range(KC):
                        last = act.activation(moT[:, j % 2, P * k:P * (k + 1)],
                                              slot[:, P * k:P * (k + 1)], ACT.Identity,
                                              scale=col("ln_g", k), bias=col("ln_b", k))
                    ring.emptied(last, ("moT", j))

            for l in range(LAYERS):
                act.wait_ge(sig("zneg_ready"), l + 1)
                for i in range(NT):
                    act.activation(ex[:, i, :], ex[:, i, :], ACT.Exp, bias=zneg[0:P, :])\
                       .then_inc(sig("ex_ready"), 1)
                for i in range(NT + 1):
                    if i < NT:
                        lns_next()
                    if i >= 1:
                        j = i - 1
                        slot = ring.wait_filled(act, ("gT", l, j))
                        for k in range(HC):
                            at = 512 * (k // 4) + P * (k % 4)
                            last = act.activation(gT[:, k, P * j:P * (j + 1)], slot[:, at:at + P],
                                                  ACT.Relu, scale=col(f"mlg_{l}", k),
                                                  bias=col(f"mlb_{l}", k))
                        ring.emptied(last, ("gT", l, j))
                        if l:
                            lns_next()
                for i in range(NT):
                    empty_turned(("yT", l, i), xlT[:, :, P * i:P * (i + 1)], P)

            lns_next(NT)
            xn_turned(1)
            act.wait_ge(sig("f0_gap"), 1)
            act.activation(p12[:, 0, :], p12[:, 1, :], ACT.Exp).then_inc(sig("f0_exp"), 1)
            for i in range(NT):
                act.wait_ge(sig("f0_in"), i + 1)
                act.activation(fg1[:, i, :], fg1[:, i, :], ACT.Gelu).then_inc(sig("f0_gelu"), 1)
                act.activation(fg2[:, i, :], fg2[:, i, :], ACT.Gelu).then_inc(sig("f0_gelu"), 1)
            for i in range(NT):
                if i >= 2:
                    ring.wait_emptied(act, ("f0o", i - 2))
                slot = ring.wait_filled(act, ("f0T", i))
                ring.emptied(copy(fT[:, i % 2, :], slot[:, 0:KC * P]), ("f0T", i))

            lns_next(NT)
            xn_turned(2)
            for i in range(NT):
                empty_turned(("hrT", i), hrT[:, :, P * i:P * (i + 1)], P)
            for j in range(KC):
                slot = ring.wait_filled(act, ("kT", j))
                ring.emptied(act.activation(ek[:, j, :], slot[:, 0:N], ACT.Identity,
                                            bias=col("k_b", j)), ("kT", j))
                slot = ring.wait_filled(act, ("qT", j))
                ring.emptied(act.activation(qT[:, j, :], slot[:, 0:N], ACT.Identity,
                                            bias=col("q_b", j)), ("qT", j))
            for j in range(KC):
                act.wait_ge(sig("kmax_ready"), j + 1)
                act.activation(ek[:, j, :], ek[:, j, :], ACT.Exp, bias=kmax[:, j:j + 1],
                               accum_out=ksum[:, j:j + 1]).then_inc(sig("ek_ready"), 1)
            ring.wait_emptied(act, ("v1", NT - 1))
            for j in range(KC):
                slot = ring.wait_filled(act, ("kn", j))
                ring.emptied(copy(kn[:, :, 128 * j:128 * (j + 1)],
                                  slot[0:P, 0:NT * 128].rearrange("p (i c) -> p i c", i=NT)),
                             ("kn", j))
            for j in range(KC):
                slot = ring.wait_filled(act, ("oT", j))
                ring.emptied(copy(oT[:, j, :], slot[:, 0:N]), ("oT", j))

            with act.Fori(0, ET // GATHERS) as it:
                for k in range(GATHERS):
                    act.wait_ge(sig("differences"), it * GATHERS + k + 1)
                    act.activation(dif[:, k, :], dif[:, k, :], ACT.Abs)\
                       .then_inc(sig("abs_ready"), 1)
            for i in range(NT + 1):
                if i < NT:
                    pass
                if i >= 1:
                    j = i - 1
                    for h in range(H):
                        act.wait_ge(sig("leaky_ready"), j * H + h + 1)
                        act.activation(S[:, h, :], S[:, h, :], ACT.Exp,
                                       bias=smax[:, 1, h:h + 1]).then_inc(sig("pair_exp"), 1)
                    for h in range(H):
                        slot = ring.wait_filled(act, ("exT", j, h))
                        if j:
                            ring.wait_emptied(act, ("att", j - 1))
                        ring.emptied(copy(exTh[:, h, :].rearrange("p (k n) -> p k n", k=NT),
                                          slot[0:P, 0:NT * 128].rearrange("p (k n) -> p k n", k=NT)
                                          [:, :, 0:P]), ("exT", j, h))

            lns_next(NT)
            xn_turned(3)
            act.wait_ge(sig("f1_gap"), 1)
            act.activation(p12[:, 0, :], p12[:, 1, :], ACT.Exp).then_inc(sig("f1_exp"), 1)
            for i in range(NT):
                if i >= 2:
                    ring.wait_emptied(act, ("f1o", i - 2))
                slot = ring.wait_filled(act, ("f1T", i))
                copy(g1T[:, i % 2, 0:KC * P], slot[:, 0:KC * P])
                ring.emptied(copy(g1T[0:HD + H + 1, i % 2, 512:512 + P],
                                  slot[0:HD + H + 1, 512:512 + P]), ("f1T", i))

        @block.vector
        def _(v):
            st = Steps(v, sig("vector_step"))
            TT, TS, STT = v.tensor_tensor, v.tensor_scalar, v.scalar_tensor_tensor
            lns, rs = [0], [0]

            def refine(r, s):
                rs[0] += 1
                v.wait_ge(sig("rsqrt_ready"), rs[0])
                t = tnew[:, 0:r.shape[1]]
                st.did(TT(t, r, r, ALU.mult))
                st.wait()
                st.did(TT(t, t, s, ALU.mult))
                st.wait()
                st.did(TS(t, t, -0.5, 1.5, ALU.mult, ALU.add))
                st.wait()
                st.did(TT(r, r, t, ALU.mult))

            def ln_stats(parts):
                i = lns[0] % NT
                lns[0] += 1
                for n, part in enumerate(parts):
                    st.did(v.bn_stats(stat[:, 12 * i + 6 * n:12 * i + 6 * (n + 1)], part))
                st.wait()
                st.did(v.bn_aggr(mv[:, i, :], stat[:, 12 * i:12 * i + 6 * len(parts)]))
                st.wait()
                TS(mv[:, i, 1:2], mv[:, i, 1:2], LN_EPS, None, ALU.add)\
                    .then_inc(sig("variance_ready"), 1)

            def ln_apply(dst, src):
                i = lns_done[0] % NT
                v.wait_ge(sig("variance_ready"), lns_done[0] + 1)
                lns_done[0] += 1
                refine(rstd[:, i:i + 1], mv[:, i, 1:2])
                st.wait()
                return TS(dst, src, mv[:, i, 0:1], rstd[:, i:i + 1], ALU.subtract, ALU.mult)

            lns_done = [0]

            def ln_x():
                for i in range(NT):
                    ln_stats([x[:, i, :]])
                for i in range(NT):
                    ln_apply(xn[:, i, :], x[:, i, :]).then_inc(sig("xn_ready"), 1)

            st.did(v.memset(iota16z[:, :], 0.0))
            st.wait()
            v.memset(zmax, -3e38).then_inc(sig("zeros_ready"), 1)
            v.wait_ge(sig("edges_loaded"), 32)
            st.did(v.tensor_copy(srcf, srci[:, :]))
            st.did(v.tensor_copy(dstf, dsti[:, :]))
            v.wait_ge(sig("pool_step"), 1)
            st.did(v.tensor_copy(iota16, iotai))
            st.wait()
            st.did(STT(out=pairf, in0=srcf, scalar=float(N), in1=dstf, op0=ALU.mult, op1=ALU.add))
            st.wait()
            st.did(v.tensor_copy(pairi[:, :], pairf))

            def one_hots(k, t):
                TS(one_hot[:, k, 0, :], iota16, srcf[:, t], None, ALU.is_equal)\
                    .then_inc(sig("one_hots_ready"), 1)
                TS(one_hot[:, k, 1, :], iota16, dstf[:, t], None, ALU.is_equal)\
                    .then_inc(sig("one_hots_ready"), 1)

            for k in range(ONE_HOTS):
                one_hots(k, slice(k, k + 1))
            v.wait_ge(sig("x_loaded"), 16)
            ln_x()
            with v.Fori(1, ET // ONE_HOTS) as it:
                for k in range(ONE_HOTS):
                    v.wait_ge(sig("one_hots_used"), it * ONE_HOTS + (k + 1 - ONE_HOTS))
                    one_hots(k, bass.ds(it * ONE_HOTS + k, 1))
            v.wait_ge(sig("one_hots_used"), ET)
            st.did(v.tensor_copy(counts[:, 0:3, 0:512],
                                 ps[0:P, 0:1536].rearrange("p (i n) -> p i n", i=3)))
            st.did(v.tensor_copy(counts[:, 0:4, 512:N],
                                 ps[0:P, 2560:2560 + 4 * (N - 512)]
                                 .rearrange("p (i n) -> p i n", i=4)))
            st.wait()
            v.tensor_copy(counts[:, 4, 512:N], ps[0:P, 3072:3072 + N - 512])\
                .then_inc(sig("counts_ready"), 1)

            v.wait_ge(sig("mix0_loaded"), 48)
            v.wait_ge(sig("pairs_filled"), 16 * NT)
            v5 = va.rearrange("p i (h e) -> p (i h) e", h=H)
            v.memset(v5[:, :, HD:HD + 1], 1.0).then_inc(sig("va_ones"), 1)
            n2 = nrm2.rearrange("p (i s h) -> p i s h", i=NT, s=2)

            def squares(i):
                v.wait_ge(sig("squares"), i + 1)
                v.tensor_reduce(nrm2[:, 16 * i:16 * (i + 1)],
                                th[:, i, :].rearrange("p (g e) -> p g e", e=HD),
                                AX_X, ALU.add).then_inc(sig("square_sums"), 1)

            for i in range(NT):
                slot = ring.wait_filled(v, ("qk", i))
                ring.emptied(TT(qk[:, i, :], slot[0:P, :], qkvr[:, 0:2 * D], ALU.add), ("qk", i))
                slot = ring.wait_filled(v, ("v", i))
                ring.emptied(TT(va[:, i, :].rearrange("p (h e) -> p h e", h=H)[:, :, 0:HD],
                                slot[0:P, 0:D].rearrange("p (h e) -> p h e", h=H),
                                qkvr[:, 2 * D:].rearrange("p (h e) -> p h e", h=H), ALU.add),
                             ("v", i))
                if i >= 1:
                    squares(i - 1)
            squares(NT - 1)
            v.wait_ge(sig("square_sums"), NT)
            refine(rn, nrm2)
            st.wait()
            TT(tn, nrm2, rn, ALU.mult).then_inc(sig("norms_ready"), 1)
            for i in range(NT):
                TT(th[:, i, :].rearrange("p (g e) -> p g e", e=HD),
                   qk[:, i, :].rearrange("p (g e) -> p g e", e=HD),
                   rn[:, 16 * i:16 * (i + 1)].unsqueeze(2).to_broadcast([P, 16, HD]),
                   ALU.mult).then_inc(sig("scaled"), 1)
            v.wait_ge(sig("tanh_norm"), 1)
            st.did(TS(pw, pw, 1.5, 0.75, ALU.mult, ALU.add))

            def feature(f, m, i):
                o = f[:, i, :].rearrange("p (h c e) -> p h c e", h=H, c=2)
                b = m[:, i, :].rearrange("p (h e) -> p h e", h=H).unsqueeze(2)\
                    .to_broadcast([P, H, 2, HD])
                return TT(o, o, b, ALU.mult)

            v.wait_ge(sig("k_cubed"), 1)
            for i in range(NT):
                v.wait_ge(sig("k_angles"), 2 * (i + 1))
                feature(kf, k3, i).then_inc(sig("kf_ready"), 1)
            st.wait()
            for i in range(NT):
                v.wait_ge(sig("q_logs"), i + 1)
                TT(q2[:, i, :].rearrange("p (h e) -> p h e", h=H),
                   q2[:, i, :].rearrange("p (h e) -> p h e", h=H),
                   pw[:, i, :].unsqueeze(2).to_broadcast([P, H, HD]),
                   ALU.mult).then_inc(sig("q_powers"), 1)
            for i in range(NT):
                v.wait_ge(sig("q_feats"), i + 1)
                v.wait_ge(sig("q_angles"), 2 * (i + 1))
                feature(qf, q2, i).then_inc(sig("qf_ready"), 1)
            slot = ring.wait_filled(v, ("kv",))
            ring.emptied(TS(kv.rearrange("p (b n) -> p b n", b=2),
                            slot.rearrange("p (b n) -> p b n", b=2)[:, :, 0:4 * (HD + 1)],
                            1.0 / N, None, ALU.mult), ("kv",))

            def heads(slot):
                return slot[0:P, :].rearrange("p (b n) -> p b n", b=2)[:, :, 0:4 * (HD + 1)]\
                    .rearrange("p b (h e) -> p b h e", h=4)

            def divide_heads(dst, slot, eps):
                s = heads(slot)
                r = rden[:, 0:H].rearrange("p (b h) -> p b h", b=2)
                st.did(TS(r, s[:, :, :, HD], eps, None, ALU.add))
                st.wait()
                st.did(v.reciprocal(r, r))
                st.wait()
                return TT(dst.rearrange("p (b h e) -> p b h e", b=2, h=4), s[:, :, :, 0:HD],
                          r.unsqueeze(3).to_broadcast([P, 2, 4, HD]), ALU.mult)

            for i in range(NT + 1):
                if i < NT:
                    slot = ring.wait_filled(v, ("mo", i))
                    if i >= 2:
                        ring.wait_filled(v, ("moT", i - 2))
                    ring.emptied(divide_heads(mo[:, i % 2, :], slot, 1e-6), ("mo", i))
                    ring.wait_emptied(v, ("mo", i))
                    ln_stats([mo[:, i % 2, :]])
                    ln_apply(mo[:, i % 2, :], mo[:, i % 2, :]).then_inc(sig("mo_ready"), 1)
                if i >= 1:
                    slot = ring.wait_filled(v, ("mw", i - 1))
                    ring.emptied(TT(x[:, i - 1, :], x[:, i - 1, :], slot[0:P, 0:D], ALU.add),
                                 ("mw", i - 1))
            ring.wait_emptied(v, ("mw", NT - 1))

            v.wait_ge(sig("bias_loaded"), 32)
            for n in range(2):
                st.did(TT(x[:, :, :], x[:, :, :],
                          biasr[:, D * n:D * (n + 1)].unsqueeze(1).to_broadcast([P, NT, D]),
                          ALU.add))
                st.wait()
            v.wait_ge(sig("cols_loaded"), 32)
            for l in range(LAYERS):
                xin, xinT = (xn, xnT) if l == 0 else (xl, xlT)
                if l:
                    ring.wait_emptied(v, ("y", l - 1, NT - 1))
                if l > 1:
                    v.wait_ge(sig("xl_ready"), NT * (l - 1))
                st.did(TS(exm, xin[:, :, :], 0.0, 1e-7, ALU.max, ALU.add))
                st.wait()
                st.did(TS(ex, exm, tcol[0:P, l:l + 1], None, ALU.mult))
                st.wait()
                v.reduce_max(zmax[0:P, :], ex, mybir.AxisListType.XY)\
                    .then_inc(sig("zmax_ready"), 1)
                v.wait_ge(sig("zall_ready"), l + 1)
                TS(zneg, zall, -1.0, HEADROOM, ALU.mult, ALU.add).then_inc(sig("zneg_ready"), 1)
                for i in range(NT):
                    v.wait_ge(sig("ex_ready"), NT * l + i + 1)
                    TT(exm[:, i, :], exm[:, i, :], ex[:, i, :], ALU.mult)\
                        .then_inc(sig("exm_ready"), 1)
                for j in range(KC):
                    slot = ring.wait_filled(v, ("den", l, j))
                    st.did(TS(hT[:, j, :], slot[:, 0:N], 1e-37, None, ALU.max))
                    st.wait()
                    ring.emptied(v.reciprocal(hT[:, j, :], hT[:, j, :]), ("den", l, j))
                    ring.wait_emptied(v, ("den", l, j))
                    slot = ring.wait_filled(v, ("num", l, j))
                    ring.emptied(TT(hT[:, j, :], hT[:, j, :], slot[:, 0:N], ALU.mult),
                                 ("num", l, j))
                    ring.wait_emptied(v, ("num", l, j))
                    if l:
                        ring.wait_emptied(v, ("yT", l - 1, NT - 1))
                    TT(hT[:, j, :], hT[:, j, :], xinT[:, j, :], ALU.add)\
                        .then_inc(sig("hT_ready"), 1)
                v.wait_ge(sig("b1_loaded"), 16 * (l + 1))
                v.wait_ge(sig("b2_loaded"), 16 * (l + 1))
                if l:
                    v.wait_ge(sig("lng_loaded"), 32 * l)
                for i in range(NT + 1):
                    if i < NT:
                        if i >= 2:
                            ring.wait_filled(v, ("gT", l, i - 2))
                        slot = ring.wait_filled(v, ("u", l, i))
                        ring.emptied(TT(u[:, i % 2, :], slot[0:P, :], b1r, ALU.add), ("u", l, i))
                        ring.wait_emptied(v, ("u", l, i))
                        ln_stats([u[:, i % 2, 0:D], u[:, i % 2, D:HID]])
                        ln_apply(u[:, i % 2, :], u[:, i % 2, :]).then_inc(sig("u_normed"), 1)
                    if i >= 1:
                        j = i - 1
                        slot = ring.wait_filled(v, ("y", l, j))
                        if l == 0:
                            ring.emptied(TT(xl[:, j, :], slot[0:P, 0:D], b2r, ALU.add),
                                         ("y", l, j))
                        else:
                            t = ytmp
                            if NT * (l - 1) + j:
                                v.wait_ge(sig("xl_ready"), NT * (l - 1) + j)
                            ring.emptied(TT(t, slot[0:P, 0:D], b2r, ALU.add), ("y", l, j))
                            ring.wait_emptied(v, ("y", l, j))
                            ln_stats([t])
                            st.did(ln_apply(t, t))
                            st.wait()
                            st.did(TT(t, t, lngr, ALU.mult))
                            st.wait()
                            st.did(TT(t, t, lnbr, ALU.add))
                            st.wait()
                            STT(out=xl[:, j, :], in0=t, scalar=0.0, in1=xl[:, j, :],
                                op0=ALU.max, op1=ALU.add).then_inc(sig("xl_ready"), 1)
                for i in range(NT):
                    slot = ring.wait_filled(v, ("cw", l, i))
                    ring.emptied(TT(x[:, i, :], x[:, i, :], slot[0:P, 0:D], ALU.add),
                                 ("cw", l, i))
                ring.wait_emptied(v, ("cw", l, NT - 1))

            ln_x()
            v.wait_ge(sig("f0_loaded"), 80)
            v.wait_ge(sig("ones_ready"), 2)
            for i in range(NT):
                slot = ring.wait_filled(v, ("f0", i))
                st.did(v.tensor_copy(lg8[:, i, :], slot[0:P, 512:512 + H]))
                ring.emptied(v.tensor_copy(fh[:, i, :], slot[0:P, 0:D]), ("f0", i))
            st.wait()
            for i in range(NT):
                st.did(v.max(top8[:, i, :], lg8[:, i, :]))
            st.wait()

            def two_weights(gap, exp):
                TT(p12[:, 1, :], top8[:, :, 1], top8[:, :, 0], ALU.subtract)\
                    .then_inc(sig(gap), 1)
                v.wait_ge(sig(exp), 1)
                st.did(TS(p12[:, 2, :], p12[:, 0, :], 1.0, None, ALU.add))
                st.wait()
                st.did(v.reciprocal(p12[:, 2, :], p12[:, 2, :]))
                st.wait()
                st.did(TT(p12[:, 0, :], p12[:, 0, :], p12[:, 2, :], ALU.mult))
                st.wait()

            two_weights("f0_gap", "f0_exp")
            ring.wait_emptied(v, ("f0", NT - 1))
            for i in range(NT):
                st.did(STT(out=fg1[:, i, :], in0=fh[:, i, :], scalar=p12[:, 2, i:i + 1],
                           in1=f0b1r, op0=ALU.mult, op1=ALU.add))
                STT(out=fg2[:, i, :], in0=fh[:, i, :], scalar=p12[:, 0, i:i + 1],
                    in1=f0b1r, op0=ALU.mult, op1=ALU.add).then_inc(sig("f0_in"), 1)
            for i in range(NT):
                v.wait_ge(sig("f0_gelu"), 2 * (i + 1))
                TT(fg1[:, i, :], fg1[:, i, :], fg2[:, i, :], ALU.add).then_inc(sig("fg_ready"), 1)
            for i in range(NT):
                slot = ring.wait_filled(v, ("f0o", i))
                ring.emptied(TT(x[:, i, :], x[:, i, :], slot[0:P, 0:D], ALU.add), ("f0o", i))
            ring.wait_emptied(v, ("f0o", NT - 1))

            ln_x()
            v.wait_ge(sig("gat_loaded"), 80)
            hea4 = hea.rearrange("p i (h e) -> p i h e", h=H)
            st.did(v.memset(hea.rearrange("p i (h e) -> p (i h) e", h=H)[:, :, HD:HD + 1], 1.0))
            for i in range(NT):
                slot = ring.wait_filled(v, ("hre", i))
                st.did(v.tensor_copy(hea4[:, i, :, 0:HD],
                                     slot[0:P, 0:D].rearrange("p (h e) -> p h e", h=H)))
                ring.emptied(v.tensor_copy(hr[:, i, 0:D], slot[0:P, D:2 * D]), ("hre", i))
                ring.wait_emptied(v, ("hre", i))
                st.wait()
                he_i = hea4[:, i, :, 0:HD]
                for n, t in ((2, he_i), (1, he_i),
                             (3, hr[:, i, 0:D].rearrange("p (h e) -> p h e", h=H))):
                    st.did(TT(tmp[:, n - 1, :].rearrange("p (h e) -> p h e", h=H), t,
                              ar[:, n, :].rearrange("p (h e) -> p h e", h=H), ALU.mult))
                st.wait()
                st.did(v.tensor_reduce(hr[:, i, D:D + H],
                                       tmp[:, 1, :].rearrange("p (h e) -> p h e", h=H),
                                       AX_X, ALU.add))
                st.did(TT(tmp[:, 0, :], tmp[:, 0, :], tmp[:, 2, :], ALU.subtract))
                st.wait()
                v.tensor_reduce(hr[:, i, D + H:D + 2 * H],
                                tmp[:, 0, :].rearrange("p (h e) -> p h e", h=H),
                                AX_X, ALU.add).then_inc(sig("table_ready"), 1)
                v.wait_ge(sig("table_ready"), i + 1)
            ring.wait_emptied(v, ("hrT", NT - 1))
            for j in range(KC):
                ins = TS(hrTs[:, j, :], hrT[:, j, :], col("a_prd", j), col("a_difT", j),
                         ALU.mult, ALU.add)
            ins.then_inc(sig("hrTs_ready"), 1)

            v.wait_ge(sig("mix1_loaded"), 64)
            for j in range(KC):
                ring.wait_emptied(v, ("kT", j))
                v.tensor_reduce(kmax[:, j:j + 1], ek[:, j, :], AX_X, ALU.max, negate=True)\
                    .then_inc(sig("kmax_ready"), 1)
            for i in range(NT):
                slot = ring.wait_filled(v, ("v1", i))
                ring.emptied(TT(v1[:, i, :], slot[0:P, 0:D], v1r, ALU.add), ("v1", i))
            st.did(v.memset(ctxb, 0.0))
            v.wait_ge(sig("ek_ready"), KC)
            st.did(v.reciprocal(krec, ksum))
            st.wait()
            slot = ring.wait_filled(v, ("ctx",))
            for j in range(KC):
                for g in range(2):
                    r = slice(HD * g, HD * (g + 1))
                    last = TS(ctxb[r, j, HD * g:HD * (g + 1)],
                              slot[r, 128 * j + HD * g:128 * j + HD * (g + 1)],
                              krec[r, j:j + 1], None, ALU.mult)
            ring.emptied(last, ("ctx",))
            for i in range(NT):
                slot = ring.wait_filled(v, ("y1", i))
                st.did(TT(x[:, i, :], x[:, i, :], b1or, ALU.add))
                st.wait()
                ring.emptied(TT(x[:, i, :], x[:, i, :], slot[0:P, 0:D], ALU.add), ("y1", i))

            def index(k, t):
                v.tensor_copy(ix[:, 3 * k:3 * k + 1], srci[:, t]).then_inc(sig("gat_step"), 1)
                v.tensor_copy(ix[:, 3 * k + 1:3 * k + 2], dsti[:, t])\
                    .then_inc(sig("indices_ready"), 1)

            def difference(k, landed):
                v.wait_ge(sig(f"gathered_{k}"), landed)
                TT(dif[:, k, :], gs[:, k, 0:D], gd[:, k, 0:D], ALU.subtract)\
                    .then_inc(sig("differences"), 1)
                TT(e8[:, k, :], gs[:, k, D + H:D + 2 * H], gd[:, k, D:D + H], ALU.add)\
                    .then_inc(sig("gat_ends"), 1)

            def score(k, t, number, sent):
                v.wait_ge(sig("abs_ready"), number)
                TT(dif[:, k, :], dif[:, k, :], ar[:, 0, :], ALU.mult)\
                    .then_inc(sig("weighted"), 1)
                v.wait_ge(sig("weighted"), number)
                if sent is not None:
                    v.wait_ge(sig("scattered"), sent)
                v.tensor_reduce(sc[:, k, :], dif[:, k, :].rearrange("p (h e) -> p h e", h=H),
                                AX_X, ALU.add).then_inc(sig("gat_sums"), 1)
                v.tensor_copy(ix[:, 3 * k + 2:3 * k + 3], pairi[:, t])\
                    .then_inc(sig("gat_pairs"), 1)
                v.wait_ge(sig("gat_sums"), number)
                v.wait_ge(sig("gat_ends"), number)
                TT(sc[:, k, :], sc[:, k, :], e8[:, k, :], ALU.add)\
                    .then_inc(sig("scores_ready"), 1)

            for k in range(GATHERS):
                index(k, slice(k, k + 1))
            for k in range(GATHERS):
                difference(k, 32)
                index(k, slice(GATHERS + k, GATHERS + k + 1))
                if k:
                    score(k - 1, slice(k - 1, k), k, None)

            def edge_tile(it, k):
                def ready():
                    difference(k, (it + 1) * 32)
                    index(k, bass.ds((it + 1) * GATHERS + k, 1))
                if k:
                    ready()
                sent = (it - 1) * (16 * GATHERS) + 16 * k
                score((k - 1) % GATHERS, bass.ds(it * GATHERS + (k - 1), 1), it * GATHERS + k,
                      None if isinstance(it, int) and sent == 0 else sent)
                if not k:
                    ready()

            for k in range(GATHERS):
                edge_tile(1, k)
            with v.Fori(2, ET // GATHERS - 1) as it:
                for k in range(GATHERS):
                    edge_tile(it, k)
            LAST = ET - GATHERS
            score(GATHERS - 1, slice(LAST - 1, LAST), LAST, 16 * (LAST - GATHERS))
            for k in range(GATHERS):
                difference(k, 32 * (ET // GATHERS))
                score(k, slice(LAST + k, LAST + k + 1), LAST + k + 1, 16 * (LAST + k + 1 - GATHERS))

            for i in range(NT + 1):
                if i < NT:
                    v.wait_ge(sig(f"pairs_loaded_{i % 2}"), 16 * (i // 2 + 1))
                    p3 = pt[i % 2].rearrange("p (d h) -> p d h", h=H)
                    for h in range(H):
                        if i:
                            ring.wait_filled(v, ("exT", i - 1, h))
                        slot = ring.wait_filled(v, ("pair", i, h))
                        ring.emptied(TT(S[:, h, :], slot[0:P, 0:N], p3[:, :, h], ALU.add),
                                     ("pair", i, h))
                        ring.wait_emptied(v, ("pair", i, h))
                        st.did(v.reduce_max(smax[:, 0, h:h + 1], S[:, h, :], AX_X))
                    st.wait()
                    st.did(TS(smax[:, 2, :], smax[:, 0, :], 0.2, None, ALU.mult))
                    st.wait()
                    if i:
                        v.wait_ge(sig("pair_exp"), H * i)
                    st.did(TT(smax[:, 1, :], smax[:, 0, :], smax[:, 2, :], ALU.max))
                    st.wait()
                    st.did(TS(smax[:, 1, :], smax[:, 1, :], -1.0, None, ALU.mult))
                    st.wait()
                    for h in range(H):
                        STT(out=S[:, h, :], in0=S[:, h, :], scalar=0.2, in1=S[:, h, :],
                            op0=ALU.mult, op1=ALU.max).then_inc(sig("leaky_ready"), 1)
                if i >= 1:
                    j = i - 1
                    slot = ring.wait_filled(v, ("att", j))
                    ring.emptied(divide_heads(otmp, slot, 1e-16), ("att", j))
                    ring.wait_emptied(v, ("att", j))
                    st.did(TT(x[:, j, :], x[:, j, :], otmp, ALU.add))
            st.wait()

            ln_x()
            v.wait_ge(sig("f1_loaded"), 64)
            for i in range(NT):
                slot = ring.wait_filled(v, ("f1", i))
                ring.emptied(TT(g1[:, i, 0:WX], slot[0:P, 0:WX], f1r, ALU.add), ("f1", i))
                ring.wait_emptied(v, ("f1", i))
                st.did(v.tensor_copy(lg8[:, i, :], g1[:, i, WX - H:WX]))
                st.wait()
                st.did(v.max(top8[:, i, :], lg8[:, i, :]))
                st.wait()
                st.did(v.max_index(idx8[:, i, :], top8[:, i, :], lg8[:, i, :]))
            st.wait()
            st.did(v.tensor_copy(idf8, idx8))
            two_weights("f1_gap", "f1_exp")
            for i in range(NT):
                comb = g1[:, i, WX - H:WX]
                st.did(TS(comb, io8, idf8[:, i, 1:2], p12[:, 0, i:i + 1], ALU.is_equal, ALU.mult))
                st.did(TS(lg8[:, i, :], io8, idf8[:, i, 0:1], p12[:, 2, i:i + 1],
                          ALU.is_equal, ALU.mult))
                st.wait()
                st.did(TT(comb, comb, lg8[:, i, :], ALU.add))
                st.did(TS(g1[:, i, D:D + HD], g1[:, i, D:D + HD], 0.0, 0.5, ALU.max, ALU.mult))
                st.did(v.memset(g1[:, i, WX:WX + 1], 0.5))
                st.wait()
                h3 = g1[:, i, 0:D].rearrange("p (h e) -> p h e", h=H)
                STT(out=h3, in0=h3, scalar=0.0, in1=comb.unsqueeze(2).to_broadcast([P, H, HD]),
                    op0=ALU.max, op1=ALU.mult).then_inc(sig("g1_ready"), 1)
            for i in range(NT):
                slot = ring.wait_filled(v, ("f1o", i))
                ring.emptied(TT(x[:, i, :], x[:, i, :], slot[0:P, 0:D], ALU.add), ("f1o", i))


def lay_out(i):
    import numpy as np

    heads = i["L1_gnn_a"].reshape(H, 5, HD).transpose(1, 0, 2).reshape(5, H * HD)
    vec = {f"mb1_{l}": i[f"L0_gnn_mb1_{l}"] for l in range(LAYERS)}
    vec |= {f"mb2_{l}": i[f"L0_gnn_mb2_{l}"] for l in range(LAYERS)}
    vec |= {f"{n}_{l}": i[f"L0_gnn_{n}_{l}"] for l in (1, 2) for n in ("lng", "lnb")}
    vec |= {"qkv_b": i["L0_mix_qkv_b"], "out_b": i["L0_mix_out_b"], "cb": i["L0_gnn_cb"],
            "f0_b1": i["L0_ffn_b1"].reshape(-1), "v_b": i["L1_mix_b_qkv"][2 * D:],
            "b_out": i["L1_mix_b_out"],
            "f1_b": np.concatenate([i["L1_ffn_b1"].reshape(-1), i["L1_ffn_bs1"], i["L1_ffn_bg"]]),
            "a_src": heads[0], "a_dst": heads[1], "a_dif": heads[2], "a_abs": heads[3],
            "t": np.concatenate([i[f"L0_gnn_t{l}"] for l in range(LAYERS)])}
    col = {f"{n}_{l}": i[f"L0_gnn_{n}_{l}"] for l in range(LAYERS) for n in ("mlg", "mlb")}
    col |= {"ln_g": i["L0_mix_ln_g"], "ln_b": i["L0_mix_ln_b"], "q_b": i["L1_mix_b_qkv"][:D],
            "k_b": i["L1_mix_b_qkv"][D:2 * D], "a_prd": heads[4], "a_difT": heads[2]}

    def experts(w):
        return w.transpose(1, 0, 2).reshape(D, H * HD)

    out = {"x": i["x"], "src": i["src"], "dst": i["dst"],
           "rows": np.concatenate([vec[n] for n, _ in ROWS]),
           "cols": np.concatenate([col[n].reshape(-1, 128).T for n, _ in COLS], axis=1)}
    out |= {f"{n}_{l}": i[f"L0_gnn_{n}_{l}"] for l in range(LAYERS) for n in ("mw1", "mw2")}
    out |= {"cw": i["L0_gnn_cw"], "qkv_w": i["L0_mix_qkv_w"], "out_w": i["L0_mix_out_w"],
            "f0_w1": experts(i["L0_ffn_W1"]), "f0_wg": i["L0_ffn_Wg"],
            "f0_w2": i["L0_ffn_W2"].reshape(H * HD, D), "f0_b2": i["L0_ffn_b2"],
            "w_er": np.concatenate([experts(i["L1_gnn_W_e"]), experts(i["L1_gnn_W_r"])], axis=1),
            "w_qkvT": i["L1_mix_W_qkv"].T, "w_outT": i["L1_mix_W_out"].T,
            "f1_w": np.concatenate([experts(i["L1_ffn_W1"]), i["L1_ffn_Ws1"], i["L1_ffn_Wg"]],
                                   axis=1),
            "f1_w2": i["L1_ffn_W2"].reshape(H * HD, D),
            "f1_w3": np.concatenate([i["L1_ffn_Ws2"], i["L1_ffn_b2"],
                                     i["L1_ffn_bs2"].reshape(1, D)])}
    return {n: np.ascontiguousarray(v) for n, v in out.items()}


def kernel(**inputs):
    import numpy as np
    import concourse.bacc as bacc
    from concourse.bass_utils import run_bass_kernel_spmd

    nc = bacc.Bacc("TRN2", target_bir_lowering=False, num_devices=1)
    laid = lay_out({n: np.asarray(v) for n, v in inputs.items()})
    arrays = {f"in_{n}": v for n, v in laid.items()}
    aps = {n: nc.dram_tensor(f"in_{n}", v.shape, mybir.dt.from_np(v.dtype),
                             kind="ExternalInput").ap() for n, v in laid.items()}
    out = nc.dram_tensor("out", (N, D), F32, kind="ExternalOutput").ap()
    build_gps(nc, aps, out)
    return run_bass_kernel_spmd(nc, [arrays], core_ids=[0]).results[0]["out"]
```

```python
from contextlib import ExitStack

import concourse.bass as bass
from concourse import mybir

F32 = mybir.dt.float32
F16 = mybir.dt.float16
F32R = mybir.dt.float32r
I32 = mybir.dt.int32
U32 = mybir.dt.uint32
ALU = mybir.AluOpType
ACT = mybir.ActivationFunctionType
AX_X = mybir.AxisListType.X
RMAX = bass.bass_isa.ReduceOp.max

N, E, D = 625, 10000, 512
P = 125
NT = N // P
ET = E // P
KC = D // 128
HID = 2 * D
HC = HID // 128
H, HD = 8, 64
LAYERS = 3
ONE_HOTS = 8
GATHERS = 4
TABLE = D + 2 * H
HEADROOM = 64.0
ARENA = 40500
HALF = 2 * ((N + 3) // 4)
PACK = 4096.0
CHUNKS = [(0, 3), (3, 6), (6, 10)]
LAG = 3
NO_EDGE = -1e30
LN_EPS = 1e-5
PI = 3.141592653589793
WX = D + HD + H
WIDE = 96
WP = D + WIDE
HW = 4 * WIDE
ROWS = [("mb1_0", HID), ("mb1_1", HID), ("mb1_2", HID), ("mb2_0", D), ("mb2_1", D), ("mb2_2", D),
        ("lng_1", D), ("lnb_1", D), ("lng_2", D), ("lnb_2", D), ("qkv_b", 3 * D), ("out_b", D),
        ("cb", D), ("f0_b1", D), ("v_b", D), ("b_out", D), ("f1_b", WX), ("a_abs", D),
        ("a_src", D), ("a_dst", D), ("a_dif", D), ("t", LAYERS)]
COLS = [("mlg_0", HC), ("mlb_0", HC), ("mlg_1", HC), ("mlb_1", HC), ("mlg_2", HC), ("mlb_2", HC),
        ("ln_g", KC), ("ln_b", KC), ("q_b", KC), ("k_b", KC), ("a_prd", KC), ("a_difT", KC)]


def offsets(parts):
    at, out = 0, {}
    for name, n in parts:
        out[name] = (at, n)
        at += n
    return out, at


ROW_AT, ROW_LEN = offsets(ROWS)
COL_AT, COL_LEN = offsets(COLS)


def psum_jobs():
    jobs = [(("xnT", 0, i), "act") for i in range(NT)]
    for i in range(NT):
        jobs += [(("qk", i), "dve"), (("v", i), "dve")]
    for l in range(LAYERS):
        for j in range(KC):
            jobs += [(("den", l, j), "dve"), (("num", l, j), "dve")]
        if l == 0:
            jobs += [(("kv",), "dve")]
            jobs += lagged(lambda i: [(("qfT", i), "act")], lambda i: [(("mo", i), "dve")],
                           lambda i: [(("moT", i), "act")], lambda i: [(("mw", i), "dve")])
        jobs += lagged(lambda i: [(("u", l, i), "dve")], lambda i: [(("gT", l, i), "act")],
                       lambda i: [(("y", l, i), "dve")])
        jobs += [(("yT", l, i), "act") for i in range(NT)]
        jobs += [(("cw", l, i), "dve") for i in range(NT)]
    jobs += [(("xnT", 1, i), "act") for i in range(NT)]
    jobs += [(("f0", i), "dve") for i in range(NT)]
    jobs += lagged(lambda i: [(("f0T", i), "act")], lambda i: [(("f0o", i), "dve")])
    jobs += [(("xnT", 2, i), "act") for i in range(NT)]
    jobs += [(("hre", i), "dve") for i in range(NT)]
    jobs += [(("hrT", i), "act") for i in range(NT)]
    for j in range(KC):
        jobs += [(("kT", j), "act"), (("qT", j), "act")]
    jobs += [(("v1", i), "dve") for i in range(NT)]
    jobs += [(("kn", j), "act") for j in range(KC)]
    jobs += [(("ctx",), "dve")]
    jobs += [(("oT", j), "act") for j in range(KC)]
    jobs += [(("y1", i), "dve") for i in range(NT)]
    for g in range(NT * H + LAG):
        if g < NT * H:
            jobs += [(("pair", g // H, g % H), "dve")]
        if g >= LAG:
            i, h = divmod(g - LAG, H)
            jobs += [(("exT", i, h), "act")]
            jobs += [(("att", i), "dve")] if h == H - 1 else []
    jobs += [(("xnT", 3, i), "act") for i in range(NT)]
    jobs += [(("f1", i), "dve") for i in range(NT)]
    jobs += lagged(lambda i: [(("f1T", i), "act")], lambda i: [(("f1o", i), "dve")])
    return jobs


def lagged(*steps):
    out = []
    for i in range(NT + len(steps) - 1):
        for n, step in enumerate(steps):
            if 0 <= i - n < NT:
                out += step(i - n) or []
    return out


class PsumRing:

    SLOTS = 4

    def __init__(self, psum, filled, emptied):
        self.psum, self.filled_sem, self.emptied_sem = psum, filled, emptied
        self.place, self.nth, count = {}, [], {"act": 0, "dve": 0}
        for k, (name, who) in enumerate(psum_jobs()):
            count[who] += 1
            self.place[name] = k
            self.nth.append((who, count[who]))

    def slot(self, name):
        return self.psum[self.place[name] % self.SLOTS]

    def claim(self, pe, name):
        k = self.place[name]
        if k >= self.SLOTS:
            who, n = self.nth[k - self.SLOTS]
            pe.wait_ge(self.emptied_sem[who], n)
        return self.slot(name)

    def filled(self, last_matmul):
        last_matmul.then_inc(self.filled_sem, 1)

    def wait_filled(self, eng, name):
        eng.wait_ge(self.filled_sem, self.place[name] + 1)
        return self.slot(name)

    def emptied(self, last_read, name):
        last_read.then_inc(self.emptied_sem[self.nth[self.place[name]][0]], 1)

    def wait_emptied(self, eng, name):
        who, n = self.nth[self.place[name]]
        eng.wait_ge(self.emptied_sem[who], n)


class Steps:

    def __init__(self, eng, sem):
        self.eng, self.sem, self.n = eng, sem, 0

    def did(self, ins):
        ins.then_inc(self.sem, 1)
        self.n += 1
        return self.n

    def wait(self, n=None):
        self.eng.wait_ge(self.sem, self.n if n is None else n)


def build_gps(nc, a, out):
    with ExitStack() as ctx:
        with nc.sbuf_tensor("arena", [128, ARENA], F32) as arena:
            pass
        rounded = {}
        for at, end, name in ((0, 13824, None), (13824, 18944, "ex_low"), (18944, 29184, None),
                              (29184, 34304, "high_0"), (34304, 39424, "high_1"),
                              (39424, ARENA, None)):
            rounded[name] = ctx.enter_context(
                nc.sbuf_tensor(name or f"beneath_{at}", [128, end - at], F32R))

        def sb(name, shape, dt=F32):
            return ctx.enter_context(nc.sbuf_tensor(name, shape, dt))

        signals = {}

        def sig(name):
            if name not in signals:
                signals[name] = ctx.enter_context(nc.semaphore(name))
            return signals[name]

        ps = ctx.enter_context(nc.psum_tensor("ps", [128, 4096], F32))
        ring = PsumRing([ps[:, 1024 * s:1024 * (s + 1)] for s in range(4)], sig("psum_filled"),
                        {"act": sig("scalar_emptied"), "dve": sig("vector_emptied")})

        table = nc.dram_tensor("table", (N, TABLE), F32, kind="Internal").ap()
        pairs = nc.dram_tensor("pairs", (N * N, H), F32, kind="Internal").ap()
        pairs_by_src = pairs.rearrange("(i p d) h -> i p (d h)", p=P, d=N)

        x = sb("x", [P, NT, D])
        counts = sb("counts", [P, NT, 2 * HALF], F32R)
        ident = sb("ident", [128, 128])
        cols = sb("cols", [128, COL_LEN])
        srci = sb("srci", [P, ET], I32)
        dsti = sb("dsti", [P, ET], I32)
        pairi = sb("pairi", [P, ET], I32)
        tcol = sb("tcol", [128, LAYERS])
        twos = sb("twos", [128, P])
        stat = sb("stat", [P, 6 * 16])
        small = sb("small", [128, 64 * 16])
        xn = sb("xn", [P, NT, D])
        xnT = sb("xnT", [128, KC, N])

        def view(at, *shape, parts=128):
            n = 1
            for s in shape:
                n *= s
            v = arena[0:parts, at:at + n]
            if len(shape) == 2:
                v = v.rearrange("p (a b) -> p a b", a=shape[0])
            if len(shape) == 3:
                v = v.rearrange("p (a b c) -> p a b c", a=shape[0], b=shape[1])
            return v

        def sm(k, *shape, parts=P):
            n = 1
            for s in shape:
                n *= s
            v = small[0:parts, 64 * k:64 * k + n]
            return v.rearrange("p (a b) -> p a b", a=shape[0]) if len(shape) == 2 else v

        def col(name, k, lo=0, hi=128):
            at = COL_AT[name][0] + k
            return cols[lo:hi, at:at + 1]

        def row(name, parts=P, lo=0, n=None):
            at, full = ROW_AT[name]
            n = n or full
            return a["rows"][at + lo:at + lo + n].partition_broadcast(parts)

        w1 = view(0, KC, HID)
        w2 = view(4096, HC, D)
        cw = view(8192, KC, D)
        b1r = view(10240, HID, parts=P)
        b2r = view(11264, D, parts=P)
        lngr = view(11776, D, parts=P)
        lnbr = view(12288, D, parts=P)
        biasr = view(33000, 2 * D, parts=P)
        ex = view(13824, NT, D, parts=P)
        exm = view(16384, NT, D, parts=P)
        u = view(18944, 2, HID, parts=P)
        xl = view(20992, NT, D, parts=P)
        xlT = view(23552, KC, N)
        ytmp = view(26052, D, parts=P)
        gT = view(26600, HC, N)
        rec = [view(39600, 2 * HALF), view(12800, 2 * HALF)]
        high_0, high_1, low = (
            rounded[name][0:P, :].rearrange("p (s i d) -> p s i d", s=2, i=NT)
            for name in ("high_0", "high_1", "ex_low"))
        high = [high_0, high_1, high_1]
        ex_low, exm_low = low[:, 0], low[:, 1]
        one_hot = view(20000, ONE_HOTS * N, parts=P).bitcast(F16) \
            .rearrange("p (k s n) -> p k s n", k=ONE_HOTS, s=2)
        iota16 = view(25000, 320, parts=P).bitcast(F16)[:, 0:N]
        fill = view(35540, N, parts=P)
        iotai = view(34304, N, parts=P)
        iota16z = view(35000, 256, parts=P).bitcast(F16)
        srcf = view(35300, ET, parts=P)
        dstf = view(35380, ET, parts=P)
        pairf = view(35460, ET, parts=P)
        dstm = view(36200, ET, parts=P)
        dstw = view(36280, ET, parts=P)
        above = view(36360, ET, parts=P)
        raw = view(36864, NT, HALF, parts=P)
        upper = view(38500, NT, HALF, parts=P)
        wqkv = view(0, KC, 3 * D)
        wo = view(6144, KC, D)
        qkvr = view(10240, 3 * D, parts=P)
        kv = view(11776, H * (HD + 1) + WIDE - HD - 1)
        qk = view(18944, NT, 2 * D, parts=P)
        kf = qk
        th = view(24064, NT, 2 * D, parts=P)
        qf = view(29184, NT, 2 * D, parts=P)
        q2 = view(34304, NT, D, parts=P)
        va = view(36864, NT * H * (HD + 1) + WIDE - HD - 1, parts=P)
        k3 = xn[:, :, :]
        qfT = view(24064, 2, H * P)
        mo = view(26100, 2, D, parts=P)
        moT = view(27200, 2, KC * P)
        f0w1 = view(0, KC, WP)
        f0w2 = view(2432, KC, D)
        f0b2 = view(4480, D)
        f0b1r = view(12800, D, parts=P)
        fh = view(13824, NT, D, parts=P)
        fg1 = view(16384, NT, D, parts=P)
        fg2 = view(18944, NT, D, parts=P)
        fT = view(21504, 2, KC * P)
        wer = view(5000, KC, 2 * D)
        ar = view(9096, 4, D, parts=P)
        hr = view(11144, NT * TABLE, parts=P).rearrange("p (i c) -> p i c", i=NT)
        hea = view(13784, NT * H * (HD + 1) + WIDE - HD - 1, parts=P)
        hrT = view(16416, KC, N)
        hrTs = view(35500, H, N)
        gs = view(18916, GATHERS, TABLE, parts=P)
        gd = view(21028, GATHERS, TABLE, parts=P)
        dif = view(23140, GATHERS, D, parts=P)
        tmp = view(23140, 3, D, parts=P)
        sc = view(25188, GATHERS, H, parts=P)
        ix = arena[0:P, 25220:25220 + 3 * GATHERS].bitcast(I32)
        wqkv1 = view(25240, KC, 3 * D)
        ek = view(31384, KC, N)
        kn = view(25240, NT, D, parts=P)
        qT = view(0, KC, N)
        v1 = xn[:, :, :]
        wo1 = view(5000, KC, D)
        ctxb = view(2500, KC, 128)
        oT = view(27840, KC, N)
        v1r = view(3100, D, parts=P)
        b1or = view(3700, D, parts=P)
        DT = N * H
        pt = [view(18916 + DT * s, DT, parts=P) for s in range(2)]
        S = view(28916, H, N, parts=P)
        exTh = view(5700, H, N, parts=P)
        otmp = view(11200, D, parts=P)
        f1w = view(0, KC, WP)
        f1w2 = view(2432, KC, D)
        f1w3 = view(4480, D, parts=HD + H + 1)
        f1r = view(4996, WX, parts=P)
        g1 = view(13824, NT, WX + 1, parts=P)
        g1T = view(16824, 2, 640)

        mv = sm(0, NT, 2)
        rstd = sm(1, NT)
        nrm2 = small[0:P, 256:336]
        rn = small[0:P, 336:416]
        tn = small[0:P, 416:496]
        pw = small[0:P, 496:536].rearrange("p (i h) -> p i h", i=NT)
        zt = small[0:P, 536:541]
        zmax = small[:, 543:544]
        zall = small[:, 541:542]
        zneg = small[:, 542:543]
        minus_half = small[0:P, 960:1024]
        lg8 = small[0:P, 544:584].rearrange("p (i h) -> p i h", i=NT)
        top8 = small[0:P, 584:624].rearrange("p (i h) -> p i h", i=NT)
        idx8 = small[0:P, 624:664].bitcast(U32).rearrange("p (i h) -> p i h", i=NT)
        idf8 = small[0:P, 664:704].rearrange("p (i h) -> p i h", i=NT)
        p12 = small[0:P, 704:724].rearrange("p (k i) -> p k i", k=4)
        io8 = small[0:P, 724:732]
        kmax = small[:, 732:736]
        ksum = small[:, 736:740]
        krec = small[:, 740:744]
        smax = small[0:P, 744:824].rearrange("p (k h) -> p k h", h=H)
        rden = small[0:P, 824:840]
        e8 = small[0:P, 840:872].rearrange("p (k h) -> p k h", h=H)

        def four_to_bank(k):
            return 512 * (k // 4) + P * (k % 4)

        block = ctx.enter_context(nc.Block())

        @block.sync
        def _(sp):
            def load(dst, src, name):
                sp.dma_start(dst, src).then_inc(sig(name), 16)

            def w(name):
                return a[name].rearrange("(k p) n -> p k n", p=128)

            load(srci[:, :], a["src"].rearrange("(p t) -> p t", t=ET), "edges_loaded")
            load(dsti[:, :], a["dst"].rearrange("(p t) -> p t", t=ET), "edges_loaded")
            load(x[:, :, :], a["x"].rearrange("(i p) d -> p i d", p=P), "x_loaded")
            load(cols[:, :], a["cols"], "cols_loaded")
            load(tcol[:, :], row("t", 128), "cols_loaded")
            load(wqkv, w("qkv_w"), "mix0_loaded")
            load(wo, w("out_w"), "mix0_loaded")
            load(qkvr, row("qkv_b"), "mix0_loaded")
            sp.wait_ge(sig("fill_ready"), 1)
            for i in range(NT):
                load(pairs_by_src[i].rearrange("p (h d) -> p h d", h=H),
                     fill.unsqueeze(1).to_broadcast([P, H, N]), "pairs_filled")
            load(cw, w("cw")[:, 0:KC, :], "cw_loaded")
            ring.wait_emptied(sp, ("v", NT - 1))
            load(w1, w("mw1_0"), "w1_loaded")
            load(b1r, row("mb1_0"), "b1_loaded")
            load(b2r, row("mb2_0"), "b2_loaded")
            ring.wait_emptied(sp, ("mw", NT - 1))
            load(w2, w("mw2_0"), "w2_loaded")
            load(biasr[:, 0:D], row("out_b"), "bias_loaded")
            load(biasr[:, D:2 * D], row("cb"), "bias_loaded")
            for l in range(1, LAYERS):
                ring.wait_emptied(sp, ("u", l - 1, NT - 1))
                load(w1, w(f"mw1_{l}"), "w1_loaded")
                load(b1r, row(f"mb1_{l}"), "b1_loaded")
                if l > 1:
                    sp.wait_ge(sig("xl_ready"), NT * (l - 1))
                load(lngr, row(f"lng_{l}"), "lng_loaded")
                load(lnbr, row(f"lnb_{l}"), "lng_loaded")
                ring.wait_emptied(sp, ("y", l - 1, NT - 1))
                load(w2, w(f"mw2_{l}"), "w2_loaded")
                load(b2r, row(f"mb2_{l}"), "b2_loaded")
                ring.wait_emptied(sp, ("cw", l - 1, NT - 1))
                load(cw, w("cw")[:, KC * l:KC * (l + 1), :], "cw_loaded")
            ring.wait_emptied(sp, ("u", LAYERS - 1, NT - 1))
            load(f0w1, w("f0_w1"), "f0_loaded")
            ring.wait_emptied(sp, ("num", LAYERS - 1, KC - 1))
            load(f0b1r, row("f0_b1"), "f0_loaded")
            ring.wait_emptied(sp, ("y", LAYERS - 1, NT - 1))
            load(f0w2, w("f0_w2"), "f0_loaded")
            load(f0b2, a["f0_b2"], "f0_loaded")
            ring.wait_emptied(sp, ("cw", LAYERS - 1, NT - 1))
            load(wer, w("w_er"), "gat_loaded")
            for n, name in enumerate(("a_abs", "a_src", "a_dst", "a_dif")):
                load(ar[:, n, :], row(name), "gat_loaded")
            ring.wait_emptied(sp, ("f0o", NT - 1))
            load(wqkv1, w("w_qkvT"), "mix1_loaded")
            load(v1r, row("v_b"), "mix1_loaded")
            load(b1or, row("b_out"), "mix1_loaded")
            for i in range(NT):
                sp.wait_ge(sig("table_ready"), i + 1)
                load(table[P * i:P * (i + 1), :], hr[:, i, :], "table_stored")
            load(wo1, w("w_outT"), "wo1_loaded")
            sp.wait_ge(sig("scattered"), 16 * ET)
            ring.wait_emptied(sp, ("y1", NT - 1))
            for i in range(NT):
                if i >= 2:
                    ring.wait_emptied(sp, ("pair", i - 2, H - 1))
                load(pt[i % 2], pairs_by_src[i], f"pairs_loaded_{i % 2}")
                if i == 0:
                    load(f1w, w("f1_w"), "f1_loaded")
                    load(f1w2, w("f1_w2"), "f1_loaded")
                    load(f1w3, a["f1_w3"], "f1_loaded")
                    load(f1r, row("f1_b"), "f1_loaded")
            for i in range(NT):
                ring.wait_emptied(sp, ("f1o", i))
                load(out[P * i:P * (i + 1), :], x[:, i, :], "out_stored")
            sp.wait_ge(sig("out_stored"), 16 * NT)

        @block.gpsimd
        def _(pool):
            st = Steps(pool, sig("pool_step"))
            st.did(pool.iota(iotai, pattern=[[1, N]], base=0, channel_multiplier=0,
                             allow_small_or_imprecise_dtypes=True))
            st.did(pool.memset(ident[:, :], 0.0))
            st.wait()
            pool.affine_select(out=ident[:, :], in_=ident[:, :], compare_op=ALU.not_equal, fill=1.0,
                               base=0, pattern=[[-1, 128]],
                               channel_multiplier=1).then_inc(sig("ident_ready"), 1)
            pool.memset(fill, NO_EDGE).then_inc(sig("fill_ready"), 1)
            pool.memset(twos[:, :], 2.0).then_inc(sig("ones_ready"), 1)
            pool.iota(io8, pattern=[[1, H]], base=0, channel_multiplier=0,
                      allow_small_or_imprecise_dtypes=True).then_inc(sig("ones_ready"), 1)
            st.did(pool.memset(minus_half, -0.5))
            st.wait()

            seen = [0]

            def rsqrt_ln(n=1):
                for _ in range(n):
                    i = seen[0] % NT
                    seen[0] += 1
                    pool.wait_ge(sig("variance_ready"), seen[0])
                    pool.tensor_tensor(rstd[:, i:i + 1], mv[:, i, 1:2], minus_half[:, 0:1],
                                       ALU.pow).then_inc(sig("rstd_ready"), 1)

            def largest_exponent(l):
                pool.wait_ge(sig("zmax_ready"), l + 1)
                pool.partition_all_reduce(zall, zmax, 128, RMAX).then_inc(sig("zall_ready"), 1)

            def leave_exm_low(l):
                for i in range(NT):
                    pool.wait_ge(sig("exm_high"), NT * l + i + 1)
                    pool.tensor_tensor(exm_low[:, i, :], exm[:, i, :],
                                       high[l][:, 1, i, :].bitcast(F32), ALU.subtract)\
                        .then_inc(sig("exm_low_ready"), 1)

            rsqrt_ln(NT)
            largest_exponent(0)
            leave_exm_low(0)
            pool.wait_ge(sig("square_sums"), NT)
            pool.tensor_tensor(rn, nrm2, minus_half[:, 0:1].to_broadcast([P, 80]),
                               ALU.pow).then_inc(sig("rnorm_ready"), 1)
            pool.wait_ge(sig("k_abs"), NT)
            st.did(pool.tensor_tensor(k3, k3, qk[:, :, D:2 * D], ALU.mult))
            st.wait()
            pool.tensor_tensor(k3, k3, qk[:, :, D:2 * D], ALU.mult).then_inc(sig("k_cubed"), 1)
            rsqrt_ln(NT)
            for l in range(LAYERS):
                lagged(lambda i: rsqrt_ln(), lambda i: None, lambda i: rsqrt_ln() if l else None)
                if l + 1 < LAYERS:
                    largest_exponent(l + 1)
                    leave_exm_low(l + 1)
            rsqrt_ln(2 * NT)
            pool.wait_ge(sig("table_stored"), 16 * NT)
            pool.wait_ge(sig("pairs_filled"), 16 * NT)

            def gather(k):
                pool.indirect_dma_start(
                    out=gs[:, k, :], out_offset=None, in_=table,
                    in_offset=bass.IndirectOffsetOnAxis(ap=ix[:, 3 * k:3 * k + 1], axis=0)
                ).then_inc(sig(f"gathered_{k}"), 16)
                pool.indirect_dma_start(
                    out=gd[:, k, :], out_offset=None, in_=table,
                    in_offset=bass.IndirectOffsetOnAxis(ap=ix[:, 3 * k + 1:3 * k + 2], axis=0)
                ).then_inc(sig(f"gathered_{k}"), 16)

            def scatter(k):
                pool.indirect_dma_start(
                    out=pairs, out_offset=bass.IndirectOffsetOnAxis(
                        ap=ix[:, 3 * k + 2:3 * k + 3], axis=0),
                    in_=sc[:, k, :], in_offset=None).then_inc(sig("scattered"), 16)

            for k in range(GATHERS):
                pool.wait_ge(sig("indices_ready"), k + 1)
                gather(k)

            def gather_and_scatter(it, k):
                pool.wait_ge(sig("indices_ready"), it * GATHERS + k + 1)
                pool.sem_inc(sig("gathers_begun"), 1)
                gather(k)
                pool.wait_ge(sig("scores_ready"), it * GATHERS + (k - GATHERS + 1))
                if not (isinstance(it, int) and it == 1 and k == 0):
                    pool.wait_ge(sig("scattered"), it * (16 * GATHERS) + 16 * (k - GATHERS))
                pool.sem_inc(sig("scatters_begun"), 1)
                scatter(k)

            for k in range(GATHERS):
                gather_and_scatter(1, k)
            with pool.Fori(2, ET // GATHERS) as it:
                for k in range(GATHERS):
                    gather_and_scatter(it, k)
            for k in range(GATHERS):
                pool.wait_ge(sig("scores_ready"), ET - GATHERS + k + 1)
                pool.wait_ge(sig("scattered"), 16 * (ET - GATHERS + k))
                scatter(k)
            for i in range(NT):
                for h in range(H):
                    pool.wait_ge(sig("pair_exp"), i * H + h + 1)
                    pool.tensor_tensor(S[:, h, :], S[:, h, :], counts[:, i, 0:N].bitcast(F32),
                                       ALU.mult).then_inc(sig("pair_weighted"), 1)
            rsqrt_ln(NT)

        @block.tensor
        def _(pe):
            mm = pe.matmul

            def turn(name, src_of, widths, at_of=None):
                slot = ring.claim(pe, name)
                for k, n in enumerate(widths):
                    at = at_of(k)
                    src = src_of(k)
                    rows = src.shape[0]
                    last = pe.transpose(slot[0:n, at:at + rows], src, ident[0:rows, 0:rows])
                ring.filled(last)

            def product(slot, m, lhsT_of, rhs_of, ks, n, extra=None):
                for lo in range(0, n, 512):
                    hi = min(lo + 512, n)
                    for k in range(ks):
                        last = mm(slot[0:m, lo:hi], lhsT_of(k), rhs_of(k)[:, lo:hi],
                                  start=(k == 0), stop=(k == ks - 1))
                return last

            def nodes(t, i):
                return lambda k: t[:, k, P * i:P * (i + 1)]

            pe.wait_ge(sig("zeros_ready"), 1)
            for n, (lo, hi) in enumerate(CHUNKS):
                if n:
                    pe.wait_ge(sig("raw_copied"), n)
                for i in range(NT):
                    mm(ps[0:P, 512 * i:512 * i + HALF], iota16z[:, 0:P], iota16z[:, 0:HALF],
                       start=True, stop=False, skip_group_check=True)
                with pe.Fori(lo, hi) as it:
                    for k in range(ONE_HOTS):
                        pe.wait_ge(sig("one_hots_ready"), it * (2 * ONE_HOTS) + 2 * (k + 1))
                        for i in range(NT):
                            last = mm(ps[0:P, 512 * i:512 * i + HALF],
                                      one_hot[:, k, 0, P * i:P * (i + 1)],
                                      one_hot[:, k, 1, 0:HALF], start=False, stop=False,
                                      skip_group_check=True)
                        last.then_inc(sig("one_hots_used"), 1)
            pe.wait_ge(sig("raw_copied"), len(CHUNKS))

            def turn_xn(n):
                for i in range(NT):
                    pe.wait_ge(sig("xn_ready"), NT * n + i + 1)
                    turn(("xnT", n, i), lambda k: xn[:, i, 128 * k:128 * (k + 1)], [128] * KC,
                         four_to_bank)

            pe.wait_ge(sig("ident_ready"), 1)
            turn_xn(0)

            pe.wait_ge(sig("mix0_loaded"), 48)
            for i in range(NT):
                ring.wait_emptied(pe, ("xnT", 0, i))
                slot = ring.claim(pe, ("qk", i))
                ring.filled(product(slot, P, nodes(xnT, i), lambda k: wqkv[:, k, :], KC, 2 * D))
                slot = ring.claim(pe, ("v", i))
                ring.filled(product(slot, P, nodes(xnT, i), lambda k: wqkv[:, k, 2 * D:], KC, D))
            def head_at(h):
                return 512 * (h // 4) + WIDE * (h % 4)

            def mix0():
                pe.wait_ge(sig("kf_ready"), NT)
                pe.wait_ge(sig("va_ones"), 2)
                slot = ring.claim(pe, ("kv",))
                for h in range(H):
                    at = head_at(h)
                    for i in range(NT):
                        v0 = (HD + 1) * (H * i + h)
                        last = mm(slot[:, at:at + WIDE], kf[:, i, 128 * h:128 * (h + 1)],
                                  va[:, v0:v0 + WIDE], start=(i == 0), stop=(i == NT - 1),
                                  skip_group_check=True)
                ring.filled(last)

                def turn_q(i):
                    pe.wait_ge(sig("qf_ready"), i + 1)
                    turn(("qfT", i), lambda k: qf[:, i, 128 * k:128 * (k + 1)], [128] * H,
                         four_to_bank)

                def attend(i):
                    slot = ring.claim(pe, ("mo", i))
                    ring.wait_emptied(pe, ("kv",))
                    ring.wait_emptied(pe, ("qfT", i))
                    for h in range(H):
                        at = head_at(h)
                        last = mm(slot[0:P, at:at + WIDE], qfT[:, i % 2, P * h:P * (h + 1)],
                                  kv[:, (HD + 1) * h:(HD + 1) * h + WIDE], start=True, stop=True,
                                  skip_group_check=True)
                    ring.filled(last)

                def turn_out(i):
                    pe.wait_ge(sig("mo_ready"), i + 1)
                    turn(("moT", i), lambda k: mo[:, i % 2, 128 * k:128 * (k + 1)], [128] * KC,
                         four_to_bank)

                def project(i):
                    slot = ring.claim(pe, ("mw", i))
                    ring.wait_emptied(pe, ("moT", i))
                    ring.filled(product(slot, P, lambda k: moT[:, i % 2, P * k:P * (k + 1)],
                                        lambda k: wo[:, k, :], KC, D))

                lagged(turn_q, attend, turn_out, project)

            for l in range(LAYERS):
                if l == 0:
                    pe.wait_ge(sig("counts_ready"), 1)
                pe.wait_ge(sig("ex_low_ready"), NT * (l + 1))
                pe.wait_ge(sig("exm_low_ready"), NT * (l + 1))
                for j in range(KC):
                    for n, (name, low) in enumerate((("den", ex_low), ("num", exm_low))):
                        slot = ring.claim(pe, (name, l, j))
                        for b in range(2):
                            for part in (high[l][:, n], low):
                                for i in range(NT):
                                    last = mm(slot[:, 512 * b:512 * b + HALF],
                                              part[:, i, 128 * j:128 * (j + 1)],
                                              counts[:, i, HALF * b:HALF * (b + 1)],
                                              start=(part is not low and i == 0),
                                              stop=(part is low and i == NT - 1))
                        ring.filled(last)
                if l == 0:
                    mix0()
                pe.wait_ge(sig("w1_loaded"), 16 * (l + 1))
                pe.wait_ge(sig("hT_ready"), KC * (l + 1))
                hT = xlT if l else xnT

                def widen(i):
                    slot = ring.claim(pe, ("u", l, i))
                    ring.filled(product(slot, P, nodes(hT, i), lambda k: w1[:, k, :], KC, HID))

                def turn_hidden(i):
                    pe.wait_ge(sig("u_normed"), NT * l + i + 1)
                    turn(("gT", l, i), lambda k: u[:, i % 2, 128 * k:128 * (k + 1)], [128] * HC,
                         four_to_bank)

                def narrow(i):
                    slot = ring.claim(pe, ("y", l, i))
                    if i == 0:
                        pe.wait_ge(sig("w2_loaded"), 16 * (l + 1))
                    ring.wait_emptied(pe, ("gT", l, i))
                    ring.filled(product(slot, P, nodes(gT, i), lambda k: w2[:, k, :], HC, D))

                lagged(widen, turn_hidden, narrow)
                for i in range(NT):
                    if l:
                        pe.wait_ge(sig("xl_ready"), NT * (l - 1) + i + 1)
                    else:
                        ring.wait_emptied(pe, ("y", l, i))
                    turn(("yT", l, i), lambda k: xl[:, i, 128 * k:128 * (k + 1)], [128] * KC,
                         four_to_bank)
                pe.wait_ge(sig("cw_loaded"), 16 * (l + 1))
                for i in range(NT):
                    slot = ring.claim(pe, ("cw", l, i))
                    ring.wait_emptied(pe, ("yT", l, i))
                    ring.filled(product(slot, P, nodes(xlT, i), lambda k: cw[:, k, :], KC, D))

            turn_xn(1)
            pe.wait_ge(sig("f0_loaded"), 64)
            for i in range(NT):
                slot = ring.claim(pe, ("f0", i))
                ring.wait_emptied(pe, ("xnT", 1, i))
                ring.filled(product(slot, P, nodes(xnT, i), lambda k: f0w1[:, k, :], KC, WP))

            def turn_f0(i):
                pe.wait_ge(sig("fg_ready"), i + 1)
                turn(("f0T", i), lambda k: fg1[:, i, 128 * k:128 * (k + 1)], [128] * KC,
                     four_to_bank)

            def out_f0(i):
                slot = ring.claim(pe, ("f0o", i))
                ring.wait_emptied(pe, ("f0T", i))
                for k in range(KC):
                    mm(slot[0:P, 0:D], fT[:, i % 2, P * k:P * (k + 1)], f0w2[:, k, :],
                       start=(k == 0), stop=False)
                ring.filled(mm(slot[0:P, 0:D], twos[:, :], f0b2, start=False, stop=True))

            lagged(turn_f0, out_f0)

            turn_xn(2)
            pe.wait_ge(sig("gat_loaded"), 80)
            for i in range(NT):
                slot = ring.claim(pe, ("hre", i))
                ring.wait_emptied(pe, ("xnT", 2, i))
                ring.filled(product(slot, P, nodes(xnT, i), lambda k: wer[:, k, :], KC, 2 * D))
            for i in range(NT):
                ring.wait_emptied(pe, ("hre", i))
                turn(("hrT", i), lambda k: hr[:, i, 128 * k:128 * (k + 1)], [128] * KC,
                     four_to_bank)

            pe.wait_ge(sig("mix1_loaded"), 48)
            for j in range(KC):
                for name, lo in (("kT", D), ("qT", 0)):
                    slot = ring.claim(pe, (name, j))
                    ring.filled(product(
                        slot, 128, lambda k: wqkv1[:, k, lo + 128 * j:lo + 128 * (j + 1)],
                        lambda k: xnT[:, k, :], KC, N))
            for i in range(NT):
                slot = ring.claim(pe, ("v1", i))
                ring.filled(product(slot, P, nodes(xnT, i), lambda k: wqkv1[:, k, 2 * D:], KC, D))
            for j in range(KC):
                pe.wait_ge(sig("ek_ready"), j + 1)
                turn(("kn", j), lambda k: ek[:, j, P * k:P * (k + 1)], [P] * NT, lambda k: 128 * k)
            slot = ring.claim(pe, ("ctx",))
            ring.wait_emptied(pe, ("kn", KC - 1))
            ring.wait_emptied(pe, ("v1", NT - 1))
            for j in range(KC):
                for i in range(NT):
                    last = mm(slot[:, 128 * j:128 * (j + 1)], kn[:, i, 128 * j:128 * (j + 1)],
                              v1[:, i, 128 * j:128 * (j + 1)], start=(i == 0),
                              stop=(i == NT - 1), skip_group_check=True)
            ring.filled(last)
            ring.wait_emptied(pe, ("ctx",))
            for j in range(KC):
                slot = ring.claim(pe, ("oT", j))
                ring.filled(product(slot, 128, lambda k: ctxb[:, j, :],
                                    lambda k: qT[:, j, :], 1, N))
            ring.wait_emptied(pe, ("oT", KC - 1))
            pe.wait_ge(sig("wo1_loaded"), 16)
            for i in range(NT):
                slot = ring.claim(pe, ("y1", i))
                ring.filled(product(slot, P, nodes(oT, i), lambda k: wo1[:, k, :], KC, D))

            pe.wait_ge(sig("hrTs_ready"), 1)
            for g in range(NT * H + LAG):
                i, h = divmod(g, H)
                if i < NT:
                    slot = ring.claim(pe, ("pair", i, h))
                    ring.filled(product(slot, P, lambda k: hrTs[:, h, P * i:P * (i + 1)],
                                        lambda k: hrT[:, h // 2, :], 1, N))
                if g < LAG:
                    continue
                i, h = divmod(g - LAG, H)
                pe.wait_ge(sig("pair_weighted"), i * H + h + 1)
                turn(("exT", i, h), lambda k: S[:, h, P * k:P * (k + 1)], [P] * NT,
                     lambda k: 128 * k)
                if h == H - 1:
                    slot = ring.claim(pe, ("att", i))
                    for h in range(H):
                        ring.wait_emptied(pe, ("exT", i, h))
                        at = head_at(h)
                        for k in range(NT):
                            v0 = (HD + 1) * (H * k + h)
                            last = mm(slot[0:P, at:at + WIDE], exTh[:, h, P * k:P * (k + 1)],
                                      hea[:, v0:v0 + WIDE], start=(k == 0), stop=(k == NT - 1),
                                      skip_group_check=True)
                    ring.filled(last)

            turn_xn(3)
            pe.wait_ge(sig("f1_loaded"), 64)
            for i in range(NT):
                slot = ring.claim(pe, ("f1", i))
                ring.wait_emptied(pe, ("xnT", 3, i))
                ring.filled(product(slot, P, nodes(xnT, i), lambda k: f1w[:, k, :], KC, WP))
            KX = HD + H + 1

            def turn_f1(i):
                pe.wait_ge(sig("g1_ready"), i + 1)
                turn(("f1T", i), lambda k: g1[:, i, 128 * k:min(128 * (k + 1), WX + 1)],
                     [128] * KC + [KX], four_to_bank)

            def out_f1(i):
                slot = ring.claim(pe, ("f1o", i))
                ring.wait_emptied(pe, ("f1T", i))
                for k in range(KC):
                    mm(slot[0:P, 0:D], g1T[:, i % 2, P * k:P * (k + 1)], f1w2[:, k, :],
                       start=(k == 0), stop=False)
                ring.filled(mm(slot[0:P, 0:D], g1T[0:KX, i % 2, 512:512 + P], f1w3,
                               start=False, stop=True))

            lagged(turn_f1, out_f1)

        @block.scalar
        def _(act):
            st = Steps(act, sig("scalar_step"))
            def copy(dst, src):
                return act.activation(dst, src, ACT.Copy)

            def empty_turned(name, dst, n, k=KC):
                slot = ring.wait_filled(act, name)
                ring.emptied(copy(dst, slot[0:128, 0:k * P].rearrange("p (k n) -> p k n", k=k)),
                             name)

            def xn_turned(n):
                for i in range(NT):
                    empty_turned(("xnT", n, i), xnT[:, :, P * i:P * (i + 1)], P)

            def exponentials(l):
                act.wait_ge(sig("zneg_ready"), l + 1)
                for i in range(NT):
                    act.activation(high[l][:, 0, i, :], ex[:, i, :], ACT.Exp,
                                   bias=zneg[0:P, :]).then_inc(sig("ex_high"), 1)
                    act.wait_ge(sig("ex_high"), NT * l + i + 1)
                    act.activation(ex[:, i, :], ex[:, i, :], ACT.Exp, bias=zneg[0:P, :])\
                       .then_inc(sig("ex_ready"), 1)
                for i in range(NT):
                    act.wait_ge(sig("exm_ready"), NT * l + i + 1)
                    act.activation(high[l][:, 1, i, :], exm[:, i, :], ACT.Copy)\
                       .then_inc(sig("exm_high"), 1)

            def copy_counts(n):
                act.wait_ge(sig("one_hots_used"), CHUNKS[n][1] * ONE_HOTS)
                if n:
                    act.wait_ge(sig("unpacked"), n)
                act.activation(raw, ps[0:P, 0:512 * NT].rearrange("p (i n) -> p i n", i=NT)
                               [:, :, 0:HALF], ACT.Copy).then_inc(sig("raw_copied"), 1)

            copy_counts(0)
            exponentials(0)
            copy_counts(1)
            copy_counts(2)
            xn_turned(0)

            for i in range(NT):
                ring.wait_emptied(act, ("qk", i))
                act.activation(th[:, i, :], qk[:, i, :], ACT.Square).then_inc(sig("squares"), 1)
                act.activation(k3[:, i, :], qk[:, i, D:], ACT.Abs).then_inc(sig("k_abs"), 1)
            act.wait_ge(sig("pairs_filled"), 16 * NT)
            act.wait_ge(sig("norms_ready"), 1)
            act.activation(pw, tn.rearrange("p (i s h) -> p i s h", i=NT, s=2)
                           [:, :, 0, :], ACT.Tanh).then_inc(sig("tanh_norm"), 1)
            for i in range(NT):
                act.wait_ge(sig("scaled"), i + 1)
                st.did(act.activation(q2[:, i, :], th[:, i, 0:D], ACT.Square))
            for i in range(NT):
                st.wait(st.n - NT + 1)
                st.did(act.activation(th[:, i, :], th[:, i, :], ACT.Tanh, scale=20.0))
            st.wait()
            act.wait_ge(sig("k_cubed"), 1)
            for f, s, n in ((kf, 1, "k_angles"), (qf, 0, "q_angles")):
                if f is qf:
                    ring.wait_filled(act, ("num", 0, KC - 1))
                for i in range(NT):
                    o = f[:, i, :].rearrange("p (h c e) -> p h c e", h=H, c=2)
                    t = th[:, i, D * s:D * (s + 1)].rearrange("p (h e) -> p h e", h=H)
                    act.activation(o[:, :, 0, :], t, ACT.Sin, scale=PI / 4, bias=PI / 2)\
                       .then_inc(sig(n), 1)
                    act.activation(o[:, :, 1, :], t, ACT.Sin, scale=PI / 4).then_inc(sig(n), 1)
            for i in range(NT):
                act.activation(q2[:, i, :], q2[:, i, :], ACT.Ln, bias=1e-19)\
                   .then_inc(sig("q_logs"), 1)
            for i in range(NT):
                act.wait_ge(sig("q_powers"), i + 1)
                act.activation(q2[:, i, :], q2[:, i, :], ACT.Exp).then_inc(sig("q_feats"), 1)

            def q_turned(i):
                slot = ring.wait_filled(act, ("qfT", i))
                if i == 0:
                    act.wait_ge(sig("q_angles"), 2 * NT)
                if i >= 2:
                    ring.wait_filled(act, ("mo", i - 2))
                o = qfT[:, i % 2, :].rearrange("p (b n) -> p b n", b=2)
                v = slot.rearrange("p (b n) -> p b n", b=2)[:, :, 0:4 * P]
                ring.emptied(copy(o, v), ("qfT", i))

            def mo_turned(i):
                slot = ring.wait_filled(act, ("moT", i))
                if i >= 2:
                    ring.wait_filled(act, ("mw", i - 2))
                for k in range(KC):
                    last = act.activation(moT[:, i % 2, P * k:P * (k + 1)],
                                          slot[:, P * k:P * (k + 1)], ACT.Identity,
                                          scale=col("ln_g", k), bias=col("ln_b", k))
                ring.emptied(last, ("moT", i))

            act.wait_ge(sig("cols_loaded"), 32)
            lagged(q_turned, lambda i: None, mo_turned)

            for l in range(LAYERS):
                for i in range(NT):
                    slot = ring.wait_filled(act, ("gT", l, i))
                    for k in range(HC):
                        at = four_to_bank(k)
                        last = act.activation(gT[:, k, P * i:P * (i + 1)], slot[:, at:at + P],
                                              ACT.Relu, scale=col(f"mlg_{l}", k),
                                              bias=col(f"mlb_{l}", k))
                    ring.emptied(last, ("gT", l, i))
                for i in range(NT):
                    empty_turned(("yT", l, i), xlT[:, :, P * i:P * (i + 1)], P)
                if l + 1 < LAYERS:
                    exponentials(l + 1)

            xn_turned(1)
            act.wait_ge(sig("f0_gap"), 1)
            act.activation(p12[:, 0, :], p12[:, 1, :], ACT.Exp).then_inc(sig("f0_exp"), 1)
            for i in range(NT):
                act.wait_ge(sig("f0_in"), i + 1)
                act.activation(fg1[:, i, :], fg1[:, i, :], ACT.Gelu).then_inc(sig("f0_gelu"), 1)
                act.activation(fg2[:, i, :], fg2[:, i, :], ACT.Gelu).then_inc(sig("f0_gelu"), 1)
            for i in range(NT):
                if i >= 2:
                    ring.wait_filled(act, ("f0o", i - 2))
                slot = ring.wait_filled(act, ("f0T", i))
                ring.emptied(copy(fT[:, i % 2, :], slot[:, 0:KC * P]), ("f0T", i))

            xn_turned(2)
            for i in range(NT):
                empty_turned(("hrT", i), hrT[:, :, P * i:P * (i + 1)], P)

            def edge_turns(lo, hi):
                with act.Fori(lo, hi) as it:
                    for k in range(GATHERS):
                        act.wait_ge(sig("differences"), it * GATHERS + k + 1)
                        act.activation(dif[:, k, :], dif[:, k, :], ACT.Abs)\
                           .then_inc(sig("abs_ready"), 1)

            def kq_turned(*js):
                for j in js:
                    slot = ring.wait_filled(act, ("kT", j))
                    ring.emptied(act.activation(ek[:, j, :], slot[:, 0:N], ACT.Identity,
                                                bias=col("k_b", j)), ("kT", j))
                    slot = ring.wait_filled(act, ("qT", j))
                    ring.emptied(act.activation(qT[:, j, :], slot[:, 0:N], ACT.Identity,
                                                bias=col("q_b", j)), ("qT", j))

            def k_exponentials():
                for j in range(KC):
                    act.wait_ge(sig("kmax_ready"), j + 1)
                    act.activation(ek[:, j, :], ek[:, j, :], ACT.Exp, bias=kmax[:, j:j + 1],
                                   accum_out=ksum[:, j:j + 1]).then_inc(sig("ek_ready"), 1)

            def k_natural():
                ring.wait_emptied(act, ("v1", NT - 1))
                for j in range(KC):
                    slot = ring.wait_filled(act, ("kn", j))
                    ring.emptied(copy(kn[:, :, 128 * j:128 * (j + 1)],
                                      slot[0:P, 0:NT * 128].rearrange("p (i c) -> p i c", i=NT)),
                                 ("kn", j))

            def out_turned():
                for j in range(KC):
                    slot = ring.wait_filled(act, ("oT", j))
                    ring.emptied(copy(oT[:, j, :], slot[:, 0:N]), ("oT", j))

            edge_turns(0, 2)
            kq_turned(0, 1)
            edge_turns(2, 4)
            kq_turned(2, 3)
            edge_turns(4, 6)
            k_exponentials()
            edge_turns(6, 8)
            k_natural()
            edge_turns(8, 12)
            out_turned()
            edge_turns(12, ET // GATHERS)
            for g in range(NT * H + LAG):
                i, h = divmod(g, H)
                if i < NT:
                    act.wait_ge(sig("leaky_ready"), g + 1)
                    act.activation(S[:, h, :], S[:, h, :], ACT.Exp,
                                   bias=smax[:, 1, h:h + 1]).then_inc(sig("pair_exp"), 1)
                if g >= LAG:
                    i, h = divmod(g - LAG, H)
                    slot = ring.wait_filled(act, ("exT", i, h))
                    if i:
                        ring.wait_filled(act, ("att", i - 1))
                    ring.emptied(copy(exTh[:, h, :].rearrange("p (k n) -> p k n", k=NT),
                                      slot[0:P, 0:NT * 128].rearrange("p (k n) -> p k n", k=NT)
                                      [:, :, 0:P]), ("exT", i, h))

            xn_turned(3)
            act.wait_ge(sig("f1_gap"), 1)
            act.activation(p12[:, 0, :], p12[:, 1, :], ACT.Exp).then_inc(sig("f1_exp"), 1)
            for i in range(NT):
                if i >= 2:
                    ring.wait_filled(act, ("f1o", i - 2))
                slot = ring.wait_filled(act, ("f1T", i))
                copy(g1T[:, i % 2, 0:KC * P], slot[:, 0:KC * P])
                ring.emptied(copy(g1T[0:HD + H + 1, i % 2, 512:512 + P],
                                  slot[0:HD + H + 1, 512:512 + P]), ("f1T", i))

        @block.vector
        def _(v):
            st = Steps(v, sig("vector_step"))
            TT, TS, STT = v.tensor_tensor, v.tensor_scalar, v.scalar_tensor_tensor
            lns, lns_done = [0], [0]

            def ln_stats(parts):
                i = lns[0] % NT
                lns[0] += 1
                for n, part in enumerate(parts):
                    st.did(v.bn_stats(stat[:, 12 * i + 6 * n:12 * i + 6 * (n + 1)], part))
                st.wait()
                st.did(v.bn_aggr(mv[:, i, :], stat[:, 12 * i:12 * i + 6 * len(parts)]))
                st.wait()
                TS(mv[:, i, 1:2], mv[:, i, 1:2], LN_EPS, None, ALU.add)\
                    .then_inc(sig("variance_ready"), 1)

            def ln_apply(dst, src):
                i = lns_done[0] % NT
                lns_done[0] += 1
                v.wait_ge(sig("rstd_ready"), lns_done[0])
                return TS(dst, src, mv[:, i, 0:1], rstd[:, i:i + 1], ALU.subtract, ALU.mult)

            def ln_x():
                for i in range(NT):
                    ln_stats([x[:, i, :]])
                for i in range(NT):
                    ln_apply(xn[:, i, :], x[:, i, :]).then_inc(sig("xn_ready"), 1)

            st.did(v.memset(iota16z[:, :], 0.0))
            st.wait()
            v.memset(zmax, -3e38).then_inc(sig("zeros_ready"), 1)
            v.wait_ge(sig("edges_loaded"), 32)
            st.did(v.tensor_copy(srcf, srci[:, :]))
            st.did(v.tensor_copy(dstf, dsti[:, :]))
            v.wait_ge(sig("pool_step"), 1)
            st.did(v.tensor_copy(iota16, iotai))
            st.wait()
            st.did(STT(out=pairf, in0=srcf, scalar=float(N), in1=dstf, op0=ALU.mult, op1=ALU.add))
            st.wait()
            st.did(v.tensor_copy(pairi[:, :], pairf))
            st.did(TS(above, dstf, float(HALF), None, ALU.is_ge))
            st.wait()
            st.did(STT(out=dstm, in0=above, scalar=-float(HALF), in1=dstf, op0=ALU.mult,
                       op1=ALU.add))
            st.did(TS(dstw, above, PACK - 1, 1.0, ALU.mult, ALU.add))
            st.wait()

            def one_hots(k, t):
                TS(one_hot[:, k, 0, :], iota16, srcf[:, t], None, ALU.is_equal)\
                    .then_inc(sig("one_hots_ready"), 1)
                TS(one_hot[:, k, 1, 0:HALF], iota16[:, 0:HALF], dstm[:, t], dstw[:, t],
                   ALU.is_equal, ALU.mult)\
                    .then_inc(sig("one_hots_ready"), 1)

            for k in range(ONE_HOTS):
                one_hots(k, slice(k, k + 1))
            v.wait_ge(sig("x_loaded"), 16)
            ln_x()

            def one_hot_turns(lo, hi):
                with v.Fori(lo, hi) as it:
                    for k in range(ONE_HOTS):
                        v.wait_ge(sig("one_hots_used"), it * ONE_HOTS + (k + 1 - ONE_HOTS))
                        one_hots(k, bass.ds(it * ONE_HOTS + k, 1))

            def messages(l, i):
                st.did(TS(exm[:, i, :], (xl if l else xn)[:, i, :], 0.0, 1e-7, ALU.max, ALU.add))
                st.wait()
                st.did(TS(ex[:, i, :], exm[:, i, :], tcol[0:P, l:l + 1], None, ALU.mult))
                st.wait()
                st.did(v.reduce_max(zt[:, i:i + 1], ex[:, i, :], AX_X))

            def largest_exponent(l):
                st.wait()
                v.reduce_max(zmax[0:P, :], zt, AX_X).then_inc(sig("zmax_ready"), 1)
                v.wait_ge(sig("zall_ready"), l + 1)
                TS(zneg, zall, -1.0, HEADROOM, ALU.mult, ALU.add).then_inc(sig("zneg_ready"), 1)

            def weigh(l, i):
                v.wait_ge(sig("ex_ready"), NT * l + i + 1)
                TT(exm[:, i, :], exm[:, i, :], ex[:, i, :], ALU.mult).then_inc(sig("exm_ready"), 1)
                v.wait_ge(sig("exm_ready"), NT * l + i + 1)
                TT(ex_low[:, i, :], ex[:, i, :], high[l][:, 0, i, :].bitcast(F32),
                   ALU.subtract).then_inc(sig("ex_low_ready"), 1)

            lower, higher = counts[:, :, 0:HALF], counts[:, :, HALF:]

            def unpack(n):
                v.wait_ge(sig("raw_copied"), n + 1)
                st.did(TS(upper, raw, 1 / PACK, (1 - PACK / 2) / PACK, ALU.mult, ALU.add))
                st.wait()
                st.did(TS(upper, upper, 1.5 * 2 ** 23, -1.5 * 2 ** 23, ALU.add, ALU.add))
                st.wait()
                st.did(STT(out=raw, in0=upper, scalar=-PACK, in1=raw, op0=ALU.mult, op1=ALU.add))
                if n == 0:
                    st.did(v.tensor_copy(higher, upper))
                    st.wait()
                    v.tensor_copy(lower, raw).then_inc(sig("unpacked"), 1)
                    return
                v.wait_ge(sig("unpacked"), n)
                st.did(TT(higher, higher.bitcast(F32), upper, ALU.add))
                st.wait()
                last = TT(lower, lower.bitcast(F32), raw, ALU.add)
                last.then_inc(sig("unpacked" if n + 1 < len(CHUNKS) else "counts_ready"), 1)

            one_hot_turns(1, 3)
            v.wait_ge(sig("cols_loaded"), 32)
            for i in range(NT):
                messages(0, i)
            largest_exponent(0)
            one_hot_turns(3, 4)
            unpack(0)
            one_hot_turns(4, 5)
            for i in range(NT):
                weigh(0, i)
            one_hot_turns(5, 7)
            unpack(1)
            one_hot_turns(7, 10)
            unpack(2)

            def heads(slot, parts=P):
                return slot[0:parts, :].rearrange("p (b n) -> p b n", b=2)[:, :, 0:HW]\
                    .rearrange("p b (h e) -> p b h e", h=4)[:, :, :, 0:HD + 1]

            v.wait_ge(sig("mix0_loaded"), 48)
            v.wait_ge(sig("counts_ready"), 1)
            va4 = va[:, 0:NT * H * (HD + 1)].rearrange("p (i h e) -> p i h e", i=NT, h=H)
            v.memset(va[:, 0:NT * H * (HD + 1)].rearrange("p (g e) -> p g e", e=HD + 1)
                     [:, :, HD:HD + 1], 1.0).then_inc(sig("va_ones"), 1)
            v.memset(va[:, NT * H * (HD + 1):], 0.0).then_inc(sig("va_ones"), 1)
            st.did(v.memset(kv[:, H * (HD + 1):], 0.0))

            def squares(i):
                v.wait_ge(sig("squares"), i + 1)
                v.tensor_reduce(nrm2[:, 16 * i:16 * (i + 1)],
                                th[:, i, :].rearrange("p (g e) -> p g e", e=HD),
                                AX_X, ALU.add).then_inc(sig("square_sums"), 1)

            for i in range(NT):
                slot = ring.wait_filled(v, ("qk", i))
                ring.emptied(TT(qk[:, i, :], slot[0:P, :], qkvr[:, 0:2 * D], ALU.add), ("qk", i))
                slot = ring.wait_filled(v, ("v", i))
                ring.emptied(TT(va4[:, i, :, 0:HD],
                                slot[0:P, 0:D].rearrange("p (h e) -> p h e", h=H),
                                qkvr[:, 2 * D:].rearrange("p (h e) -> p h e", h=H), ALU.add),
                             ("v", i))
                if i >= 1:
                    squares(i - 1)
            squares(NT - 1)
            v.wait_ge(sig("square_sums"), NT)
            v.wait_ge(sig("rnorm_ready"), 1)
            TT(tn, nrm2, rn, ALU.mult).then_inc(sig("norms_ready"), 1)
            for i in range(NT):
                TT(th[:, i, :].rearrange("p (g e) -> p g e", e=HD),
                   qk[:, i, :].rearrange("p (g e) -> p g e", e=HD),
                   rn[:, 16 * i:16 * (i + 1)].unsqueeze(2).to_broadcast([P, 16, HD]),
                   ALU.mult).then_inc(sig("scaled"), 1)
            def aggregate(l, j):
                xT, r = (xlT if l else xnT), rec[j % 2]
                r2 = r.rearrange("p (b n) -> p b n", b=2)

                def halves(slot):
                    return slot.rearrange("p (b n) -> p b n", b=2)[:, :, 0:HALF]

                slot = ring.wait_filled(v, ("den", l, j))
                if KC * l + j >= 2:
                    ring.wait_emptied(v, ("num", *divmod(KC * l + j - 2, KC)))
                st.did(TS(r2, halves(slot), 1e-37, None, ALU.max))
                st.wait()
                ring.emptied(v.reciprocal(r, r), ("den", l, j))
                ring.wait_emptied(v, ("den", l, j))
                slot = ring.wait_filled(v, ("num", l, j))
                ring.emptied(TT(r2, r2, halves(slot), ALU.mult), ("num", l, j))
                ring.wait_emptied(v, ("num", l, j))
                TT(xT[:, j, :], xT[:, j, :], r[:, 0:N], ALU.add).then_inc(sig("hT_ready"), 1)

            aggregate(0, 0)
            v.wait_ge(sig("tanh_norm"), 1)
            st.did(TS(pw, pw, 1.5, 0.75, ALU.mult, ALU.add))

            def feature(f, m, i):
                o = f[:, i, :].rearrange("p (h c e) -> p h c e", h=H, c=2)
                b = m[:, i, :].rearrange("p (h e) -> p h e", h=H).unsqueeze(2)\
                    .to_broadcast([P, H, 2, HD])
                return TT(o, o, b, ALU.mult)

            v.wait_ge(sig("k_cubed"), 1)
            for i in range(NT):
                v.wait_ge(sig("k_angles"), 2 * (i + 1))
                feature(kf, k3, i).then_inc(sig("kf_ready"), 1)
            aggregate(0, 1)
            st.wait()
            for i in range(NT):
                v.wait_ge(sig("q_logs"), i + 1)
                TT(q2[:, i, :].rearrange("p (h e) -> p h e", h=H),
                   q2[:, i, :].rearrange("p (h e) -> p h e", h=H),
                   pw[:, i, :].unsqueeze(2).to_broadcast([P, H, HD]),
                   ALU.mult).then_inc(sig("q_powers"), 1)
            aggregate(0, 2)
            for i in range(NT):
                v.wait_ge(sig("q_feats"), i + 1)
                v.wait_ge(sig("q_angles"), 2 * (i + 1))
                feature(qf, q2, i).then_inc(sig("qf_ready"), 1)
            aggregate(0, 3)
            slot = ring.wait_filled(v, ("kv",))
            ring.emptied(TS(kv[:, 0:H * (HD + 1)].rearrange("p (b h e) -> p b h e", b=2, h=4),
                            heads(slot, 128), 1.0 / N, None, ALU.mult), ("kv",))

            def divide_heads(dst, slot, eps):
                s = heads(slot)
                r = rden[:, 0:H].rearrange("p (b h) -> p b h", b=2)
                st.did(TS(r, s[:, :, :, HD], eps, None, ALU.add))
                st.wait()
                st.did(v.reciprocal(r, r))
                st.wait()
                return TT(dst.rearrange("p (b h e) -> p b h e", b=2, h=4), s[:, :, :, 0:HD],
                          r.unsqueeze(3).to_broadcast([P, 2, 4, HD]), ALU.mult)

            def attended(i):
                slot = ring.wait_filled(v, ("mo", i))
                if i >= 2:
                    ring.wait_filled(v, ("moT", i - 2))
                ring.emptied(divide_heads(mo[:, i % 2, :], slot, 1e-6), ("mo", i))
                ring.wait_emptied(v, ("mo", i))
                ln_stats([mo[:, i % 2, :]])
                ln_apply(mo[:, i % 2, :], mo[:, i % 2, :]).then_inc(sig("mo_ready"), 1)

            def add_to_x(name, i):
                slot = ring.wait_filled(v, name)
                ring.emptied(TT(x[:, i, :], x[:, i, :], slot[0:P, 0:D], ALU.add), name)

            lagged(attended, lambda i: None, lambda i: add_to_x(("mw", i), i))

            v.wait_ge(sig("bias_loaded"), 32)
            ring.wait_emptied(v, ("mw", NT - 1))
            for n in range(2):
                st.did(TT(x[:, :, :], x[:, :, :],
                          biasr[:, D * n:D * (n + 1)].unsqueeze(1).to_broadcast([P, NT, D]),
                          ALU.add))
                st.wait()
            for l in range(LAYERS):
                if l:
                    for j in range(KC):
                        aggregate(l, j)
                v.wait_ge(sig("b1_loaded"), 16 * (l + 1))
                v.wait_ge(sig("b2_loaded"), 16 * (l + 1))
                if l:
                    v.wait_ge(sig("lng_loaded"), 32 * l)
                for i in range(NT + 2):
                    j = i - 2
                    if i < NT:
                        if i >= 2:
                            ring.wait_filled(v, ("gT", l, i - 2))
                        slot = ring.wait_filled(v, ("u", l, i))
                        ring.emptied(TT(u[:, i % 2, :], slot[0:P, :], b1r, ALU.add), ("u", l, i))
                        ring.wait_emptied(v, ("u", l, i))
                        ln_stats([u[:, i % 2, 0:D], u[:, i % 2, D:HID]])
                    if j >= 0:
                        if l and NT * (l - 1) + j:
                            v.wait_ge(sig("xl_ready"), NT * (l - 1) + j)
                        slot = ring.wait_filled(v, ("y", l, j))
                        y = ytmp if l else xl[:, j, :]
                        ring.emptied(TT(y, slot[0:P, 0:D], b2r, ALU.add), ("y", l, j))
                        ring.wait_emptied(v, ("y", l, j))
                        if l:
                            ln_stats([y])
                    if i < NT:
                        ln_apply(u[:, i % 2, :], u[:, i % 2, :]).then_inc(sig("u_normed"), 1)
                    if j >= 0:
                        if l:
                            st.did(ln_apply(y, y))
                            st.wait()
                            st.did(TT(y, y, lngr, ALU.mult))
                            st.wait()
                            st.did(TT(y, y, lnbr, ALU.add))
                            st.wait()
                            STT(out=xl[:, j, :], in0=y, scalar=0.0, in1=xl[:, j, :],
                                op0=ALU.max, op1=ALU.add).then_inc(sig("xl_ready"), 1)
                            v.wait_ge(sig("xl_ready"), NT * (l - 1) + j + 1)
                        if l + 1 < LAYERS:
                            messages(l + 1, j)
                if l + 1 < LAYERS:
                    largest_exponent(l + 1)
                for i in range(NT + 1):
                    if l + 1 < LAYERS and i < NT:
                        weigh(l + 1, i)
                    if i >= 1:
                        add_to_x(("cw", l, i - 1), i - 1)
            ring.wait_emptied(v, ("cw", LAYERS - 1, NT - 1))

            ln_x()
            v.wait_ge(sig("f0_loaded"), 64)
            v.wait_ge(sig("ones_ready"), 2)
            for i in range(NT):
                slot = ring.wait_filled(v, ("f0", i))
                st.did(v.tensor_copy(lg8[:, i, :], slot[0:P, 512:512 + H]))
                ring.emptied(v.tensor_copy(fh[:, i, :], slot[0:P, 0:D]), ("f0", i))
            st.wait()
            for i in range(NT):
                st.did(v.max(top8[:, i, :], lg8[:, i, :]))
            st.wait()

            def two_weights(gap, exp):
                TT(p12[:, 1, :], top8[:, :, 1], top8[:, :, 0], ALU.subtract)\
                    .then_inc(sig(gap), 1)
                v.wait_ge(sig(exp), 1)
                st.did(TS(p12[:, 2, :], p12[:, 0, :], 1.0, None, ALU.add))
                st.wait()
                st.did(v.reciprocal(p12[:, 2, :], p12[:, 2, :]))
                st.wait()
                st.did(TT(p12[:, 0, :], p12[:, 0, :], p12[:, 2, :], ALU.mult))
                st.wait()

            two_weights("f0_gap", "f0_exp")
            ring.wait_emptied(v, ("f0", NT - 1))
            for i in range(NT):
                st.did(STT(out=fg1[:, i, :], in0=fh[:, i, :], scalar=p12[:, 2, i:i + 1],
                           in1=f0b1r, op0=ALU.mult, op1=ALU.add))
                STT(out=fg2[:, i, :], in0=fh[:, i, :], scalar=p12[:, 0, i:i + 1],
                    in1=f0b1r, op0=ALU.mult, op1=ALU.add).then_inc(sig("f0_in"), 1)
            for i in range(NT):
                v.wait_ge(sig("f0_gelu"), 2 * (i + 1))
                TT(fg1[:, i, :], fg1[:, i, :], fg2[:, i, :], ALU.add).then_inc(sig("fg_ready"), 1)
            for i in range(NT):
                add_to_x(("f0o", i), i)
            ring.wait_emptied(v, ("f0o", NT - 1))

            ln_x()
            v.wait_ge(sig("gat_loaded"), 80)
            flat = hea[:, 0:NT * H * (HD + 1)]
            hea4 = flat.rearrange("p (i h e) -> p i h e", i=NT, h=H)
            st.did(v.memset(flat.rearrange("p (g e) -> p g e", e=HD + 1)[:, :, HD:HD + 1], 1.0))
            st.did(v.memset(hea[:, NT * H * (HD + 1):], 0.0))
            st.did(v.memset(hrTs, 0.0))
            for i in range(NT):
                slot = ring.wait_filled(v, ("hre", i))
                st.did(v.tensor_copy(hea4[:, i, :, 0:HD],
                                     slot[0:P, 0:D].rearrange("p (h e) -> p h e", h=H)))
                ring.emptied(v.tensor_copy(hr[:, i, 0:D], slot[0:P, D:2 * D]), ("hre", i))
                ring.wait_emptied(v, ("hre", i))
                st.wait()
                he_i = hea4[:, i, :, 0:HD]
                for n, t in ((2, he_i), (1, he_i),
                             (3, hr[:, i, 0:D].rearrange("p (h e) -> p h e", h=H))):
                    st.did(TT(tmp[:, n - 1, :].rearrange("p (h e) -> p h e", h=H), t,
                              ar[:, n, :].rearrange("p (h e) -> p h e", h=H), ALU.mult))
                st.wait()
                st.did(v.tensor_reduce(hr[:, i, D:D + H],
                                       tmp[:, 1, :].rearrange("p (h e) -> p h e", h=H),
                                       AX_X, ALU.add))
                st.did(TT(tmp[:, 0, :], tmp[:, 0, :], tmp[:, 2, :], ALU.subtract))
                st.wait()
                v.tensor_reduce(hr[:, i, D + H:D + 2 * H],
                                tmp[:, 0, :].rearrange("p (h e) -> p h e", h=H),
                                AX_X, ALU.add).then_inc(sig("table_ready"), 1)
                v.wait_ge(sig("table_ready"), i + 1)
            ring.wait_emptied(v, ("hrT", NT - 1))
            st.wait()
            for h in range(H):
                half = slice(HD * (h % 2), HD * (h % 2 + 1))
                ins = TS(hrTs[half, h, :], hrT[half, h // 2, :],
                         col("a_prd", h // 2, HD * (h % 2), HD * (h % 2 + 1)),
                         col("a_difT", h // 2, HD * (h % 2), HD * (h % 2 + 1)), ALU.mult, ALU.add)
            ins.then_inc(sig("hrTs_ready"), 1)

            def k_largest(*js):
                for j in js:
                    ring.wait_emptied(v, ("kT", j))
                    v.tensor_reduce(kmax[:, j:j + 1], ek[:, j, :], AX_X, ALU.max, negate=True)\
                        .then_inc(sig("kmax_ready"), 1)

            def values():
                for i in range(NT):
                    slot = ring.wait_filled(v, ("v1", i))
                    ring.emptied(TT(v1[:, i, :], slot[0:P, 0:D], v1r, ALU.add), ("v1", i))

            def context():
                st.did(v.memset(ctxb, 0.0))
                v.wait_ge(sig("ek_ready"), KC)
                st.did(v.reciprocal(krec, ksum))
                st.wait()
                slot = ring.wait_filled(v, ("ctx",))
                for j in range(KC):
                    for g in range(2):
                        r = slice(HD * g, HD * (g + 1))
                        last = TS(ctxb[r, j, HD * g:HD * (g + 1)],
                                  slot[r, 128 * j + HD * g:128 * j + HD * (g + 1)],
                                  krec[r, j:j + 1], None, ALU.mult)
                ring.emptied(last, ("ctx",))

            def mix1_out():
                for i in range(NT):
                    slot = ring.wait_filled(v, ("y1", i))
                    st.did(TT(x[:, i, :], x[:, i, :], b1or, ALU.add))
                    st.wait()
                    ring.emptied(TT(x[:, i, :], x[:, i, :], slot[0:P, 0:D], ALU.add), ("y1", i))

            def index(k, t):
                v.tensor_copy(ix[:, 3 * k:3 * k + 1], srci[:, t]).then_inc(sig("gat_step"), 1)
                v.tensor_copy(ix[:, 3 * k + 1:3 * k + 2], dsti[:, t])\
                    .then_inc(sig("indices_ready"), 1)

            def difference(k, landed):
                v.wait_ge(sig(f"gathered_{k}"), landed)
                TT(dif[:, k, :], gs[:, k, 0:D], gd[:, k, 0:D], ALU.subtract)\
                    .then_inc(sig("differences"), 1)
                TT(e8[:, k, :], gs[:, k, D + H:D + 2 * H], gd[:, k, D:D + H], ALU.add)\
                    .then_inc(sig("gat_ends"), 1)

            def score(k, t, number, sent):
                v.wait_ge(sig("abs_ready"), number)
                TT(dif[:, k, :], dif[:, k, :], ar[:, 0, :], ALU.mult)\
                    .then_inc(sig("weighted"), 1)
                v.wait_ge(sig("weighted"), number)
                if sent is not None:
                    v.wait_ge(sig("scattered"), sent)
                v.tensor_reduce(sc[:, k, :], dif[:, k, :].rearrange("p (h e) -> p h e", h=H),
                                AX_X, ALU.add).then_inc(sig("gat_sums"), 1)
                v.tensor_copy(ix[:, 3 * k + 2:3 * k + 3], pairi[:, t])\
                    .then_inc(sig("gat_pairs"), 1)
                v.wait_ge(sig("gat_sums"), number)
                v.wait_ge(sig("gat_ends"), number)
                TT(sc[:, k, :], sc[:, k, :], e8[:, k, :], ALU.add)\
                    .then_inc(sig("scores_ready"), 1)

            for k in range(GATHERS):
                index(k, slice(k, k + 1))
            for k in range(GATHERS):
                difference(k, 32)
                index(k, slice(GATHERS + k, GATHERS + k + 1))
                if k:
                    score(k - 1, slice(k - 1, k), k, None)

            def edge_tile(it, k):
                def ready():
                    difference(k, (it + 1) * 32)
                    index(k, bass.ds((it + 1) * GATHERS + k, 1))
                if k:
                    ready()
                sent = (it - 1) * (16 * GATHERS) + 16 * k
                score((k - 1) % GATHERS, bass.ds(it * GATHERS + (k - 1), 1), it * GATHERS + k,
                      None if isinstance(it, int) and sent == 0 else sent)
                if not k:
                    ready()

            for k in range(GATHERS):
                edge_tile(1, k)

            def edge_turns(lo, hi):
                with v.Fori(lo, hi) as it:
                    for k in range(GATHERS):
                        edge_tile(it, k)

            k_largest(0, 1)
            edge_turns(2, 4)
            k_largest(2, 3)
            edge_turns(4, 6)
            values()
            edge_turns(6, 10)
            context()
            edge_turns(10, 14)
            mix1_out()
            edge_turns(14, ET // GATHERS - 1)
            LAST = ET - GATHERS
            score(GATHERS - 1, slice(LAST - 1, LAST), LAST, 16 * (LAST - GATHERS))
            for k in range(GATHERS):
                difference(k, 32 * (ET // GATHERS))
                score(k, slice(LAST + k, LAST + k + 1), LAST + k + 1, 16 * (LAST + k + 1 - GATHERS))

            for g in range(NT * H + LAG):
                i, h = divmod(g, H)
                if i < NT:
                    if h == 0:
                        v.wait_ge(sig(f"pairs_loaded_{i % 2}"), 16 * (i // 2 + 1))
                    p3 = pt[i % 2].rearrange("p (d h) -> p d h", h=H)
                    if i:
                        ring.wait_filled(v, ("exT", i - 1, h))
                    slot = ring.wait_filled(v, ("pair", i, h))
                    ring.emptied(v.tensor_tensor_reduce(
                        S[:, h, :], slot[0:P, 0:N], p3[:, :, h], 1.0, -3e38, ALU.add, ALU.max,
                        smax[:, 0, h:h + 1]), ("pair", i, h))
                    ring.wait_emptied(v, ("pair", i, h))
                    st.did(TS(smax[:, 2, h:h + 1], smax[:, 0, h:h + 1], -0.2, None, ALU.mult))
                    st.wait()
                    st.did(STT(out=smax[:, 1, h:h + 1], in0=smax[:, 0, h:h + 1], scalar=-1.0,
                               in1=smax[:, 2, h:h + 1], op0=ALU.mult, op1=ALU.min))
                    st.wait()
                    STT(out=S[:, h, :], in0=S[:, h, :], scalar=0.2, in1=S[:, h, :],
                        op0=ALU.mult, op1=ALU.max).then_inc(sig("leaky_ready"), 1)
                if g >= LAG and (g - LAG) % H == H - 1:
                    j = (g - LAG) // H
                    slot = ring.wait_filled(v, ("att", j))
                    ring.emptied(divide_heads(otmp, slot, 1e-16), ("att", j))
                    ring.wait_emptied(v, ("att", j))
                    st.did(TT(x[:, j, :], x[:, j, :], otmp, ALU.add))
            st.wait()

            ln_x()
            v.wait_ge(sig("f1_loaded"), 64)
            for i in range(NT):
                slot = ring.wait_filled(v, ("f1", i))
                ring.emptied(TT(g1[:, i, 0:WX], slot[0:P, 0:WX], f1r, ALU.add), ("f1", i))
                ring.wait_emptied(v, ("f1", i))
                st.did(v.tensor_copy(lg8[:, i, :], g1[:, i, WX - H:WX]))
                st.wait()
                st.did(v.max(top8[:, i, :], lg8[:, i, :]))
                st.wait()
                st.did(v.max_index(idx8[:, i, :], top8[:, i, :], lg8[:, i, :]))
            st.wait()
            st.did(v.tensor_copy(idf8, idx8))
            two_weights("f1_gap", "f1_exp")
            for i in range(NT):
                comb = g1[:, i, WX - H:WX]
                st.did(TS(comb, io8, idf8[:, i, 1:2], p12[:, 0, i:i + 1], ALU.is_equal, ALU.mult))
                st.did(TS(lg8[:, i, :], io8, idf8[:, i, 0:1], p12[:, 2, i:i + 1],
                          ALU.is_equal, ALU.mult))
                st.wait()
                st.did(TT(comb, comb, lg8[:, i, :], ALU.add))
                st.did(TS(g1[:, i, D:D + HD], g1[:, i, D:D + HD], 0.0, 0.5, ALU.max, ALU.mult))
                st.did(v.memset(g1[:, i, WX:WX + 1], 0.5))
                st.wait()
                h3 = g1[:, i, 0:D].rearrange("p (h e) -> p h e", h=H)
                STT(out=h3, in0=h3, scalar=0.0, in1=comb.unsqueeze(2).to_broadcast([P, H, HD]),
                    op0=ALU.max, op1=ALU.mult).then_inc(sig("g1_ready"), 1)
            for i in range(NT):
                add_to_x(("f1o", i), i)


def lay_out(i):
    import numpy as np

    heads = i["L1_gnn_a"].reshape(H, 5, HD).transpose(1, 0, 2).reshape(5, H * HD)
    vec = {f"mb1_{l}": i[f"L0_gnn_mb1_{l}"] for l in range(LAYERS)}
    vec |= {f"mb2_{l}": i[f"L0_gnn_mb2_{l}"] for l in range(LAYERS)}
    vec |= {f"{n}_{l}": i[f"L0_gnn_{n}_{l}"] for l in (1, 2) for n in ("lng", "lnb")}
    vec |= {"qkv_b": i["L0_mix_qkv_b"], "out_b": i["L0_mix_out_b"], "cb": i["L0_gnn_cb"],
            "f0_b1": i["L0_ffn_b1"].reshape(-1), "v_b": i["L1_mix_b_qkv"][2 * D:],
            "b_out": i["L1_mix_b_out"],
            "f1_b": np.concatenate([i["L1_ffn_b1"].reshape(-1), i["L1_ffn_bs1"], i["L1_ffn_bg"]]),
            "a_src": heads[0], "a_dst": heads[1], "a_dif": heads[2], "a_abs": heads[3],
            "t": np.concatenate([i[f"L0_gnn_t{l}"] for l in range(LAYERS)])}
    col = {f"{n}_{l}": i[f"L0_gnn_{n}_{l}"] for l in range(LAYERS) for n in ("mlg", "mlb")}
    col |= {"ln_g": i["L0_mix_ln_g"], "ln_b": i["L0_mix_ln_b"], "q_b": i["L1_mix_b_qkv"][:D],
            "k_b": i["L1_mix_b_qkv"][D:2 * D], "a_prd": heads[4], "a_difT": heads[2]}

    def experts(w):
        return w.transpose(1, 0, 2).reshape(D, H * HD)

    def zeros(rows, columns):
        return np.zeros((rows, columns), np.float32)

    out = {"x": i["x"], "src": i["src"], "dst": i["dst"],
           "rows": np.concatenate([vec[n] for n, _ in ROWS]),
           "cols": np.concatenate([col[n].reshape(-1, 128).T for n, _ in COLS], axis=1)}
    out |= {f"{n}_{l}": i[f"L0_gnn_{n}_{l}"] for l in range(LAYERS) for n in ("mw1", "mw2")}
    out |= {"cw": i["L0_gnn_cw"], "qkv_w": i["L0_mix_qkv_w"], "out_w": i["L0_mix_out_w"],
            "f0_w1": np.concatenate([experts(i["L0_ffn_W1"]), i["L0_ffn_Wg"],
                                     zeros(D, WP - D - H)], axis=1),
            "f0_w2": i["L0_ffn_W2"].reshape(H * HD, D), 
            "f0_b2": np.concatenate([i["L0_ffn_b2"], zeros(128 - H, D)]),
            "w_er": np.concatenate([experts(i["L1_gnn_W_e"]), experts(i["L1_gnn_W_r"])], axis=1),
            "w_qkvT": i["L1_mix_W_qkv"].T, "w_outT": i["L1_mix_W_out"].T,
            "f1_w": np.concatenate([experts(i["L1_ffn_W1"]), i["L1_ffn_Ws1"], i["L1_ffn_Wg"],
                                    zeros(D, WP - WX)], axis=1),
            "f1_w2": i["L1_ffn_W2"].reshape(H * HD, D),
            "f1_w3": np.concatenate([i["L1_ffn_Ws2"], i["L1_ffn_b2"],
                                     i["L1_ffn_bs2"].reshape(1, D)])}
    return {n: np.ascontiguousarray(v) for n, v in out.items()}


def kernel(**inputs):
    import numpy as np
    import concourse.bacc as bacc
    from concourse.bass_utils import run_bass_kernel_spmd

    nc = bacc.Bacc("TRN2", target_bir_lowering=False, num_devices=1)
    laid = lay_out({n: np.asarray(v) for n, v in inputs.items()})
    arrays = {f"in_{n}": v for n, v in laid.items()}
    aps = {n: nc.dram_tensor(f"in_{n}", v.shape, mybir.dt.from_np(v.dtype),
                             kind="ExternalInput").ap() for n, v in laid.items()}
    out = nc.dram_tensor("out", (N, D), F32, kind="ExternalOutput").ap()
    build_gps(nc, aps, out)
    return run_bass_kernel_spmd(nc, [arrays], core_ids=[0]).results[0]["out"]
```

```python
from contextlib import ExitStack

import concourse.bass as bass
from concourse import mybir

F32 = mybir.dt.float32
F16 = mybir.dt.float16
F32R = mybir.dt.float32r
I32 = mybir.dt.int32
U32 = mybir.dt.uint32
ALU = mybir.AluOpType
ACT = mybir.ActivationFunctionType
AX_X = mybir.AxisListType.X
RMAX = bass.bass_isa.ReduceOp.max

N, E, D = 625, 10000, 512
P = 125
NT = N // P
ET = E // P
KC = D // 128
HID = 2 * D
HC = HID // 128
H, HD = 8, 64
LAYERS = 3
ONE_HOTS = 8
TURN = 5
GATHERS = TURN - 1
TURNS = ET // TURN
TABLE = D + 2 * H
HEADROOM = 64.0
ARENA = 40500
HALF = 2 * ((N + 3) // 4)
PACK = 4096.0
CHUNKS = [(0, 3), (3, 6), (6, 10)]
TURNED_LAG = 1
SUM_LAG = 2
NORM_LAG = 3
LAG = 4
NO_EDGE = -1e30
LN_EPS = 1e-5
PI = 3.141592653589793
WX = D + HD + H
WIDE = 96
WP = D + WIDE
HW = 4 * WIDE
ROWS = [("mb1_0", HID), ("mb1_1", HID), ("mb1_2", HID), ("mb2_0", D), ("mb2_1", D), ("mb2_2", D),
        ("lng_1", D), ("lnb_1", D), ("lng_2", D), ("lnb_2", D), ("qkv_b", 3 * D), ("out_b", D),
        ("cb", D), ("f0_b1", D), ("v_b", D), ("b_out", D), ("f1_b", WX), ("a_abs", D),
        ("a_src", D), ("a_dst", D), ("a_dif", D), ("t", LAYERS)]
COLS = [("mlg_0", HC), ("mlb_0", HC), ("mlg_1", HC), ("mlb_1", HC), ("mlg_2", HC), ("mlb_2", HC),
        ("ln_g", KC), ("ln_b", KC), ("q_b", KC), ("k_b", KC), ("a_prd", KC), ("a_difT", KC)]


def offsets(parts):
    at, out = 0, {}
    for name, n in parts:
        out[name] = (at, n)
        at += n
    return out, at


ROW_AT, ROW_LEN = offsets(ROWS)
COL_AT, COL_LEN = offsets(COLS)


BESIDE_EDGES = ("kT", "qT", "v1", "kn", "ctx", "oT", "y1")

BESIDE_SUMS = ("pair", "exT")


def psum_jobs():
    jobs = [(("xnT", 0, i), "act") for i in range(NT)]
    jobs += [((name, i), "dve") for name in ("qk", "v") for i in range(NT)]
    for l in range(LAYERS):
        for j in range(KC):
            jobs += [(("den", l, j), "dve"), (("num", l, j), "dve")]
        if l == 0:
            jobs += [(("kv",), "dve")]
            jobs += lagged(lambda i: [(("qfT", i), "act")], lambda i: [(("mo", i), "dve")],
                           lambda i: [(("moT", i), "act")], lambda i: [(("mw", i), "dve")])
        jobs += lagged(lambda i: [(("u", l, i), "dve")], lambda i: [(("gT", l, i), "act")],
                       lambda i: [(("y", l, i), "dve")])
        jobs += [(("yT", l, i), "act") for i in range(NT)]
        jobs += lagged(lambda i: [(("cw", l, i), "dve")], lambda i: [],
                       lambda i: [(("xnT", 1, i), "act")] if l + 1 == LAYERS else [])
    jobs += [(("f0", i), "dve") for i in range(NT)]
    jobs += lagged(lambda i: [(("f0T", i), "act")], lambda i: [(("f0o", i), "dve")],
                   lambda i: [], lambda i: [(("xnT", 2, i), "act")])
    jobs += [(("hre", i), "dve") for i in range(NT)]
    jobs += [(("hrT", i), "act") for i in range(NT)]
    jobs += [((name, j), "act") for name in ("kT", "qT") for j in range(KC)]
    jobs += [(("v1", i), "dve") for i in range(NT)]
    jobs += [(("kn", j), "act") for j in range(KC)]
    jobs += [(("ctx",), "dve")]
    jobs += [(("oT", j), "act") for j in range(KC)]
    jobs += [(("y1", i), "dve") for i in range(NT)]
    for g in range(NT * H + LAG):
        if g < NT * H:
            jobs += [(("pair", g // H, g % H), "dve")]
        if g >= LAG:
            i, h = divmod(g - LAG, H)
            jobs += [(("exT", i, h), "act")]
    jobs += [(("xnT", 3, i), "act") for i in range(NT)]
    jobs += [(("f1", i), "dve") for i in range(NT)]
    jobs += lagged(lambda i: [(("f1T", i), "act")], lambda i: [(("f1o", i), "dve")])
    return jobs


def lagged(*steps):
    out = []
    for i in range(NT + len(steps) - 1):
        for n, step in enumerate(steps):
            if 0 <= i - n < NT:
                out += step(i - n) or []
    return out


class PsumRing:

    SLOTS = 4

    def __init__(self, psum, filled, emptied):
        self.psum, self.filled_sem, self.emptied_sem = psum, filled, emptied
        self.place, self.nth, count = {}, [], {"act": 0, "dve": 0}
        self.at, self.before, last = [], [], {}
        for k, (name, who) in enumerate(psum_jobs()):
            count[who] += 1
            self.place[name] = k
            self.nth.append((who, count[who]))
            at = k % (2 if name[0] in BESIDE_EDGES else 3 if name[0] in BESIDE_SUMS else
                      self.SLOTS)
            self.at.append(at)
            self.before.append(last.get(at))
            last[at] = k

    def slot(self, name):
        return self.psum[self.at[self.place[name]]]

    def claim(self, pe, name):
        before = self.before[self.place[name]]
        if before is not None:
            who, n = self.nth[before]
            pe.wait_ge(self.emptied_sem[who], n)
        return self.slot(name)

    def filled(self, last_matmul):
        last_matmul.then_inc(self.filled_sem, 1)

    def wait_filled(self, eng, name):
        eng.wait_ge(self.filled_sem, self.place[name] + 1)
        return self.slot(name)

    def emptied(self, last_read, name):
        last_read.then_inc(self.emptied_sem[self.nth[self.place[name]][0]], 1)

    def wait_emptied(self, eng, name):
        who, n = self.nth[self.place[name]]
        eng.wait_ge(self.emptied_sem[who], n)


class Steps:

    def __init__(self, eng, sem):
        self.eng, self.sem, self.n = eng, sem, 0

    def did(self, ins):
        ins.then_inc(self.sem, 1)
        self.n += 1
        return self.n

    def wait(self, n=None):
        self.eng.wait_ge(self.sem, self.n if n is None else n)


def build_gps(nc, a, out):
    with ExitStack() as ctx:
        with nc.sbuf_tensor("arena", [128, ARENA], F32) as arena:
            pass
        rounded = {}
        for at, end, name in ((0, 13824, None), (13824, 18944, "ex_low"), (18944, 29184, None),
                              (29184, 34304, "high_0"), (34304, 39424, "high_1"),
                              (39424, ARENA, None)):
            rounded[name] = ctx.enter_context(
                nc.sbuf_tensor(name or f"beneath_{at}", [128, end - at], F32R))

        def sb(name, shape, dt=F32):
            return ctx.enter_context(nc.sbuf_tensor(name, shape, dt))

        signals = {}

        def sig(name):
            if name not in signals:
                signals[name] = ctx.enter_context(nc.semaphore(name))
            return signals[name]

        ps = ctx.enter_context(nc.psum_tensor("ps", [128, 4096], F32))
        ring = PsumRing([ps[:, 1024 * s:1024 * (s + 1)] for s in range(4)], sig("psum_filled"),
                        {"act": sig("scalar_emptied"), "dve": sig("vector_emptied")})

        table = nc.dram_tensor("table", (N, TABLE), F32, kind="Internal").ap()
        pairs = nc.dram_tensor("pairs", (N * N, H), F32, kind="Internal").ap()
        pairs_by_src = pairs.rearrange("(i p d) h -> i p (d h)", p=P, d=N)

        x = sb("x", [P, NT, D])
        counts = sb("counts", [P, NT, 2 * HALF], F32R)
        ident = sb("ident", [128, 128])
        cols = sb("cols", [128, COL_LEN])
        srci = sb("srci", [P, ET], I32)
        dsti = sb("dsti", [P, ET], I32)
        pairi = sb("pairi", [P, ET], I32)
        tcol = sb("tcol", [128, LAYERS])
        twos = sb("twos", [128, P])
        stat = sb("stat", [P, 6 * 16])
        small = sb("small", [128, 64 * 16])
        xn = sb("xn", [P, NT, D])
        xnT = sb("xnT", [128, KC, N])

        def view(at, *shape, parts=128):
            n = 1
            for s in shape:
                n *= s
            v = arena[0:parts, at:at + n]
            if len(shape) == 2:
                v = v.rearrange("p (a b) -> p a b", a=shape[0])
            if len(shape) == 3:
                v = v.rearrange("p (a b c) -> p a b c", a=shape[0], b=shape[1])
            return v

        def sm(k, *shape, parts=P):
            n = 1
            for s in shape:
                n *= s
            v = small[0:parts, 64 * k:64 * k + n]
            return v.rearrange("p (a b) -> p a b", a=shape[0]) if len(shape) == 2 else v

        def col(name, k, lo=0, hi=128):
            at = COL_AT[name][0] + k
            return cols[lo:hi, at:at + 1]

        def row(name, parts=P, lo=0, n=None):
            at, full = ROW_AT[name]
            n = n or full
            return a["rows"][at + lo:at + lo + n].partition_broadcast(parts)

        w1 = view(0, KC, HID)
        w2 = view(4096, HC, D)
        cw = view(8192, KC, D)
        b1r = view(10240, HID, parts=P)
        b2r = view(11264, D, parts=P)
        lngr = view(11776, D, parts=P)
        lnbr = view(12288, D, parts=P)
        biasr = view(33000, 2 * D, parts=P)
        ex = view(13824, NT, D, parts=P)
        exm = view(16384, NT, D, parts=P)
        u = view(18944, 2, HID, parts=P)
        xl = view(20992, NT, D, parts=P)
        xlT = view(23552, KC, N)
        ytmp = view(26052, D, parts=P)
        gT = view(26600, HC, N)
        rec = [view(39600, 2 * HALF), view(12800, 2 * HALF)]
        high_0, high_1, low = (
            rounded[name][0:P, :].rearrange("p (s i d) -> p s i d", s=2, i=NT)
            for name in ("high_0", "high_1", "ex_low"))
        high = [high_0, high_1, high_1]
        ex_low, exm_low = low[:, 0], low[:, 1]
        one_hot = view(20000, ONE_HOTS * N, parts=P).bitcast(F16) \
            .rearrange("p (k s n) -> p k s n", k=ONE_HOTS, s=2)
        iota16 = view(25000, 320, parts=P).bitcast(F16)[:, 0:N]
        fill = view(35540, N, parts=P)
        iotai = view(34304, N, parts=P)
        iota16z = view(35000, 256, parts=P).bitcast(F16)
        srcf = view(35300, ET, parts=P)
        dstf = view(35380, ET, parts=P)
        pairf = view(35460, ET, parts=P)
        dstm = view(36200, ET, parts=P)
        dstw = view(36280, ET, parts=P)
        above = view(36360, ET, parts=P)
        neg_dstm = view(36630, ET, parts=P)
        neg_dstw = view(36720, ET, parts=P)
        far = view(25400, ONE_HOTS // 2 * 160, parts=P).bitcast(F16)\
            .rearrange("p (k n) -> p k n", k=ONE_HOTS // 2)
        raw = view(36864, NT, HALF, parts=P)
        upper = view(38500, NT, HALF, parts=P)
        wqkv = view(0, KC, 3 * D)
        wo = view(6144, KC, D)
        qkvr = view(10240, 3 * D, parts=P)
        kv = view(11776, H * (HD + 1) + WIDE - HD - 1)
        qk = view(18944, NT, 2 * D, parts=P)
        kf = qk
        th = view(24064, NT, 2 * D, parts=P)
        qf = view(29184, NT, 2 * D, parts=P)
        q2 = view(34304, NT, D, parts=P)
        va = view(36864, NT * H * (HD + 1) + WIDE - HD - 1, parts=P)
        k3 = xn[:, :, :]
        qfT = view(24064, 2, H * P)
        mo = view(26100, 2, D, parts=P)
        moT = view(27200, 2, KC * P)
        f0w1 = view(0, KC, WP)
        f0w2 = view(2432, KC, D)
        f0b2 = view(4480, D)
        f0b1r = view(12800, D, parts=P)
        fh = view(13824, NT, D, parts=P)
        fg1 = view(16384, NT, D, parts=P)
        fg2 = view(18944, NT, D, parts=P)
        fT = view(21504, 2, KC * P)
        wer = view(5000, KC, 2 * D)
        ar = view(9096, 4, D, parts=P)
        hr = view(11144, NT * TABLE, parts=P).rearrange("p (i c) -> p i c", i=NT)
        hea = view(13784, NT * H * (HD + 1) + WIDE - HD - 1, parts=P)
        hrT = view(16416, KC, N)
        hrTs = view(35500, H, N)
        gs = view(18916, GATHERS, TABLE, parts=P)
        gd = view(21028, GATHERS, TABLE, parts=P)
        edge_hots = view(4220, N + 1, parts=P).bitcast(F16)[:, 0:2 * N]\
            .rearrange("p (s n) -> p s n", s=2)
        edge_iota = view(34840, 320, parts=P).bitcast(F16)[:, 0:N]
        edge_ident = view(33900, 128, parts=P).bitcast(F16)[:, 0:2 * P]\
            .rearrange("p (s n) -> p s n", s=2)
        edge_srcf = view(34030, ET, parts=P)
        edge_dstf = view(34110, ET, parts=P)
        hotsT = view(34200, NT, P, parts=P)
        edge_iota32 = view(34200, N, parts=P)
        difs = [view(23140 + D * k, D, parts=P) for k in range(GATHERS)] + [view(9608, D, parts=P)]
        tmp = view(23140, 3, D, parts=P)
        sc = view(10120, TURN, H, parts=P)
        ix = arena[0:P, 10160:10160 + 3 * TURN].bitcast(I32)
        wqkv1 = view(25240, KC, 3 * D)
        ek = view(31384, KC, N)
        kn = view(25240, NT, D, parts=P)
        qT = view(0, KC, N)
        v1 = xn[:, :, :]
        wo1 = view(5000, KC, D)
        ctxb = view(2500, KC, 128)
        oT = view(27840, KC, N)
        v1r = view(3100, D, parts=P)
        b1or = view(3700, D, parts=P)
        DT = N * H
        pt = [view(18916 + DT * s, DT, parts=P) for s in range(2)]
        S = view(28916, H, N, parts=P)
        exTh = view(5700, H, N, parts=P)
        otmp = view(11200, D, parts=P)
        S_low = view(11800, 2, N, parts=P)
        f1w = view(0, KC, WP)
        f1w2 = view(2432, KC, D)
        f1w3 = view(4480, D, parts=HD + H + 1)
        f1r = view(4996, WX, parts=P)
        g1 = view(13824, NT, WX + 1, parts=P)
        g1T = view(16824, 2, 640)

        mv = sm(0, NT, 2)
        rstd = sm(1, NT)
        nrm2 = small[0:P, 256:336]
        rn = small[0:P, 336:416]
        tn = small[0:P, 416:496]
        pw = small[0:P, 496:536].rearrange("p (i h) -> p i h", i=NT)
        zt = small[0:P, 536:541]
        zmax = small[:, 543:544]
        zall = small[:, 541:542]
        zneg = small[:, 542:543]
        minus_half = small[0:P, 960:1024]
        lg8 = small[0:P, 544:584].rearrange("p (i h) -> p i h", i=NT)
        top8 = small[0:P, 584:624].rearrange("p (i h) -> p i h", i=NT)
        idx8 = small[0:P, 624:664].bitcast(U32).rearrange("p (i h) -> p i h", i=NT)
        idf8 = small[0:P, 664:704].rearrange("p (i h) -> p i h", i=NT)
        p12 = small[0:P, 704:724].rearrange("p (k i) -> p k i", k=4)
        io8 = small[0:P, 724:732]
        kmax = small[:, 732:736]
        ksum = small[:, 736:740]
        krec = small[:, 740:744]
        smax = small[0:P, 744:744 + 88].rearrange("p (k h) -> p k h", h=H)
        rden = small[0:P, 952:960]
        ends = small[0:P, 872:952].rearrange("p (i h s) -> p i h s", i=NT, h=H)
        e8 = small[0:P, 840:872].rearrange("p (k h) -> p k h", h=H)

        def four_to_bank(k):
            return 512 * (k // 4) + P * (k % 4)

        block = ctx.enter_context(nc.Block())

        @block.sync
        def _(sp):
            def load(dst, src, name):
                sp.dma_start(dst, src).then_inc(sig(name), 16)

            def w(name):
                return a[name].rearrange("(k p) n -> p k n", p=128)

            load(srci[:, :], a["src"].rearrange("(p t) -> p t", t=ET), "edges_loaded")
            load(dsti[:, :], a["dst"].rearrange("(p t) -> p t", t=ET), "edges_loaded")
            load(x[:, :, :], a["x"].rearrange("(i p) d -> p i d", p=P), "x_loaded")
            load(cols[:, :], a["cols"], "cols_loaded")
            load(tcol[:, :], row("t", 128), "cols_loaded")
            load(wqkv, w("qkv_w"), "mix0_loaded")
            load(wo, w("out_w"), "mix0_loaded")
            load(qkvr, row("qkv_b"), "mix0_loaded")
            sp.wait_ge(sig("fill_ready"), 1)
            for i in range(NT):
                load(pairs_by_src[i].rearrange("p (h d) -> p h d", h=H),
                     fill.unsqueeze(1).to_broadcast([P, H, N]), "pairs_filled")
            load(cw, w("cw")[:, 0:KC, :], "cw_loaded")
            ring.wait_emptied(sp, ("v", NT - 1))
            load(w1, w("mw1_0"), "w1_loaded")
            load(b1r, row("mb1_0"), "b1_loaded")
            load(b2r, row("mb2_0"), "b2_loaded")
            ring.wait_emptied(sp, ("mw", NT - 1))
            load(w2, w("mw2_0"), "w2_loaded")
            load(biasr[:, 0:D], row("out_b"), "bias_loaded")
            load(biasr[:, D:2 * D], row("cb"), "bias_loaded")
            for l in range(1, LAYERS):
                ring.wait_emptied(sp, ("u", l - 1, NT - 1))
                load(w1, w(f"mw1_{l}"), "w1_loaded")
                load(b1r, row(f"mb1_{l}"), "b1_loaded")
                if l > 1:
                    sp.wait_ge(sig("xl_ready"), NT * (l - 1))
                load(lngr, row(f"lng_{l}"), "lng_loaded")
                load(lnbr, row(f"lnb_{l}"), "lng_loaded")
                ring.wait_emptied(sp, ("y", l - 1, NT - 1))
                load(w2, w(f"mw2_{l}"), "w2_loaded")
                load(b2r, row(f"mb2_{l}"), "b2_loaded")
                ring.wait_emptied(sp, ("cw", l - 1, NT - 1))
                load(cw, w("cw")[:, KC * l:KC * (l + 1), :], "cw_loaded")
            ring.wait_emptied(sp, ("u", LAYERS - 1, NT - 1))
            load(f0w1, w("f0_w1"), "f0_loaded")
            ring.wait_emptied(sp, ("num", LAYERS - 1, KC - 1))
            load(f0b1r, row("f0_b1"), "f0_loaded")
            ring.wait_emptied(sp, ("y", LAYERS - 1, NT - 1))
            load(f0w2, w("f0_w2"), "f0_loaded")
            load(f0b2, a["f0_b2"], "f0_loaded")
            ring.wait_emptied(sp, ("cw", LAYERS - 1, NT - 1))
            load(wer, w("w_er"), "gat_loaded")
            for n, name in enumerate(("a_abs", "a_src", "a_dst", "a_dif")):
                load(ar[:, n, :], row(name), "gat_loaded")
            ring.wait_emptied(sp, ("f0o", NT - 1))
            load(wqkv1, w("w_qkvT"), "mix1_loaded")
            load(v1r, row("v_b"), "mix1_loaded")
            load(b1or, row("b_out"), "mix1_loaded")
            for i in range(NT):
                sp.wait_ge(sig("table_ready"), i + 1)
                load(table[P * i:P * (i + 1), :], hr[:, i, :], "table_stored")
            load(wo1, w("w_outT"), "wo1_loaded")
            sp.wait_ge(sig("scattered"), 16 * ET)
            ring.wait_emptied(sp, ("y1", NT - 1))
            for i in range(NT):
                if i >= 2:
                    ring.wait_emptied(sp, ("pair", i - 2, H - 1))
                load(pt[i % 2], pairs_by_src[i], f"pairs_loaded_{i % 2}")
                if i == 0:
                    load(f1w, w("f1_w"), "f1_loaded")
                    load(f1w2, w("f1_w2"), "f1_loaded")
                    load(f1w3, a["f1_w3"], "f1_loaded")
                    load(f1r, row("f1_b"), "f1_loaded")
            for i in range(NT):
                ring.wait_emptied(sp, ("f1o", i))
                load(out[P * i:P * (i + 1), :], x[:, i, :], "out_stored")
            sp.wait_ge(sig("out_stored"), 16 * NT)

        @block.gpsimd
        def _(pool):
            st = Steps(pool, sig("pool_step"))
            st.did(pool.iota(iotai, pattern=[[1, N]], base=0, channel_multiplier=0,
                             allow_small_or_imprecise_dtypes=True))
            st.did(pool.memset(ident[:, :], 0.0))
            st.wait()
            pool.affine_select(out=ident[:, :], in_=ident[:, :], compare_op=ALU.not_equal, fill=1.0,
                               base=0, pattern=[[-1, 128]],
                               channel_multiplier=1).then_inc(sig("ident_ready"), 1)
            pool.memset(fill, NO_EDGE).then_inc(sig("fill_ready"), 1)
            pool.memset(twos[:, :], 2.0).then_inc(sig("ones_ready"), 1)
            pool.iota(io8, pattern=[[1, H]], base=0, channel_multiplier=0,
                      allow_small_or_imprecise_dtypes=True).then_inc(sig("ones_ready"), 1)
            st.did(pool.memset(minus_half, -0.5))
            st.wait()

            seen = [0]

            def rsqrt_ln(n=1):
                for _ in range(n):
                    i = seen[0] % NT
                    seen[0] += 1
                    pool.wait_ge(sig("variance_ready"), seen[0])
                    pool.tensor_tensor(rstd[:, i:i + 1], mv[:, i, 1:2], minus_half[:, 0:1],
                                       ALU.pow).then_inc(sig("rstd_ready"), 1)

            def largest_exponent(l):
                pool.wait_ge(sig("zmax_ready"), l + 1)
                pool.partition_all_reduce(zall, zmax, 128, RMAX).then_inc(sig("zall_ready"), 1)

            def leave_exm_low(l):
                for i in range(NT):
                    pool.wait_ge(sig("exm_high"), NT * l + i + 1)
                    pool.tensor_tensor(exm_low[:, i, :], exm[:, i, :],
                                       high[l][:, 1, i, :].bitcast(F32), ALU.subtract)\
                        .then_inc(sig("exm_low_ready"), 1)

            rsqrt_ln(NT)
            pool.wait_ge(sig("cols_loaded"), 32)
            for i in range(NT):
                pool.wait_ge(sig("xn_ready"), i + 1)
                st.did(pool.tensor_scalar(exm[:, i, :], xn[:, i, :], 0.0, 1e-7, ALU.max, ALU.add))
                st.wait()
                pool.tensor_scalar(ex[:, i, :], exm[:, i, :], tcol[0:P, 0:1], None, ALU.mult)\
                    .then_inc(sig("messages_ready"), 1)
            largest_exponent(0)
            for i in range(NT):
                pool.wait_ge(sig("ex_ready"), i + 1)
                pool.tensor_tensor(exm[:, i, :], exm[:, i, :], ex[:, i, :], ALU.mult)\
                    .then_inc(sig("exm_ready"), 1)
                pool.wait_ge(sig("exm_ready"), i + 1)
                pool.tensor_tensor(ex_low[:, i, :], ex[:, i, :], high[0][:, 0, i, :].bitcast(F32),
                                   ALU.subtract).then_inc(sig("ex_low_ready"), 1)
            leave_exm_low(0)

            for i in range(NT):
                pool.wait_ge(sig("square_sums"), i + 1)
                pool.tensor_tensor(rn[:, 2 * H * i:2 * H * (i + 1)],
                                   nrm2[:, 2 * H * i:2 * H * (i + 1)],
                                   minus_half[:, 0:1].to_broadcast([P, 2 * H]),
                                   ALU.pow).then_inc(sig("rnorm_ready"), 1)
                pool.wait_ge(sig("k_abs"), i + 1)
                st.did(pool.tensor_tensor(k3[:, i, :], k3[:, i, :], qk[:, i, D:], ALU.mult))
                st.wait()
                pool.tensor_tensor(k3[:, i, :], k3[:, i, :], qk[:, i, D:], ALU.mult)\
                    .then_inc(sig("k_cubed"), 1)
            rsqrt_ln(NT)
            for l in range(LAYERS):
                lagged(lambda i: rsqrt_ln(), lambda i: None, lambda i: rsqrt_ln() if l else None)
                if l + 1 < LAYERS:
                    largest_exponent(l + 1)
                    leave_exm_low(l + 1)
            rsqrt_ln(2 * NT)
            pool.iota(edge_iota32, pattern=[[1, N]], base=0, channel_multiplier=0,
                      allow_small_or_imprecise_dtypes=True).then_inc(sig("edge_iota_ready"), 1)
            pool.wait_ge(sig("table_stored"), 16 * NT)
            pool.wait_ge(sig("pairs_filled"), 16 * NT)

            def gather(k, rows, ends):
                pool.indirect_dma_start(
                    out=rows[:, k, :], out_offset=None, in_=table,
                    in_offset=bass.IndirectOffsetOnAxis(ap=ix[:, 3 * k + ends:3 * k + ends + 1],
                                                        axis=0)
                ).then_inc(sig(f"gathered_{k}"), 16)

            def scatter(k):
                pool.indirect_dma_start(
                    out=pairs, out_offset=bass.IndirectOffsetOnAxis(
                        ap=ix[:, 3 * k + 2:3 * k + 3], axis=0),
                    in_=sc[:, k, :], in_offset=None).then_inc(sig("scattered"), 16)

            for k in range(GATHERS):
                pool.wait_ge(sig("indices_ready"), k + 1)
                gather(k, gs, 0)
                gather(k, gd, 1)

            def gather_sources(it, k):
                pool.wait_ge(sig("indices_ready"), it * GATHERS + k + 1)
                pool.sem_inc(sig("gathers_begun"), 1)
                gather(k, gs, 0)

            def scatter_before(it, k):
                pool.wait_ge(sig("scores_ready"), it * TURN + (k - TURN + 1))
                if not (isinstance(it, int) and it == 1 and k == 0):
                    pool.wait_ge(sig("scattered"), it * (16 * TURN) + 16 * (k - TURN))
                pool.sem_inc(sig("scatters_begun"), 1)
                scatter(k)

            def pool_turn(it):
                for k in range(GATHERS):
                    gather_sources(it, k)
                    scatter_before(it, k)
                    gather(k, gd, 1)
                scatter_before(it, GATHERS)

            pool_turn(1)
            with pool.Fori(2, TURNS) as it:
                pool_turn(it)
            for k in range(TURN):
                pool.wait_ge(sig("scores_ready"), ET - TURN + k + 1)
                pool.wait_ge(sig("scattered"), 16 * (ET - TURN + k))
                scatter(k)
            for g in range(NT * H + LAG + SUM_LAG):
                i, h = divmod(g, H)
                if i < NT:
                    pool.wait_ge(sig("larger_ready"), g + 1)
                    pool.tensor_tensor(S[:, h, :], S[:, h, :], counts[:, i, 0:N].bitcast(F32),
                                       ALU.mult).then_inc(sig("pair_weighted"), 1)
                if g >= LAG + SUM_LAG and (g - LAG - SUM_LAG) % H == H - 1:
                    rsqrt_ln()

        @block.tensor
        def _(pe):
            mm = pe.matmul

            def turn(name, src_of, widths, at_of=None):
                slot = ring.claim(pe, name)
                for k, n in enumerate(widths):
                    at = at_of(k)
                    src = src_of(k)
                    rows = src.shape[0]
                    last = pe.transpose(slot[0:n, at:at + rows], src, ident[0:rows, 0:rows])
                ring.filled(last)

            def product(slot, m, lhsT_of, rhs_of, ks, n, extra=None):
                for lo in range(0, n, 512):
                    hi = min(lo + 512, n)
                    for k in range(ks):
                        last = mm(slot[0:m, lo:hi], lhsT_of(k), rhs_of(k)[:, lo:hi],
                                  start=(k == 0), stop=(k == ks - 1))
                return last

            def nodes(t, i):
                return lambda k: t[:, k, P * i:P * (i + 1)]

            pe.wait_ge(sig("zeros_ready"), 1)
            for n, (lo, hi) in enumerate(CHUNKS):
                if n:
                    pe.wait_ge(sig("raw_copied"), n)
                for i in range(NT):
                    mm(ps[0:P, 512 * i:512 * i + HALF], iota16z[:, 0:P], iota16z[:, 0:HALF],
                       start=True, stop=False, skip_group_check=True)
                with pe.Fori(lo, hi) as it:
                    for k in range(ONE_HOTS):
                        pe.wait_ge(sig("one_hots_ready"),
                                   it * (3 * ONE_HOTS // 2) + k + 1 + k // 2 + 1)
                        if k % 2:
                            pe.wait_ge(sig("scalar_hots_ready"),
                                       it * (ONE_HOTS // 2) + (k + 1) // 2)
                        for i in range(NT):
                            last = mm(ps[0:P, 512 * i:512 * i + HALF],
                                      one_hot[:, k, 0, P * i:P * (i + 1)],
                                      one_hot[:, k, 1, 0:HALF], start=False, stop=False,
                                      skip_group_check=True)
                        last.then_inc(sig("one_hots_used"), 1)
            pe.wait_ge(sig("raw_copied"), len(CHUNKS))

            def turn_xn(n, tiles=range(NT)):
                for i in tiles:
                    pe.wait_ge(sig("xn_ready"), NT * n + i + 1)
                    turn(("xnT", n, i), lambda k: xn[:, i, 128 * k:128 * (k + 1)], [128] * KC,
                         four_to_bank)

            pe.wait_ge(sig("ident_ready"), 1)
            turn_xn(0)

            pe.wait_ge(sig("mix0_loaded"), 48)
            for i in range(NT):
                ring.wait_emptied(pe, ("xnT", 0, i))
                slot = ring.claim(pe, ("qk", i))
                ring.filled(product(slot, P, nodes(xnT, i), lambda k: wqkv[:, k, :], KC, 2 * D))
            for i in range(NT):
                slot = ring.claim(pe, ("v", i))
                ring.filled(product(slot, P, nodes(xnT, i), lambda k: wqkv[:, k, 2 * D:], KC, D))
            def head_at(h):
                return 512 * (h // 4) + WIDE * (h % 4)

            def mix0():
                pe.wait_ge(sig("kf_ready"), NT)
                pe.wait_ge(sig("va_ones"), 2)
                slot = ring.claim(pe, ("kv",))
                for h in range(H):
                    at = head_at(h)
                    for i in range(NT):
                        v0 = (HD + 1) * (H * i + h)
                        last = mm(slot[:, at:at + WIDE], kf[:, i, 128 * h:128 * (h + 1)],
                                  va[:, v0:v0 + WIDE], start=(i == 0), stop=(i == NT - 1),
                                  skip_group_check=True)
                ring.filled(last)

                def turn_q(i):
                    pe.wait_ge(sig("qf_ready"), i + 1)
                    turn(("qfT", i), lambda k: qf[:, i, 128 * k:128 * (k + 1)], [128] * H,
                         four_to_bank)

                def attend(i):
                    slot = ring.claim(pe, ("mo", i))
                    ring.wait_emptied(pe, ("kv",))
                    ring.wait_emptied(pe, ("qfT", i))
                    for h in range(H):
                        at = head_at(h)
                        last = mm(slot[0:P, at:at + WIDE], qfT[:, i % 2, P * h:P * (h + 1)],
                                  kv[:, (HD + 1) * h:(HD + 1) * h + WIDE], start=True, stop=True,
                                  skip_group_check=True)
                    ring.filled(last)

                def turn_out(i):
                    pe.wait_ge(sig("mo_ready"), i + 1)
                    turn(("moT", i), lambda k: mo[:, i % 2, 128 * k:128 * (k + 1)], [128] * KC,
                         four_to_bank)

                def project(i):
                    slot = ring.claim(pe, ("mw", i))
                    ring.wait_emptied(pe, ("moT", i))
                    ring.filled(product(slot, P, lambda k: moT[:, i % 2, P * k:P * (k + 1)],
                                        lambda k: wo[:, k, :], KC, D))

                lagged(turn_q, attend, turn_out, project)

            for l in range(LAYERS):
                if l == 0:
                    pe.wait_ge(sig("counts_ready"), 1)
                pe.wait_ge(sig("ex_low_ready"), NT * (l + 1))
                pe.wait_ge(sig("exm_low_ready"), NT * (l + 1))
                for j in range(KC):
                    for n, (name, low) in enumerate((("den", ex_low), ("num", exm_low))):
                        slot = ring.claim(pe, (name, l, j))
                        for b in range(2):
                            for part in (high[l][:, n], low):
                                for i in range(NT):
                                    last = mm(slot[:, 512 * b:512 * b + HALF],
                                              part[:, i, 128 * j:128 * (j + 1)],
                                              counts[:, i, HALF * b:HALF * (b + 1)],
                                              start=(part is not low and i == 0),
                                              stop=(part is low and i == NT - 1))
                        ring.filled(last)
                if l == 0:
                    mix0()
                pe.wait_ge(sig("w1_loaded"), 16 * (l + 1))
                hT = xlT if l else xnT

                def widen(i):
                    slot = ring.claim(pe, ("u", l, i))
                    for k in range(KC):
                        if i == 0:
                            pe.wait_ge(sig("hT_ready"), KC * l + k + 1)
                        for lo in range(0, HID, 512):
                            last = mm(slot[0:P, lo:lo + 512], nodes(hT, i)(k),
                                      w1[:, k, lo:lo + 512], start=(k == 0), stop=(k == KC - 1))
                    ring.filled(last)

                def turn_hidden(i):
                    pe.wait_ge(sig("u_normed"), NT * l + i + 1)
                    turn(("gT", l, i), lambda k: u[:, i % 2, 128 * k:128 * (k + 1)], [128] * HC,
                         four_to_bank)

                def narrow(i):
                    slot = ring.claim(pe, ("y", l, i))
                    if i == 0:
                        pe.wait_ge(sig("w2_loaded"), 16 * (l + 1))
                    ring.wait_emptied(pe, ("gT", l, i))
                    ring.filled(product(slot, P, nodes(gT, i), lambda k: w2[:, k, :], HC, D))

                lagged(widen, turn_hidden, narrow)
                for i in range(NT):
                    if l:
                        pe.wait_ge(sig("xl_ready"), NT * (l - 1) + i + 1)
                    else:
                        ring.wait_emptied(pe, ("y", l, i))
                    turn(("yT", l, i), lambda k: xl[:, i, 128 * k:128 * (k + 1)], [128] * KC,
                         four_to_bank)
                pe.wait_ge(sig("cw_loaded"), 16 * (l + 1))

                def mix_layers(i):
                    slot = ring.claim(pe, ("cw", l, i))
                    ring.wait_emptied(pe, ("yT", l, i))
                    ring.filled(product(slot, P, nodes(xlT, i), lambda k: cw[:, k, :], KC, D))

                lagged(mix_layers, lambda i: None,
                       lambda i: turn_xn(1, [i]) if l + 1 == LAYERS else None)

            pe.wait_ge(sig("f0_loaded"), 64)
            for i in range(NT):
                slot = ring.claim(pe, ("f0", i))
                ring.wait_emptied(pe, ("xnT", 1, i))
                ring.filled(product(slot, P, nodes(xnT, i), lambda k: f0w1[:, k, :], KC, WP))

            def turn_f0(i):
                pe.wait_ge(sig("fg_ready"), i + 1)
                turn(("f0T", i), lambda k: fg1[:, i, 128 * k:128 * (k + 1)], [128] * KC,
                     four_to_bank)

            def out_f0(i):
                slot = ring.claim(pe, ("f0o", i))
                ring.wait_emptied(pe, ("f0T", i))
                for k in range(KC):
                    mm(slot[0:P, 0:D], fT[:, i % 2, P * k:P * (k + 1)], f0w2[:, k, :],
                       start=(k == 0), stop=False)
                ring.filled(mm(slot[0:P, 0:D], twos[:, :], f0b2, start=False, stop=True))

            lagged(turn_f0, out_f0, lambda i: None, lambda i: turn_xn(2, [i]))

            pe.wait_ge(sig("gat_loaded"), 80)
            for i in range(NT):
                slot = ring.claim(pe, ("hre", i))
                ring.wait_emptied(pe, ("xnT", 2, i))
                ring.filled(product(slot, P, nodes(xnT, i), lambda k: wer[:, k, :], KC, 2 * D))
            for i in range(NT):
                ring.wait_emptied(pe, ("hre", i))
                turn(("hrT", i), lambda k: hr[:, i, 128 * k:128 * (k + 1)], [128] * KC,
                     four_to_bank)

            turned, product_at = ring.psum[2], ring.psum[3]

            def edge_turn(it):
                pe.wait_ge(sig("edge_hots_ready"), it + 1)
                for i in range(NT):
                    for s in range(2):
                        at = 512 * (i // 4) + P * (i % 4)
                        last = mm(turned[0:P, at:at + P], edge_hots[:, s, P * i:P * (i + 1)],
                                  edge_ident[:, s, :], start=(s == 0), stop=(s == 1))
                last.then_inc(sig("edge_turned"), 1)
                if not (isinstance(it, int) and it == 0):
                    pe.wait_ge(sig("scores_ready"), it * TURN)
                pe.wait_ge(sig("hotsT_ready"), it + 1)
                for b, n in ((0, 256), (1, 256 + H)):
                    for i in range(NT):
                        last = mm(product_at[0:P, 512 * b:512 * b + n], hotsT[:, i, :],
                                  hr[:, i, 256 * b:256 * b + n], start=(i == 0),
                                  stop=(i == NT - 1))
                last.then_inc(sig("edge_product"), 1)

            def edge_turns(lo, hi):
                with pe.Fori(lo, hi) as it:
                    edge_turn(it)

            ring.wait_emptied(pe, ("hrT", NT - 1))
            pe.wait_ge(sig("table_ready"), NT)
            edge_turn(0)
            edge_turns(1, 2)

            pe.wait_ge(sig("mix1_loaded"), 48)
            for n in range(2 * KC):
                name, lo, j = (("kT", D), ("qT", 0))[n // KC] + (n % KC,)
                slot = ring.claim(pe, (name, j))
                ring.filled(product(
                    slot, 128, lambda k: wqkv1[:, k, lo + 128 * j:lo + 128 * (j + 1)],
                    lambda k: xnT[:, k, :], KC, N))
                edge_turns(n + 2, n + 3)

            def value(i):
                slot = ring.claim(pe, ("v1", i))
                ring.filled(product(slot, P, nodes(xnT, i), lambda k: wqkv1[:, k, 2 * D:], KC, D))

            def mix1_project(i):
                slot = ring.claim(pe, ("y1", i))
                ring.filled(product(slot, P, nodes(oT, i), lambda k: wo1[:, k, :], KC, D))

            value(0)
            value(1)
            edge_turns(10, 11)
            value(2)
            value(3)
            edge_turns(11, 12)
            value(4)
            for j in range(KC):
                pe.wait_ge(sig("ek_ready"), j + 1)
                turn(("kn", j), lambda k: ek[:, j, P * k:P * (k + 1)], [P] * NT, lambda k: 128 * k)
            edge_turns(12, 13)
            slot = ring.claim(pe, ("ctx",))
            ring.wait_emptied(pe, ("kn", KC - 1))
            ring.wait_emptied(pe, ("v1", NT - 1))
            for j in range(KC):
                for i in range(NT):
                    last = mm(slot[:, 128 * j:128 * (j + 1)], kn[:, i, 128 * j:128 * (j + 1)],
                              v1[:, i, 128 * j:128 * (j + 1)], start=(i == 0),
                              stop=(i == NT - 1), skip_group_check=True)
            ring.filled(last)
            edge_turns(13, 14)
            ring.wait_emptied(pe, ("ctx",))
            for j in range(KC):
                slot = ring.claim(pe, ("oT", j))
                ring.filled(product(slot, 128, lambda k: ctxb[:, j, :],
                                    lambda k: qT[:, j, :], 1, N))
            edge_turns(14, 15)
            ring.wait_emptied(pe, ("oT", KC - 1))
            pe.wait_ge(sig("wo1_loaded"), 16)
            mix1_project(0)
            mix1_project(1)
            edge_turns(15, 16)
            for i in range(2, NT):
                mix1_project(i)
            pe.wait_ge(sig("scores_ready"), ET)

            pe.wait_ge(sig("hrTs_ready"), 1)
            sums = ring.psum[3]
            for g in range(NT * H + LAG + TURNED_LAG):
                i, h = divmod(g, H)
                if i < NT:
                    slot = ring.claim(pe, ("pair", i, h))
                    ring.filled(product(slot, P, lambda k: hrTs[:, h, P * i:P * (i + 1)],
                                        lambda k: hrT[:, h // 2, :], 1, N))
                i, h = divmod(g - LAG, H)
                if 0 <= i < NT:
                    pe.wait_ge(sig("pair_weighted"), i * H + h + 1)
                    turn(("exT", i, h), lambda k: S[:, h, P * k:P * (k + 1)], [P] * NT,
                         lambda k: 128 * k)
                i, h = divmod(g - LAG - TURNED_LAG, H)
                if 0 <= i < NT:
                    ring.wait_emptied(pe, ("exT", i, h))
                    if i and h % 4 == 0:
                        pe.wait_ge(sig("sums_used"), 2 * i - 1 + h // 4)
                    at = head_at(h)
                    for k in range(NT):
                        v0 = (HD + 1) * (H * k + h)
                        last = mm(sums[0:P, at:at + WIDE], exTh[:, h, P * k:P * (k + 1)],
                                  hea[:, v0:v0 + WIDE], start=(k == 0), stop=(k == NT - 1),
                                  skip_group_check=True)
                    last.then_inc(sig("head_summed"), 1)
            pe.wait_ge(sig("sums_used"), 2 * NT)

            turn_xn(3)
            pe.wait_ge(sig("f1_loaded"), 64)
            for i in range(NT):
                slot = ring.claim(pe, ("f1", i))
                ring.wait_emptied(pe, ("xnT", 3, i))
                ring.filled(product(slot, P, nodes(xnT, i), lambda k: f1w[:, k, :], KC, WP))
            KX = HD + H + 1

            def turn_f1(i):
                pe.wait_ge(sig("g1_ready"), i + 1)
                turn(("f1T", i), lambda k: g1[:, i, 128 * k:min(128 * (k + 1), WX + 1)],
                     [128] * KC + [KX], four_to_bank)

            def out_f1(i):
                slot = ring.claim(pe, ("f1o", i))
                ring.wait_emptied(pe, ("f1T", i))
                for k in range(KC):
                    mm(slot[0:P, 0:D], g1T[:, i % 2, P * k:P * (k + 1)], f1w2[:, k, :],
                       start=(k == 0), stop=False)
                ring.filled(mm(slot[0:P, 0:D], g1T[0:KX, i % 2, 512:512 + P], f1w3,
                               start=False, stop=True))

            lagged(turn_f1, out_f1)

        @block.scalar
        def _(act):
            st = Steps(act, sig("scalar_step"))
            def copy(dst, src):
                return act.activation(dst, src, ACT.Copy)

            def empty_turned(name, dst, n, k=KC):
                slot = ring.wait_filled(act, name)
                ring.emptied(copy(dst, slot[0:128, 0:k * P].rearrange("p (k n) -> p k n", k=k)),
                             name)

            def xn_turned(n):
                for i in range(NT):
                    empty_turned(("xnT", n, i), xnT[:, :, P * i:P * (i + 1)], P)

            def one_hots(it, k):
                static = isinstance(it, int) and it == 0
                t = slice(k, k + 1) if static else bass.ds(it * ONE_HOTS + k, 1)
                if not static:
                    act.wait_ge(sig("one_hots_used"), it * ONE_HOTS + (k + 1 - ONE_HOTS))
                act.activation(far[:, k // 2, 0:HALF], iota16[:, 0:HALF], ACT.Abs,
                               bias=neg_dstm[:, t]).then_inc(sig("far_ready"), 1)
                act.wait_ge(sig("far_ready"), it * (ONE_HOTS // 2) + (k + 1) // 2)
                act.activation(one_hot[:, k, 1, 0:HALF], far[:, k // 2, 0:HALF], ACT.Relu,
                               scale=neg_dstw[:, t], bias=dstw[:, t])\
                    .then_inc(sig("scalar_hots_ready"), 1)

            def one_hot_turns(lo, hi):
                with act.Fori(lo, hi) as it:
                    for k in range(1, ONE_HOTS, 2):
                        one_hots(it, k)

            def exponentials(l, tiles=range(NT)):
                act.wait_ge(sig("zneg_ready"), l + 1)
                for i in tiles:
                    act.activation(high[l][:, 0, i, :], ex[:, i, :], ACT.Exp,
                                   bias=zneg[0:P, :]).then_inc(sig("ex_high"), 1)
                    act.wait_ge(sig("ex_high"), NT * l + i + 1)
                    act.activation(ex[:, i, :], ex[:, i, :], ACT.Exp, bias=zneg[0:P, :])\
                       .then_inc(sig("ex_ready"), 1)

            def high_of_exm(l):
                for i in range(NT):
                    act.wait_ge(sig("exm_ready"), NT * l + i + 1)
                    act.activation(high[l][:, 1, i, :], exm[:, i, :], ACT.Copy)\
                       .then_inc(sig("exm_high"), 1)

            def copy_counts(n):
                act.wait_ge(sig("one_hots_used"), CHUNKS[n][1] * ONE_HOTS)
                if n:
                    act.wait_ge(sig("unpacked"), n)
                act.activation(raw, ps[0:P, 0:512 * NT].rearrange("p (i n) -> p i n", i=NT)
                               [:, :, 0:HALF], ACT.Copy).then_inc(sig("raw_copied"), 1)

            act.wait_ge(sig("hot_terms_ready"), 2)
            for k in range(1, ONE_HOTS, 2):
                one_hots(0, k)
            one_hot_turns(1, 3)
            copy_counts(0)
            one_hot_turns(3, 6)
            copy_counts(1)
            one_hot_turns(6, 7)
            exponentials(0, range(3))
            one_hot_turns(7, 8)
            exponentials(0, range(3, NT))
            one_hot_turns(8, 9)
            high_of_exm(0)
            one_hot_turns(9, 10)
            copy_counts(2)
            xn_turned(0)

            for i in range(NT):
                ring.wait_emptied(act, ("qk", i))
                act.activation(th[:, i, :], qk[:, i, :], ACT.Square).then_inc(sig("squares"), 1)
                act.activation(k3[:, i, :], qk[:, i, D:], ACT.Abs).then_inc(sig("k_abs"), 1)
            act.wait_ge(sig("norms_ready"), 1)
            act.activation(pw, tn.rearrange("p (i s h) -> p i s h", i=NT, s=2)
                           [:, :, 0, :], ACT.Tanh).then_inc(sig("tanh_norm"), 1)

            def halves_tanh(s):
                for i in range(NT):
                    act.wait_ge(sig("scaled_k" if s else "scaled_q"), i + 1)
                    t = th[:, i, D * s:D * (s + 1)]
                    if not s:
                        st.wait(st.n - NT + i + 1)
                    act.activation(t, t, ACT.Tanh, scale=20.0).then_inc(sig("tanh_done"), 1)

            def angles(f, s, name):
                for i in range(NT):
                    act.wait_ge(sig("tanh_done"), NT * (1 - s) + i + 1)
                    if s:
                        act.wait_ge(sig("scaled_q"), i + 1)
                    o = f[:, i, :].rearrange("p (h c e) -> p h c e", h=H, c=2)
                    t = th[:, i, D * s:D * (s + 1)].rearrange("p (h e) -> p h e", h=H)
                    act.activation(o[:, :, 0, :], t, ACT.Sin, scale=PI / 4, bias=PI / 2)\
                       .then_inc(sig(name), 1)
                    act.activation(o[:, :, 1, :], t, ACT.Sin, scale=PI / 4)\
                       .then_inc(sig(name), 1)

            halves_tanh(1)
            act.wait_ge(sig("k_cubed"), NT)
            angles(kf, 1, "k_angles")
            act.wait_ge(sig("pairs_filled"), 16 * NT)
            for i in range(NT):
                act.wait_ge(sig("scaled_q"), i + 1)
                st.did(act.activation(q2[:, i, :], th[:, i, 0:D], ACT.Square))
            halves_tanh(0)
            ring.wait_filled(act, ("num", 0, KC - 1))
            angles(qf, 0, "q_angles")
            for i in range(NT):
                act.activation(q2[:, i, :], q2[:, i, :], ACT.Ln, bias=1e-19)\
                   .then_inc(sig("q_logs"), 1)
            for i in range(NT):
                act.wait_ge(sig("q_powers"), i + 1)
                act.activation(q2[:, i, :], q2[:, i, :], ACT.Exp).then_inc(sig("q_feats"), 1)

            def q_turned(i):
                slot = ring.wait_filled(act, ("qfT", i))
                if i == 0:
                    act.wait_ge(sig("q_angles"), 2 * NT)
                if i >= 2:
                    ring.wait_filled(act, ("mo", i - 2))
                o = qfT[:, i % 2, :].rearrange("p (b n) -> p b n", b=2)
                v = slot.rearrange("p (b n) -> p b n", b=2)[:, :, 0:4 * P]
                ring.emptied(copy(o, v), ("qfT", i))

            def mo_turned(i):
                slot = ring.wait_filled(act, ("moT", i))
                if i >= 2:
                    ring.wait_filled(act, ("mw", i - 2))
                for k in range(KC):
                    last = act.activation(moT[:, i % 2, P * k:P * (k + 1)],
                                          slot[:, P * k:P * (k + 1)], ACT.Identity,
                                          scale=col("ln_g", k), bias=col("ln_b", k))
                ring.emptied(last, ("moT", i))

            act.wait_ge(sig("cols_loaded"), 32)
            lagged(q_turned, lambda i: None, mo_turned)

            for l in range(LAYERS):
                for i in range(NT):
                    slot = ring.wait_filled(act, ("gT", l, i))
                    for k in range(HC):
                        at = four_to_bank(k)
                        last = act.activation(gT[:, k, P * i:P * (i + 1)], slot[:, at:at + P],
                                              ACT.Relu, scale=col(f"mlg_{l}", k),
                                              bias=col(f"mlb_{l}", k))
                    ring.emptied(last, ("gT", l, i))
                for i in range(NT):
                    empty_turned(("yT", l, i), xlT[:, :, P * i:P * (i + 1)], P)
                if l + 1 < LAYERS:
                    exponentials(l + 1)
                    high_of_exm(l + 1)

            xn_turned(1)
            act.wait_ge(sig("f0_gap"), 1)
            act.activation(p12[:, 0, :], p12[:, 1, :], ACT.Exp).then_inc(sig("f0_exp"), 1)
            for i in range(NT):
                act.wait_ge(sig("f0_in"), 2 * i + 1)
                act.activation(fg1[:, i, :], fg1[:, i, :], ACT.Gelu).then_inc(sig("f0_gelu"), 1)
                act.wait_ge(sig("f0_in"), 2 * i + 2)
                act.activation(fg2[:, i, :], fg2[:, i, :], ACT.Gelu).then_inc(sig("f0_gelu"), 1)
            for i in range(NT):
                if i >= 2:
                    ring.wait_filled(act, ("f0o", i - 2))
                slot = ring.wait_filled(act, ("f0T", i))
                ring.emptied(copy(fT[:, i % 2, :], slot[:, 0:KC * P]), ("f0T", i))

            xn_turned(2)
            for i in range(NT):
                empty_turned(("hrT", i), hrT[:, :, P * i:P * (i + 1)], P)

            def edge_turns(lo, hi):
                with act.Fori(lo, hi) as it:
                    act.wait_ge(sig("edge_turned"), it + 1)
                    act.activation(hotsT[:, 0:4, :], ring.psum[2][0:P, 0:4 * P]
                                   .rearrange("p (i n) -> p i n", i=4), ACT.Copy)\
                       .then_inc(sig("scalar_edge_step"), 1)
                    act.activation(hotsT[:, 4, :], ring.psum[2][0:P, 512:512 + P], ACT.Copy)\
                       .then_inc(sig("hotsT_ready"), 1)
                    for k in range(GATHERS):
                        act.wait_ge(sig("differences"), it * GATHERS + k + 1)
                        act.activation(difs[k], difs[k], ACT.Abs)\
                           .then_inc(sig("abs_ready"), 1)
                    act.wait_ge(sig("edge_product"), it + 1)
                    act.activation(difs[GATHERS].rearrange("p (b n) -> p b n", b=2),
                                   ring.psum[3][0:P, :].rearrange("p (b n) -> p b n", b=2)
                                   [:, :, 0:256], ACT.Abs).then_inc(sig("abs_ready"), 1)

            def kq_turned(name, dst, bias, *js):
                for j in js:
                    slot = ring.wait_filled(act, (name, j))
                    ring.emptied(act.activation(dst[:, j, :], slot[:, 0:N], ACT.Identity,
                                                bias=col(bias, j)), (name, j))

            def k_exponentials():
                for j in range(KC):
                    act.wait_ge(sig("kmax_ready"), j + 1)
                    act.activation(ek[:, j, :], ek[:, j, :], ACT.Exp, bias=kmax[:, j:j + 1],
                                   accum_out=ksum[:, j:j + 1]).then_inc(sig("ek_ready"), 1)

            def k_natural():
                ring.wait_emptied(act, ("v1", NT - 1))
                for j in range(KC):
                    slot = ring.wait_filled(act, ("kn", j))
                    ring.emptied(copy(kn[:, :, 128 * j:128 * (j + 1)],
                                      slot[0:P, 0:NT * 128].rearrange("p (i c) -> p i c", i=NT)),
                                 ("kn", j))

            def out_turned():
                for j in range(KC):
                    slot = ring.wait_filled(act, ("oT", j))
                    ring.emptied(copy(oT[:, j, :], slot[:, 0:N]), ("oT", j))

            edge_turns(0, 3)
            kq_turned("kT", ek, "k_b", 0, 1)
            edge_turns(3, 5)
            kq_turned("kT", ek, "k_b", 2, 3)
            edge_turns(5, 7)
            kq_turned("qT", qT, "q_b", 0, 1)
            k_exponentials()
            edge_turns(7, 9)
            kq_turned("qT", qT, "q_b", 2, 3)
            edge_turns(9, 12)
            k_natural()
            edge_turns(12, 14)
            out_turned()
            edge_turns(14, TURNS)
            for g in range(NT * H + LAG):
                if g >= LAG:
                    i, h = divmod(g - LAG, H)
                    slot = ring.wait_filled(act, ("exT", i, h))
                    if i:
                        act.wait_ge(sig("head_summed"), (i - 1) * H + h + 1)
                    ring.emptied(copy(exTh[:, h, :].rearrange("p (k n) -> p k n", k=NT),
                                      slot[0:P, 0:NT * 128].rearrange("p (k n) -> p k n", k=NT)
                                      [:, :, 0:P]), ("exT", i, h))
                i, h = divmod(g, H)
                if i < NT:
                    act.wait_ge(sig("bias_ready"), g + 1)
                    if g >= 2:
                        act.wait_ge(sig("larger_ready"), g - 1)
                    act.activation(S_low[:, g % 2, :], S[:, h, :], ACT.Exp, scale=0.2,
                                   bias=smax[:, 3 + h, 1:2]).then_inc(sig("exp_low"), 1)
                    act.wait_ge(sig("exp_low"), g + 1)
                    act.activation(S[:, h, :], S[:, h, :], ACT.Exp,
                                   bias=smax[:, 3 + h, 0:1]).then_inc(sig("pair_exp"), 1)

            xn_turned(3)
            act.wait_ge(sig("f1_gap"), 1)
            act.activation(p12[:, 0, :], p12[:, 1, :], ACT.Exp).then_inc(sig("f1_exp"), 1)
            for i in range(NT):
                if i >= 2:
                    ring.wait_filled(act, ("f1o", i - 2))
                slot = ring.wait_filled(act, ("f1T", i))
                copy(g1T[:, i % 2, 0:KC * P], slot[:, 0:KC * P])
                ring.emptied(copy(g1T[0:HD + H + 1, i % 2, 512:512 + P],
                                  slot[0:HD + H + 1, 512:512 + P]), ("f1T", i))

        @block.vector
        def _(v):
            st = Steps(v, sig("vector_step"))
            TT, TS, STT = v.tensor_tensor, v.tensor_scalar, v.scalar_tensor_tensor
            lns, lns_done = [0], [0]

            def ln_stats(parts):
                i = lns[0] % NT
                lns[0] += 1
                for n, part in enumerate(parts):
                    st.did(v.bn_stats(stat[:, 12 * i + 6 * n:12 * i + 6 * (n + 1)], part))
                st.wait()
                st.did(v.bn_aggr(mv[:, i, :], stat[:, 12 * i:12 * i + 6 * len(parts)]))
                st.wait()
                TS(mv[:, i, 1:2], mv[:, i, 1:2], LN_EPS, None, ALU.add)\
                    .then_inc(sig("variance_ready"), 1)

            def ln_apply(dst, src):
                i = lns_done[0] % NT
                lns_done[0] += 1
                v.wait_ge(sig("rstd_ready"), lns_done[0])
                return TS(dst, src, mv[:, i, 0:1], rstd[:, i:i + 1], ALU.subtract, ALU.mult)

            def stats_of_x(i):
                ln_stats([x[:, i, :]])

            def normed_x(i):
                ln_apply(xn[:, i, :], x[:, i, :]).then_inc(sig("xn_ready"), 1)

            st.did(v.memset(iota16z[:, :], 0.0))
            st.wait()
            v.memset(zmax, -3e38).then_inc(sig("zeros_ready"), 1)
            v.wait_ge(sig("edges_loaded"), 32)
            st.did(v.tensor_copy(srcf, srci[:, :]))
            st.did(v.tensor_copy(dstf, dsti[:, :]))
            v.wait_ge(sig("pool_step"), 1)
            st.did(v.tensor_copy(iota16, iotai))
            st.wait()
            st.did(STT(out=pairf, in0=srcf, scalar=float(N), in1=dstf, op0=ALU.mult, op1=ALU.add))
            st.wait()
            st.did(v.tensor_copy(pairi[:, :], pairf))
            st.did(TS(above, dstf, float(HALF), None, ALU.is_ge))
            st.wait()
            st.did(STT(out=dstm, in0=above, scalar=-float(HALF), in1=dstf, op0=ALU.mult,
                       op1=ALU.add))
            st.did(TS(dstw, above, PACK - 1, 1.0, ALU.mult, ALU.add))
            st.wait()
            TS(neg_dstm, dstm, -1.0, None, ALU.mult).then_inc(sig("hot_terms_ready"), 1)
            TS(neg_dstw, dstw, -1.0, None, ALU.mult).then_inc(sig("hot_terms_ready"), 1)

            def one_hots(k, t):
                TS(one_hot[:, k, 0, :], iota16, srcf[:, t], None, ALU.is_equal)\
                    .then_inc(sig("one_hots_ready"), 1)
                if k % 2 == 0:
                    TS(one_hot[:, k, 1, 0:HALF], iota16[:, 0:HALF], dstm[:, t], dstw[:, t],
                       ALU.is_equal, ALU.mult).then_inc(sig("one_hots_ready"), 1)

            for k in range(ONE_HOTS):
                one_hots(k, slice(k, k + 1))

            def one_hot_turns(lo, hi):
                with v.Fori(lo, hi) as it:
                    for k in range(ONE_HOTS):
                        v.wait_ge(sig("one_hots_used"), it * ONE_HOTS + (k + 1 - ONE_HOTS))
                        one_hots(k, bass.ds(it * ONE_HOTS + k, 1))

            def messages(l, i):
                st.did(TS(exm[:, i, :], (xl if l else xn)[:, i, :], 0.0, 1e-7, ALU.max, ALU.add))
                st.wait()
                st.did(TS(ex[:, i, :], exm[:, i, :], tcol[0:P, l:l + 1], None, ALU.mult))
                st.wait()
                st.did(v.reduce_max(zt[:, i:i + 1], ex[:, i, :], AX_X))

            def largest_exponent(l):
                st.wait()
                v.reduce_max(zmax[0:P, :], zt, AX_X).then_inc(sig("zmax_ready"), 1)
                v.wait_ge(sig("zall_ready"), l + 1)
                TS(zneg, zall, -1.0, HEADROOM, ALU.mult, ALU.add).then_inc(sig("zneg_ready"), 1)

            def weigh(l, i):
                v.wait_ge(sig("ex_ready"), NT * l + i + 1)
                TT(exm[:, i, :], exm[:, i, :], ex[:, i, :], ALU.mult).then_inc(sig("exm_ready"), 1)
                v.wait_ge(sig("exm_ready"), NT * l + i + 1)
                TT(ex_low[:, i, :], ex[:, i, :], high[l][:, 0, i, :].bitcast(F32),
                   ALU.subtract).then_inc(sig("ex_low_ready"), 1)

            lower, higher = counts[:, :, 0:HALF], counts[:, :, HALF:]

            def unpack(n):
                v.wait_ge(sig("raw_copied"), n + 1)
                st.did(TS(upper, raw, 1 / PACK, (1 - PACK / 2) / PACK, ALU.mult, ALU.add))
                st.wait()
                st.did(TS(upper, upper, 1.5 * 2 ** 23, -1.5 * 2 ** 23, ALU.add, ALU.add))
                st.wait()
                st.did(STT(out=raw, in0=upper, scalar=-PACK, in1=raw, op0=ALU.mult, op1=ALU.add))
                if n == 0:
                    st.did(v.tensor_copy(higher, upper))
                    st.wait()
                    v.tensor_copy(lower, raw).then_inc(sig("unpacked"), 1)
                    return
                v.wait_ge(sig("unpacked"), n)
                st.did(TT(higher, higher.bitcast(F32), upper, ALU.add))
                st.wait()
                last = TT(lower, lower.bitcast(F32), raw, ALU.add)
                last.then_inc(sig("unpacked" if n + 1 < len(CHUNKS) else "counts_ready"), 1)

            v.wait_ge(sig("x_loaded"), 16)
            for i in range(3):
                stats_of_x(i)
            one_hot_turns(1, 2)
            for i in range(3, NT):
                stats_of_x(i)
            for i in range(NT):
                normed_x(i)
            one_hot_turns(2, 4)
            unpack(0)
            one_hot_turns(4, 5)
            for i in range(NT):
                v.wait_ge(sig("messages_ready"), i + 1)
                st.did(v.reduce_max(zt[:, i:i + 1], ex[:, i, :], AX_X))
            largest_exponent(0)
            one_hot_turns(5, 7)
            unpack(1)
            one_hot_turns(7, 10)
            unpack(2)

            def heads(slot, parts=P):
                return slot[0:parts, :].rearrange("p (b n) -> p b n", b=2)[:, :, 0:HW]\
                    .rearrange("p b (h e) -> p b h e", h=4)[:, :, :, 0:HD + 1]

            v.wait_ge(sig("mix0_loaded"), 48)
            v.wait_ge(sig("counts_ready"), 1)
            va4 = va[:, 0:NT * H * (HD + 1)].rearrange("p (i h e) -> p i h e", i=NT, h=H)
            v.memset(va[:, 0:NT * H * (HD + 1)].rearrange("p (g e) -> p g e", e=HD + 1)
                     [:, :, HD:HD + 1], 1.0).then_inc(sig("va_ones"), 1)
            v.memset(va[:, NT * H * (HD + 1):], 0.0).then_inc(sig("va_ones"), 1)
            st.did(v.memset(kv[:, H * (HD + 1):], 0.0))

            def squares(i):
                v.wait_ge(sig("squares"), i + 1)
                v.tensor_reduce(nrm2[:, 16 * i:16 * (i + 1)],
                                th[:, i, :].rearrange("p (g e) -> p g e", e=HD),
                                AX_X, ALU.add).then_inc(sig("square_sums"), 1)

            for i in range(NT):
                slot = ring.wait_filled(v, ("qk", i))
                ring.emptied(TT(qk[:, i, :], slot[0:P, :], qkvr[:, 0:2 * D], ALU.add), ("qk", i))
                if i >= 1:
                    squares(i - 1)
            squares(NT - 1)

            def values0(*tiles):
                for i in tiles:
                    slot = ring.wait_filled(v, ("v", i))
                    ring.emptied(TT(va4[:, i, :, 0:HD],
                                    slot[0:P, 0:D].rearrange("p (h e) -> p h e", h=H),
                                    qkvr[:, 2 * D:].rearrange("p (h e) -> p h e", h=H), ALU.add),
                                 ("v", i))

            def scaled(s, name):
                for i in range(NT):
                    TT(th[:, i, D * s:D * (s + 1)].rearrange("p (g e) -> p g e", e=HD),
                       qk[:, i, D * s:D * (s + 1)].rearrange("p (g e) -> p g e", e=HD),
                       rn[:, 16 * i + H * s:16 * i + H * (s + 1)].unsqueeze(2)
                       .to_broadcast([P, H, HD]), ALU.mult).then_inc(sig(name), 1)

            values0(0, 1)
            v.wait_ge(sig("square_sums"), NT)
            v.wait_ge(sig("rnorm_ready"), NT)
            TT(tn, nrm2, rn, ALU.mult).then_inc(sig("norms_ready"), 1)
            scaled(1, "scaled_k")
            values0(2)
            scaled(0, "scaled_q")
            values0(3, 4)

            def aggregate(l, j):
                xT, r = (xlT if l else xnT), rec[j % 2]
                r2 = r.rearrange("p (b n) -> p b n", b=2)

                def halves(slot):
                    return slot.rearrange("p (b n) -> p b n", b=2)[:, :, 0:HALF]

                slot = ring.wait_filled(v, ("den", l, j))
                if KC * l + j >= 2:
                    ring.wait_emptied(v, ("num", *divmod(KC * l + j - 2, KC)))
                st.did(TS(r2, halves(slot), 1e-37, None, ALU.max))
                st.wait()
                ring.emptied(v.reciprocal(r, r), ("den", l, j))
                ring.wait_emptied(v, ("den", l, j))
                slot = ring.wait_filled(v, ("num", l, j))
                ring.emptied(TT(r2, r2, halves(slot), ALU.mult), ("num", l, j))
                ring.wait_emptied(v, ("num", l, j))
                TT(xT[:, j, :], xT[:, j, :], r[:, 0:N], ALU.add).then_inc(sig("hT_ready"), 1)

            aggregate(0, 0)
            aggregate(0, 1)
            v.wait_ge(sig("tanh_norm"), 1)
            st.did(TS(pw, pw, 1.5, 0.75, ALU.mult, ALU.add))

            def feature(f, m, i):
                o = f[:, i, :].rearrange("p (h c e) -> p h c e", h=H, c=2)
                b = m[:, i, :].rearrange("p (h e) -> p h e", h=H).unsqueeze(2)\
                    .to_broadcast([P, H, 2, HD])
                return TT(o, o, b, ALU.mult)

            v.wait_ge(sig("k_cubed"), NT)
            for i in range(NT):
                v.wait_ge(sig("k_angles"), 2 * (i + 1))
                feature(kf, k3, i).then_inc(sig("kf_ready"), 1)
            aggregate(0, 2)
            aggregate(0, 3)
            slot = ring.wait_filled(v, ("kv",))
            ring.emptied(TS(kv[:, 0:H * (HD + 1)].rearrange("p (b h e) -> p b h e", b=2, h=4),
                            heads(slot, 128), 1.0 / N, None, ALU.mult), ("kv",))
            st.wait()
            for i in range(NT):
                v.wait_ge(sig("q_logs"), i + 1)
                TT(q2[:, i, :].rearrange("p (h e) -> p h e", h=H),
                   q2[:, i, :].rearrange("p (h e) -> p h e", h=H),
                   pw[:, i, :].unsqueeze(2).to_broadcast([P, H, HD]),
                   ALU.mult).then_inc(sig("q_powers"), 1)
            for i in range(NT):
                v.wait_ge(sig("q_feats"), i + 1)
                v.wait_ge(sig("q_angles"), 2 * (i + 1))
                feature(qf, q2, i).then_inc(sig("qf_ready"), 1)

            def divide_heads(dst, slot, eps):
                s = heads(slot)
                r = rden[:, 0:H].rearrange("p (b h) -> p b h", b=2)
                st.did(TS(r, s[:, :, :, HD], eps, None, ALU.add))
                st.wait()
                st.did(v.reciprocal(r, r))
                st.wait()
                return TT(dst.rearrange("p (b h e) -> p b h e", b=2, h=4), s[:, :, :, 0:HD],
                          r.unsqueeze(3).to_broadcast([P, 2, 4, HD]), ALU.mult)

            def attended(i):
                slot = ring.wait_filled(v, ("mo", i))
                if i >= 2:
                    ring.wait_filled(v, ("moT", i - 2))
                ring.emptied(divide_heads(mo[:, i % 2, :], slot, 1e-6), ("mo", i))
                ring.wait_emptied(v, ("mo", i))
                ln_stats([mo[:, i % 2, :]])
                ln_apply(mo[:, i % 2, :], mo[:, i % 2, :]).then_inc(sig("mo_ready"), 1)

            def add_to_x(name, i):
                slot = ring.wait_filled(v, name)
                ring.emptied(TT(x[:, i, :], x[:, i, :], slot[0:P, 0:D], ALU.add), name)

            lagged(attended, lambda i: None, lambda i: add_to_x(("mw", i), i))

            for l in range(LAYERS):
                if l:
                    for j in range(KC):
                        aggregate(l, j)
                v.wait_ge(sig("b1_loaded"), 16 * (l + 1))
                v.wait_ge(sig("b2_loaded"), 16 * (l + 1))
                if l:
                    v.wait_ge(sig("lng_loaded"), 32 * l)
                for i in range(NT + 2):
                    j = i - 2
                    if i < NT:
                        if i >= 2:
                            ring.wait_filled(v, ("gT", l, i - 2))
                        slot = ring.wait_filled(v, ("u", l, i))
                        ring.emptied(TT(u[:, i % 2, :], slot[0:P, :], b1r, ALU.add), ("u", l, i))
                        ring.wait_emptied(v, ("u", l, i))
                        ln_stats([u[:, i % 2, 0:D], u[:, i % 2, D:HID]])
                    if j >= 0:
                        if l and NT * (l - 1) + j:
                            v.wait_ge(sig("xl_ready"), NT * (l - 1) + j)
                        slot = ring.wait_filled(v, ("y", l, j))
                        y = ytmp if l else xl[:, j, :]
                        ring.emptied(TT(y, slot[0:P, 0:D], b2r, ALU.add), ("y", l, j))
                        ring.wait_emptied(v, ("y", l, j))
                        if l:
                            ln_stats([y])
                    if i < NT:
                        ln_apply(u[:, i % 2, :], u[:, i % 2, :]).then_inc(sig("u_normed"), 1)
                    if j >= 0:
                        if l:
                            st.did(ln_apply(y, y))
                            st.wait()
                            st.did(TT(y, y, lngr, ALU.mult))
                            st.wait()
                            st.did(TT(y, y, lnbr, ALU.add))
                            st.wait()
                            STT(out=xl[:, j, :], in0=y, scalar=0.0, in1=xl[:, j, :],
                                op0=ALU.max, op1=ALU.add).then_inc(sig("xl_ready"), 1)
                            v.wait_ge(sig("xl_ready"), NT * (l - 1) + j + 1)
                        if l + 1 < LAYERS:
                            messages(l + 1, j)
                if l + 1 < LAYERS:
                    largest_exponent(l + 1)
                if l == 0:
                    v.wait_ge(sig("bias_loaded"), 32)
                    ring.wait_emptied(v, ("mw", NT - 1))
                    for n in range(2):
                        st.did(TT(x[:, :, :], x[:, :, :],
                                  biasr[:, D * n:D * (n + 1)].unsqueeze(1).to_broadcast([P, NT, D]),
                                  ALU.add))
                        st.wait()
                for i in range(NT + 1):
                    if l + 1 < LAYERS and i < NT:
                        weigh(l + 1, i)
                    if i >= 1:
                        add_to_x(("cw", l, i - 1), i - 1)
                    if l + 1 == LAYERS:
                        if i >= 1:
                            ring.wait_emptied(v, ("cw", l, i - 1))
                            stats_of_x(i - 1)
                        if i >= 2:
                            normed_x(i - 2)
            normed_x(NT - 1)

            v.wait_ge(sig("f0_loaded"), 64)
            v.wait_ge(sig("ones_ready"), 2)
            for i in range(NT):
                slot = ring.wait_filled(v, ("f0", i))
                st.did(v.tensor_copy(lg8[:, i, :], slot[0:P, 512:512 + H]))
                st.wait()
                st.did(v.max(top8[:, i, :], lg8[:, i, :]))
                ring.emptied(v.tensor_copy(fh[:, i, :], slot[0:P, 0:D]), ("f0", i))
            st.wait()

            def two_weights(gap, exp):
                TT(p12[:, 1, :], top8[:, :, 1], top8[:, :, 0], ALU.subtract)\
                    .then_inc(sig(gap), 1)
                v.wait_ge(sig(exp), 1)
                st.did(TS(p12[:, 2, :], p12[:, 0, :], 1.0, None, ALU.add))
                st.wait()
                st.did(v.reciprocal(p12[:, 2, :], p12[:, 2, :]))
                st.wait()
                st.did(TT(p12[:, 0, :], p12[:, 0, :], p12[:, 2, :], ALU.mult))
                st.wait()

            def fg_sum(i):
                v.wait_ge(sig("f0_gelu"), 2 * (i + 1))
                TT(fg1[:, i, :], fg1[:, i, :], fg2[:, i, :], ALU.add).then_inc(sig("fg_ready"), 1)

            two_weights("f0_gap", "f0_exp")
            ring.wait_emptied(v, ("f0", NT - 1))
            for i in range(NT):
                for n, t in ((2, fg1), (0, fg2)):
                    STT(out=t[:, i, :], in0=fh[:, i, :], scalar=p12[:, n, i:i + 1],
                        in1=f0b1r, op0=ALU.mult, op1=ALU.add).then_inc(sig("f0_in"), 1)
                if i:
                    fg_sum(i - 1)
            fg_sum(NT - 1)
            for i in range(NT):
                add_to_x(("f0o", i), i)
                ring.wait_emptied(v, ("f0o", i))
                stats_of_x(i)
                if i:
                    normed_x(i - 1)
            normed_x(NT - 1)

            v.wait_ge(sig("gat_loaded"), 80)
            flat = hea[:, 0:NT * H * (HD + 1)]
            hea4 = flat.rearrange("p (i h e) -> p i h e", i=NT, h=H)
            st.did(v.memset(flat.rearrange("p (g e) -> p g e", e=HD + 1)[:, :, HD:HD + 1], 1.0))
            st.did(v.memset(hea[:, NT * H * (HD + 1):], 0.0))
            st.did(v.memset(hrTs, 0.0))
            for i in range(NT):
                slot = ring.wait_filled(v, ("hre", i))
                st.did(v.tensor_copy(hea4[:, i, :, 0:HD],
                                     slot[0:P, 0:D].rearrange("p (h e) -> p h e", h=H)))
                ring.emptied(v.tensor_copy(hr[:, i, 0:D], slot[0:P, D:2 * D]), ("hre", i))
                ring.wait_emptied(v, ("hre", i))
                st.wait()
                he_i = hea4[:, i, :, 0:HD]
                for n, t in ((2, he_i), (1, he_i),
                             (3, hr[:, i, 0:D].rearrange("p (h e) -> p h e", h=H))):
                    st.did(TT(tmp[:, n - 1, :].rearrange("p (h e) -> p h e", h=H), t,
                              ar[:, n, :].rearrange("p (h e) -> p h e", h=H), ALU.mult))
                st.wait()
                st.did(v.tensor_reduce(hr[:, i, D:D + H],
                                       tmp[:, 1, :].rearrange("p (h e) -> p h e", h=H),
                                       AX_X, ALU.add))
                st.did(TT(tmp[:, 0, :], tmp[:, 0, :], tmp[:, 2, :], ALU.subtract))
                st.wait()
                v.tensor_reduce(hr[:, i, D + H:D + 2 * H],
                                tmp[:, 0, :].rearrange("p (h e) -> p h e", h=H),
                                AX_X, ALU.add).then_inc(sig("table_ready"), 1)
                v.wait_ge(sig("table_ready"), i + 1)
                st.did(TT(ends[:, i, :, 0], hr[:, i, D:D + H], hr[:, i, D + H:], ALU.add))
                st.wait()
                st.did(TS(ends[:, i, :, 1], ends[:, i, :, 0], 0.2, None, ALU.mult))
            ring.wait_emptied(v, ("hrT", NT - 1))
            st.wait()
            for h in range(H):
                half = slice(HD * (h % 2), HD * (h % 2 + 1))
                ins = TS(hrTs[half, h, :], hrT[half, h // 2, :],
                         col("a_prd", h // 2, HD * (h % 2), HD * (h % 2 + 1)),
                         col("a_difT", h // 2, HD * (h % 2), HD * (h % 2 + 1)), ALU.mult, ALU.add)
            ins.then_inc(sig("hrTs_ready"), 1)

            def k_largest(*js):
                for j in js:
                    ring.wait_emptied(v, ("kT", j))
                    v.tensor_reduce(kmax[:, j:j + 1], ek[:, j, :], AX_X, ALU.max, negate=True)\
                        .then_inc(sig("kmax_ready"), 1)

            def values(*tiles):
                for i in tiles:
                    slot = ring.wait_filled(v, ("v1", i))
                    ring.emptied(TT(v1[:, i, :], slot[0:P, 0:D], v1r, ALU.add), ("v1", i))

            def context():
                st.did(v.memset(ctxb, 0.0))
                v.wait_ge(sig("ek_ready"), KC)
                st.did(v.reciprocal(krec, ksum))
                st.wait()
                slot = ring.wait_filled(v, ("ctx",))
                for j in range(KC):
                    for g in range(2):
                        r = slice(HD * g, HD * (g + 1))
                        last = TS(ctxb[r, j, HD * g:HD * (g + 1)],
                                  slot[r, 128 * j + HD * g:128 * j + HD * (g + 1)],
                                  krec[r, j:j + 1], None, ALU.mult)
                ring.emptied(last, ("ctx",))

            def mix1_out(*tiles):
                for i in tiles:
                    slot = ring.wait_filled(v, ("y1", i))
                    st.did(TT(x[:, i, :], x[:, i, :], b1or, ALU.add))
                    st.wait()
                    ring.emptied(TT(x[:, i, :], x[:, i, :], slot[0:P, 0:D], ALU.add), ("y1", i))

            def index(k, t):
                v.tensor_copy(ix[:, 3 * k:3 * k + 1], srci[:, t]).then_inc(sig("gat_step"), 1)
                v.tensor_copy(ix[:, 3 * k + 1:3 * k + 2], dsti[:, t])\
                    .then_inc(sig("indices_ready"), 1)

            def difference(k, landed):
                v.wait_ge(sig(f"gathered_{k}"), landed)
                TT(difs[k], gd[:, k, 0:D], gs[:, k, 0:D], ALU.subtract)\
                    .then_inc(sig("differences"), 1)
                TT(e8[:, k, :], gd[:, k, D:D + H], gs[:, k, D:D + H], ALU.subtract)\
                    .then_inc(sig("gat_ends"), 1)

            def edge_one_hots(it):
                if not (isinstance(it, int) and it == 0):
                    v.wait_ge(sig("edge_turned"), it)
                t = slice(GATHERS, TURN) if isinstance(it, int) and it == 0 \
                    else bass.ds(it * TURN + GATHERS, 1)
                TS(edge_hots[:, 0, :], edge_iota, edge_dstf[:, t], None, ALU.is_equal)\
                    .then_inc(sig("gat_step"), 1)
                TS(edge_hots[:, 1, :], edge_iota, edge_srcf[:, t], None, ALU.is_equal)\
                    .then_inc(sig("edge_hots_ready"), 1)

            def score(k, t, number, ends_number, sent):
                v.wait_ge(sig("abs_ready"), number)
                TT(difs[k], difs[k], ar[:, 0, :], ALU.mult)\
                    .then_inc(sig("weighted"), 1)
                v.wait_ge(sig("weighted"), number)
                if sent is not None:
                    v.wait_ge(sig("scattered"), sent)
                v.tensor_reduce(sc[:, k, :], difs[k].rearrange("p (h e) -> p h e", h=H),
                                AX_X, ALU.add).then_inc(sig("gat_sums"), 1)
                v.tensor_copy(ix[:, 3 * k + 2:3 * k + 3], pairi[:, t])\
                    .then_inc(sig("gat_pairs"), 1)
                v.wait_ge(sig("gat_sums"), number)
                if k < GATHERS:
                    v.wait_ge(sig("gat_ends"), ends_number)
                    e = e8[:, k, :]
                else:
                    e = ring.psum[3][0:P, 768:768 + H]
                TT(sc[:, k, :], sc[:, k, :], e, ALU.add).then_inc(sig("scores_ready"), 1)

            def edge_tile(it, k):
                static = isinstance(it, int)

                def one(at):
                    return slice(at, at + 1) if static else bass.ds(at, 1)

                def ready():
                    if k < GATHERS:
                        difference(k, (it + 1) * 32)
                        if not (static and it + 1 == TURNS):
                            index(k, one((it + 1) * TURN + k))
                    elif not (static and it + 1 == TURNS):
                        edge_one_hots(it + 1)
                if k:
                    ready()
                if not (static and it == 0 and k == 0):
                    sent = (it - 1) * (16 * TURN) + 16 * k
                    done = it * GATHERS + k if k else None
                    score((k - 1) % TURN, one(it * TURN + (k - 1)), it * TURN + k, done,
                          None if static and sent <= 0 else sent)
                if not k:
                    ready()

            def edge_turns(lo, hi):
                with v.Fori(lo, hi) as it:
                    for k in range(TURN):
                        edge_tile(it, k)

            for k in range(GATHERS):
                index(k, slice(k, k + 1))
            st.did(v.tensor_copy(edge_srcf, srci[:, :]))
            st.did(v.tensor_copy(edge_dstf, dsti[:, :]))
            v.wait_ge(sig("edge_iota_ready"), 1)
            st.did(v.tensor_copy(edge_iota, edge_iota32))
            st.did(v.tensor_copy(edge_ident[:, 0, :], ident[0:P, 0:P]))
            st.did(TS(edge_ident[:, 1, :], ident[0:P, 0:P], -1.0, None, ALU.mult))
            st.wait()
            edge_one_hots(0)
            for it in range(2):
                for k in range(TURN):
                    edge_tile(it, k)
            edge_turns(2, 6)
            k_largest(0, 1, 2, 3)
            edge_turns(6, 10)
            values(0, 1)
            edge_turns(10, 11)
            values(2, 3)
            edge_turns(11, 12)
            values(4)
            edge_turns(12, 13)
            context()
            edge_turns(13, 15)
            mix1_out(0, 1)
            for k in range(TURN):
                edge_tile(TURNS - 1, k)
            score(GATHERS, slice(ET - 1, ET), ET, None, 16 * (ET - TURN))
            mix1_out(2, 3, 4)

            for g in range(NT * H + LAG + SUM_LAG + NORM_LAG):
                i, h = divmod(g, H)
                if i < NT:
                    if h == 0:
                        v.wait_ge(sig(f"pairs_loaded_{i % 2}"), 16 * (i // 2 + 1))
                    p3 = pt[i % 2].rearrange("p (d h) -> p d h", h=H)
                    if i:
                        ring.wait_filled(v, ("exT", i - 1, h))
                    slot = ring.wait_filled(v, ("pair", i, h))
                    ring.emptied(v.tensor_tensor_reduce(
                        S[:, h, :], slot[0:P, 0:N], p3[:, :, h], 1.0, -3e38, ALU.add, ALU.max,
                        smax[:, 0, h:h + 1]), ("pair", i, h))
                    ring.wait_emptied(v, ("pair", i, h))
                    st.did(STT(out=smax[:, 2, h:h + 1], in0=smax[:, 0, h:h + 1], scalar=-1.0,
                               in1=ends[:, i, h, 0:1], op0=ALU.mult, op1=ALU.subtract))
                    st.wait()
                    st.did(STT(out=smax[:, 1, h:h + 1], in0=smax[:, 2, h:h + 1], scalar=0.2,
                               in1=smax[:, 2, h:h + 1], op0=ALU.mult, op1=ALU.min))
                    st.wait()
                    TS(smax[:, 3 + h, 0:2], ends[:, i, h, :], smax[:, 1, h:h + 1], None, ALU.add)\
                        .then_inc(sig("bias_ready"), 1)
                if 1 <= g <= NT * H:
                    v.wait_ge(sig("pair_exp"), g)
                    before = S[:, (g - 1) % H, :]
                    TT(before, before, S_low[:, (g - 1) % 2, :], ALU.max)\
                        .then_inc(sig("larger_ready"), 1)
                j, h = divmod(g - LAG - SUM_LAG, H)
                if 0 <= j < NT and h % 4 == 3:
                    b = h // 4
                    v.wait_ge(sig("head_summed"), j * H + h + 1)
                    s4 = ring.psum[3][0:P, 512 * b:512 * b + HW]\
                        .rearrange("p (h e) -> p h e", h=4)
                    o, r = otmp[:, 256 * b:256 * (b + 1)], rden[:, 4 * b:4 * (b + 1)]
                    st.did(TS(r, s4[:, :, HD], 1e-16, None, ALU.add))
                    st.wait()
                    st.did(v.reciprocal(r, r))
                    st.wait()
                    TT(o.rearrange("p (h e) -> p h e", h=4), s4[:, :, 0:HD],
                       r.unsqueeze(2).to_broadcast([P, 4, HD]), ALU.mult)\
                        .then_inc(sig("sums_used"), 1)
                    v.wait_ge(sig("sums_used"), 2 * j + b + 1)
                    st.did(TT(x[:, j, 256 * b:256 * (b + 1)], x[:, j, 256 * b:256 * (b + 1)], o,
                              ALU.add))
                    if b:
                        st.wait()
                        stats_of_x(j)
                j, left = divmod(g - LAG - SUM_LAG - NORM_LAG, H)
                if 0 <= j < NT and left == H - 1:
                    normed_x(j)

            v.wait_ge(sig("f1_loaded"), 64)
            for i in range(NT):
                slot = ring.wait_filled(v, ("f1", i))
                ring.emptied(TT(g1[:, i, 0:WX], slot[0:P, 0:WX], f1r, ALU.add), ("f1", i))
                ring.wait_emptied(v, ("f1", i))
                st.did(v.tensor_copy(lg8[:, i, :], g1[:, i, WX - H:WX]))
                st.wait()
                st.did(v.max(top8[:, i, :], lg8[:, i, :]))
                st.wait()
                st.did(v.max_index(idx8[:, i, :], top8[:, i, :], lg8[:, i, :]))
            st.wait()
            st.did(v.tensor_copy(idf8, idx8))
            two_weights("f1_gap", "f1_exp")
            for i in range(NT):
                comb = g1[:, i, WX - H:WX]
                st.did(TS(comb, io8, idf8[:, i, 1:2], p12[:, 0, i:i + 1], ALU.is_equal, ALU.mult))
                st.did(TS(lg8[:, i, :], io8, idf8[:, i, 0:1], p12[:, 2, i:i + 1],
                          ALU.is_equal, ALU.mult))
                st.wait()
                st.did(TT(comb, comb, lg8[:, i, :], ALU.add))
                st.did(TS(g1[:, i, D:D + HD], g1[:, i, D:D + HD], 0.0, 0.5, ALU.max, ALU.mult))
                st.did(v.memset(g1[:, i, WX:WX + 1], 0.5))
                st.wait()
                h3 = g1[:, i, 0:D].rearrange("p (h e) -> p h e", h=H)
                STT(out=h3, in0=h3, scalar=0.0, in1=comb.unsqueeze(2).to_broadcast([P, H, HD]),
                    op0=ALU.max, op1=ALU.mult).then_inc(sig("g1_ready"), 1)
            for i in range(NT):
                add_to_x(("f1o", i), i)


def lay_out(i):
    import numpy as np

    heads = i["L1_gnn_a"].reshape(H, 5, HD).transpose(1, 0, 2).reshape(5, H * HD)
    vec = {f"mb1_{l}": i[f"L0_gnn_mb1_{l}"] for l in range(LAYERS)}
    vec |= {f"mb2_{l}": i[f"L0_gnn_mb2_{l}"] for l in range(LAYERS)}
    vec |= {f"{n}_{l}": i[f"L0_gnn_{n}_{l}"] for l in (1, 2) for n in ("lng", "lnb")}
    vec |= {"qkv_b": i["L0_mix_qkv_b"], "out_b": i["L0_mix_out_b"], "cb": i["L0_gnn_cb"],
            "f0_b1": i["L0_ffn_b1"].reshape(-1), "v_b": i["L1_mix_b_qkv"][2 * D:],
            "b_out": i["L1_mix_b_out"],
            "f1_b": np.concatenate([i["L1_ffn_b1"].reshape(-1), i["L1_ffn_bs1"], i["L1_ffn_bg"]]),
            "a_src": heads[0], "a_dst": heads[1], "a_dif": heads[2], "a_abs": heads[3],
            "t": np.concatenate([i[f"L0_gnn_t{l}"] for l in range(LAYERS)])}
    col = {f"{n}_{l}": i[f"L0_gnn_{n}_{l}"] for l in range(LAYERS) for n in ("mlg", "mlb")}
    col |= {"ln_g": i["L0_mix_ln_g"], "ln_b": i["L0_mix_ln_b"], "q_b": i["L1_mix_b_qkv"][:D],
            "k_b": i["L1_mix_b_qkv"][D:2 * D], "a_prd": heads[4], "a_difT": heads[2]}

    def experts(w):
        return w.transpose(1, 0, 2).reshape(D, H * HD)

    def zeros(rows, columns):
        return np.zeros((rows, columns), np.float32)

    out = {"x": i["x"], "src": i["src"], "dst": i["dst"],
           "rows": np.concatenate([vec[n] for n, _ in ROWS]),
           "cols": np.concatenate([col[n].reshape(-1, 128).T for n, _ in COLS], axis=1)}
    out |= {f"{n}_{l}": i[f"L0_gnn_{n}_{l}"] for l in range(LAYERS) for n in ("mw1", "mw2")}
    out |= {"cw": i["L0_gnn_cw"], "qkv_w": i["L0_mix_qkv_w"], "out_w": i["L0_mix_out_w"],
            "f0_w1": np.concatenate([experts(i["L0_ffn_W1"]), i["L0_ffn_Wg"],
                                     zeros(D, WP - D - H)], axis=1),
            "f0_w2": i["L0_ffn_W2"].reshape(H * HD, D),
            "f0_b2": np.concatenate([i["L0_ffn_b2"], zeros(128 - H, D)]),
            "w_er": np.concatenate([experts(i["L1_gnn_W_e"]), experts(i["L1_gnn_W_r"])], axis=1),
            "w_qkvT": i["L1_mix_W_qkv"].T, "w_outT": i["L1_mix_W_out"].T,
            "f1_w": np.concatenate([experts(i["L1_ffn_W1"]), i["L1_ffn_Ws1"], i["L1_ffn_Wg"],
                                    zeros(D, WP - WX)], axis=1),
            "f1_w2": i["L1_ffn_W2"].reshape(H * HD, D),
            "f1_w3": np.concatenate([i["L1_ffn_Ws2"], i["L1_ffn_b2"],
                                     i["L1_ffn_bs2"].reshape(1, D)])}
    return {n: np.ascontiguousarray(v) for n, v in out.items()}


def kernel(**inputs):
    import numpy as np
    import concourse.bacc as bacc
    from concourse.bass_utils import run_bass_kernel_spmd

    nc = bacc.Bacc("TRN2", target_bir_lowering=False, num_devices=1)
    laid = lay_out({n: np.asarray(v) for n, v in inputs.items()})
    arrays = {f"in_{n}": v for n, v in laid.items()}
    aps = {n: nc.dram_tensor(f"in_{n}", v.shape, mybir.dt.from_np(v.dtype),
                             kind="ExternalInput").ap() for n, v in laid.items()}
    out = nc.dram_tensor("out", (N, D), F32, kind="ExternalOutput").ap()
    build_gps(nc, aps, out)
    return run_bass_kernel_spmd(nc, [arrays], core_ids=[0]).results[0]["out"]
```
